# Optimizing a Trainium2 kernel written in Bass

```python
import numpy as np
import jax
import jax.numpy as jnp

def _softmax(x, axis=-1):
    return jax.nn.softmax(x, axis=axis)

def _gelu(x):
    return jax.nn.gelu(x, approximate=True)

def _silu(x):
    return jax.nn.silu(x)

def _sigmoid(x):
    return jax.nn.sigmoid(x)

def _layernorm(x, axis=-1, eps=1e-05):
    m = jnp.mean(x, axis=axis, keepdims=True)
    v = jnp.var(x, axis=axis, keepdims=True)
    return (x - m) / jnp.sqrt(v + eps)

def _scatter_add(tgt, idx, src, axis=0):
    return tgt.at[idx].add(src)

def _segment_sum(src, seg, n):
    return jax.ops.segment_sum(src, seg, n)
kernel_name = 'mk_sandwich_d1_jaxref_r4_da7661'

def setup_inputs(seed: int=0):
    np.random.seed(seed)
    _w = jnp.asarray

    def _L0_attn_setup():
        import jax, jax.numpy as jnp
        import numpy as np
        GROUP = 64
        MAX_REL = 32

        def _silu(x):
            return x * jax.nn.sigmoid(x)

        def _ln(x, w, b, eps=1e-05):
            m = x.mean(-1, keepdims=True)
            v = ((x - m) ** 2).mean(-1, keepdims=True)
            return (x - m) / jnp.sqrt(v + eps) * w + b

        def _rope(x):
            n, d = (x.shape[-2], x.shape[-1])
            half = d // 2
            pos = jnp.arange(n, dtype=x.dtype)
            inv_freq = 10000.0 ** (-jnp.arange(half, dtype=x.dtype) / half)
            sinusoid = pos[:, None] * inv_freq[None, :]
            sin, cos = (jnp.sin(sinusoid), jnp.cos(sinusoid))
            x1, x2 = (x[..., :half], x[..., half:])
            return jnp.concatenate([x1 * cos - x2 * sin, x2 * cos + x1 * sin], axis=-1)
        key = jax.random.key(seed)
        ks = jax.random.split(key, 8)
        B, N, D, QK, H = (4, 1024, 256, 64, 512)
        s = 0.02
        return {'x': jax.random.normal(ks[0], (B, N, D), dtype=jnp.float32), 'ln1_w': jnp.ones((D,), jnp.float32), 'ln1_b': jnp.zeros((D,), jnp.float32), 'Wqk': jax.random.normal(ks[1], (QK, D), jnp.float32) * s, 'bqk': jnp.zeros((QK,), jnp.float32), 'Wv': jax.random.normal(ks[2], (H, D), jnp.float32) * s, 'bv': jnp.zeros((H,), jnp.float32), 'Wg': jax.random.normal(ks[3], (H, D), jnp.float32) * s, 'bg': jnp.zeros((H,), jnp.float32), 'Wo': jax.random.normal(ks[4], (D, H), jnp.float32) * s, 'bo': jnp.zeros((D,), jnp.float32), 'ln2_w': jnp.ones((D,), jnp.float32), 'ln2_b': jnp.zeros((D,), jnp.float32), 'gamma': jax.random.normal(ks[5], (4, QK), jnp.float32) * 0.02, 'beta': jnp.zeros((4, QK), jnp.float32), 'pos_emb': jax.random.normal(ks[6], (2 * MAX_REL + 1,), jnp.float32)}
    _L0_attn_in = _L0_attn_setup()

    def _L0_ffn_setup():
        import jax, jax.numpy as jnp
        import numpy as np
        DIM = 256
        INTER = 256
        E = 32
        K = 4
        G = 8
        LG = 4
        ROUTE_SCALE = 1.0
        CAP_FACTOR = 1.25
        B, S = (4, 512)

        def _gate(xf, wg):
            logits = xf @ wg.T
            scores = jax.nn.softmax(logits, axis=-1)
            sg = scores.reshape(-1, G, E // G)
            group_scores = sg.max(axis=-1)
            _, gtop = jax.lax.top_k(group_scores, LG)
            keep_g = jnp.sum(jax.nn.one_hot(gtop, G, dtype=jnp.float32), axis=1) > 0
            masked = jnp.where(keep_g[:, :, None], sg, -jnp.inf).reshape(-1, E)
            _, idx = jax.lax.top_k(masked, K)
            w = jnp.take_along_axis(scores, idx, axis=1)
            w = w / (w.sum(-1, keepdims=True) + 1e-09) * ROUTE_SCALE
            return (w.astype(xf.dtype), idx)

        def _forward(x, wg, w1, w2, w3, sw1, sw2, sw3):
            shape = x.shape
            xf = x.reshape(-1, DIM)
            N = xf.shape[0]
            cap = max(1, int(CAP_FACTOR * N * K / E))
            w, idx = _gate(xf, wg)
            fe = idx.reshape(-1)
            oh = jax.nn.one_hot(fe, E, dtype=jnp.int32)
            pos = (jnp.cumsum(oh, axis=0) * oh).sum(-1) - 1
            keep = pos < cap
            dest = jnp.where(keep, fe * cap + pos, E * cap)
            tok = jnp.arange(N * K, dtype=jnp.int32) // K
            buf_tok = jnp.full((E * cap + 1,), N, jnp.int32).at[dest].set(tok)[:-1]
            buf_w = jnp.zeros((E * cap + 1,), x.dtype).at[dest].set(w.reshape(-1))[:-1]
            xp = jnp.concatenate([xf, jnp.zeros((1, DIM), x.dtype)], axis=0)
            xe = xp[buf_tok].reshape(E, cap, DIM)
            h = jax.nn.silu(jnp.einsum('ecd,edh->ech', xe, w1)) * jnp.einsum('ecd,edh->ech', xe, w3)
            out = jnp.einsum('ech,ehd->ecd', h, w2) * buf_w.reshape(E, cap, 1)
            y = jnp.zeros((N + 1, DIM), x.dtype).at[buf_tok].add(out.reshape(E * cap, DIM))[:N]
            z = jax.nn.silu(xf @ sw1) * (xf @ sw3) @ sw2
            return (y + z).reshape(shape)
        key = jax.random.key(seed)
        ks = jax.random.split(key, 9)
        sd = DIM ** (-0.5)
        si = INTER ** (-0.5)
        x = jax.random.normal(ks[0], (B, S, DIM), jnp.float32)
        wg = jax.random.normal(ks[1], (E, DIM), jnp.float32) * sd
        w1 = jax.random.normal(ks[2], (E, DIM, INTER), jnp.float32) * sd
        w3 = jax.random.normal(ks[3], (E, DIM, INTER), jnp.float32) * sd
        w2 = jax.random.normal(ks[4], (E, INTER, DIM), jnp.float32) * si
        sw1 = jax.random.normal(ks[5], (DIM, INTER), jnp.float32) * sd
        sw3 = jax.random.normal(ks[6], (DIM, INTER), jnp.float32) * sd
        sw2 = jax.random.normal(ks[7], (INTER, DIM), jnp.float32) * si
        return dict(x=x, wg=wg, w1=w1, w2=w2, w3=w3, sw1=sw1, sw2=sw2, sw3=sw3)
    _L0_ffn_in = _L0_ffn_setup()
    _d = {'L0_attn_x': _L0_attn_in['x'], 'L0_attn_ln1_w': _L0_attn_in['ln1_w'], 'L0_attn_ln1_b': _L0_attn_in['ln1_b'], 'L0_attn_Wqk': _L0_attn_in['Wqk'], 'L0_attn_bqk': _L0_attn_in['bqk'], 'L0_attn_Wv': _L0_attn_in['Wv'], 'L0_attn_bv': _L0_attn_in['bv'], 'L0_attn_Wg': _L0_attn_in['Wg'], 'L0_attn_bg': _L0_attn_in['bg'], 'L0_attn_Wo': _L0_attn_in['Wo'], 'L0_attn_bo': _L0_attn_in['bo'], 'L0_attn_ln2_w': _L0_attn_in['ln2_w'], 'L0_attn_ln2_b': _L0_attn_in['ln2_b'], 'L0_attn_gamma': _L0_attn_in['gamma'], 'L0_attn_beta': _L0_attn_in['beta'], 'L0_attn_pos_emb': _L0_attn_in['pos_emb'], 'L0_ffn_wg': _L0_ffn_in['wg'], 'L0_ffn_w1': _L0_ffn_in['w1'], 'L0_ffn_w2': _L0_ffn_in['w2'], 'L0_ffn_w3': _L0_ffn_in['w3'], 'L0_ffn_sw1': _L0_ffn_in['sw1'], 'L0_ffn_sw2': _L0_ffn_in['sw2'], 'L0_ffn_sw3': _L0_ffn_in['sw3']}
    _x0 = _d['L0_attn_x']
    _d['L0_attn_x'] = jax.random.normal(jax.random.fold_in(jax.random.key(seed), 1), (2, 4096, 256), dtype=_x0.dtype)
    del _x0
    return _d

def reference(L0_attn_x, L0_attn_ln1_w, L0_attn_ln1_b, L0_attn_Wqk, L0_attn_bqk, L0_attn_Wv, L0_attn_bv, L0_attn_Wg, L0_attn_bg, L0_attn_Wo, L0_attn_bo, L0_attn_ln2_w, L0_attn_ln2_b, L0_attn_gamma, L0_attn_beta, L0_attn_pos_emb, L0_ffn_wg, L0_ffn_w1, L0_ffn_w2, L0_ffn_w3, L0_ffn_sw1, L0_ffn_sw2, L0_ffn_sw3):

    def _L0_attn_ref(x, ln1_w, ln1_b, Wqk, bqk, Wv, bv, Wg, bg, Wo, bo, ln2_w, ln2_b, gamma, beta, pos_emb):
        import jax, jax.numpy as jnp
        import numpy as np
        GROUP = 64
        MAX_REL = 32

        def _silu(x):
            return x * jax.nn.sigmoid(x)

        def _ln(x, w, b, eps=1e-05):
            m = x.mean(-1, keepdims=True)
            v = ((x - m) ** 2).mean(-1, keepdims=True)
            return (x - m) / jnp.sqrt(v + eps) * w + b

        def _rope(x):
            n, d = (x.shape[-2], x.shape[-1])
            half = d // 2
            pos = jnp.arange(n, dtype=x.dtype)
            inv_freq = 10000.0 ** (-jnp.arange(half, dtype=x.dtype) / half)
            sinusoid = pos[:, None] * inv_freq[None, :]
            sin, cos = (jnp.sin(sinusoid), jnp.cos(sinusoid))
            x1, x2 = (x[..., :half], x[..., half:])
            return jnp.concatenate([x1 * cos - x2 * sin, x2 * cos + x1 * sin], axis=-1)
        b, n, d = x.shape
        G = GROUP
        x = _ln(x, ln1_w, ln1_b)
        qk = _silu(x @ Wqk.T + bqk)
        v = _silu(x @ Wv.T + bv)
        heads = qk[..., None, :] * gamma + beta
        quad_q, lin_q, quad_k, lin_k = (heads[..., i, :] for i in range(4))
        quad_q, lin_q, quad_k, lin_k = map(_rope, (quad_q, lin_q, quad_k, lin_k))
        g = n // G
        rs = lambda t: t.reshape(b, g, G, t.shape[-1])
        qq, lq, qkk, lk, vg = map(rs, (quad_q, lin_q, quad_k, lin_k, v))
        idx = jnp.arange(G)
        dist = jnp.clip(jnp.abs(idx[:, None] - idx[None, :]), 0, MAX_REL)
        bias = pos_emb[dist]
        quad_att = jnp.einsum('bgid,bgjd->bgij', qq, qkk) / G + bias
        attn = jax.nn.relu(quad_att) ** 2
        quad_out = jnp.einsum('bgij,bgje->bgie', attn, vg)
        lin_kv = jnp.einsum('bgnd,bgne->bde', lk, vg) / n
        lin_out = jnp.einsum('bgnd,bde->bgne', lq, lin_kv)
        qo = quad_out.reshape(b, n, -1)
        lo = lin_out.reshape(b, n, -1)
        gate = _silu(x @ Wg.T + bg)
        out = gate * (qo + lo)
        out = out @ Wo.T + bo
        return _ln(out, ln2_w, ln2_b)

    def _L0_ffn_ref(x, wg, w1, w2, w3, sw1, sw2, sw3):
        import jax, jax.numpy as jnp
        import numpy as np
        DIM = 256
        INTER = 256
        E = 32
        K = 4
        G = 8
        LG = 4
        ROUTE_SCALE = 1.0
        CAP_FACTOR = 1.25
        B, S = (4, 512)

        def _gate(xf, wg):
            logits = xf @ wg.T
            scores = jax.nn.softmax(logits, axis=-1)
            sg = scores.reshape(-1, G, E // G)
            group_scores = sg.max(axis=-1)
            _, gtop = jax.lax.top_k(group_scores, LG)
            keep_g = jnp.sum(jax.nn.one_hot(gtop, G, dtype=jnp.float32), axis=1) > 0
            masked = jnp.where(keep_g[:, :, None], sg, -jnp.inf).reshape(-1, E)
            _, idx = jax.lax.top_k(masked, K)
            w = jnp.take_along_axis(scores, idx, axis=1)
            w = w / (w.sum(-1, keepdims=True) + 1e-09) * ROUTE_SCALE
            return (w.astype(xf.dtype), idx)

        def _forward(x, wg, w1, w2, w3, sw1, sw2, sw3):
            shape = x.shape
            xf = x.reshape(-1, DIM)
            N = xf.shape[0]
            cap = max(1, int(CAP_FACTOR * N * K / E))
            w, idx = _gate(xf, wg)
            fe = idx.reshape(-1)
            oh = jax.nn.one_hot(fe, E, dtype=jnp.int32)
            pos = (jnp.cumsum(oh, axis=0) * oh).sum(-1) - 1
            keep = pos < cap
            dest = jnp.where(keep, fe * cap + pos, E * cap)
            tok = jnp.arange(N * K, dtype=jnp.int32) // K
            buf_tok = jnp.full((E * cap + 1,), N, jnp.int32).at[dest].set(tok)[:-1]
            buf_w = jnp.zeros((E * cap + 1,), x.dtype).at[dest].set(w.reshape(-1))[:-1]
            xp = jnp.concatenate([xf, jnp.zeros((1, DIM), x.dtype)], axis=0)
            xe = xp[buf_tok].reshape(E, cap, DIM)
            h = jax.nn.silu(jnp.einsum('ecd,edh->ech', xe, w1)) * jnp.einsum('ecd,edh->ech', xe, w3)
            out = jnp.einsum('ech,ehd->ecd', h, w2) * buf_w.reshape(E, cap, 1)
            y = jnp.zeros((N + 1, DIM), x.dtype).at[buf_tok].add(out.reshape(E * cap, DIM))[:N]
            z = jax.nn.silu(xf @ sw1) * (xf @ sw3) @ sw2
            return (y + z).reshape(shape)
        return _forward(x, wg, w1, w2, w3, sw1, sw2, sw3)
    x = L0_attn_x
    x = x + _layernorm(_L0_attn_ref(_layernorm(x, axis=-1), L0_attn_ln1_w, L0_attn_ln1_b, L0_attn_Wqk, L0_attn_bqk, L0_attn_Wv, L0_attn_bv, L0_attn_Wg, L0_attn_bg, L0_attn_Wo, L0_attn_bo, L0_attn_ln2_w, L0_attn_ln2_b, L0_attn_gamma, L0_attn_beta, L0_attn_pos_emb), axis=-1)
    x = x + _layernorm(_L0_ffn_ref(_layernorm(x, axis=-1), L0_ffn_wg, L0_ffn_w1, L0_ffn_w2, L0_ffn_w3, L0_ffn_sw1, L0_ffn_sw2, L0_ffn_sw3), axis=-1)
    return x

_drawn_inputs = setup_inputs


def setup_inputs(seed=0):
    import zlib

    import numpy as np

    out = dict(_drawn_inputs(seed))
    spreads = {'L0_attn_ln1_w': (1.0, 0.2),
     'L0_attn_ln1_b': (0.0, 0.1),
     'L0_attn_bqk': (0.0, 2.0),
     'L0_attn_bv': (0.0, 0.1),
     'L0_attn_bg': (0.0, 0.1),
     'L0_attn_bo': (0.0, 0.1),
     'L0_attn_ln2_w': (1.0, 0.2),
     'L0_attn_ln2_b': (0.0, 0.1),
     'L0_attn_beta': (0.0, 0.8)}
    factors = {'L0_attn_Wqk': 8.0, 'L0_attn_gamma': 8.0}
    for name, (base, spread) in spreads.items():
        noise = np.random.default_rng([zlib.crc32(name.encode()), seed]).standard_normal(out[name].shape)
        drawn = base * np.exp(spread * noise) if base else spread * noise
        out[name] = jnp.asarray(drawn.astype(out[name].dtype))
    for name, factor in factors.items():
        out[name] = (out[name] * factor).astype(out[name].dtype)
    return out
```

```python
import concourse.bass as bass
from concourse import mybir
from contextlib import ExitStack

P = 128
EPS = 1e-5


def build_program(nc, x, wqk_t, wv_t, wg_t, wo_t, ln1_w, ln1_b, bqk, bg, bv, bo, ln2_w, ln2_b,
                  gamma, beta, pos_emb, rope, consts, token_ids, route_t, w1, w2, w3, sw1, sw2, sw3, out):
    F32, F32R, I32, U32, BF16 = (mybir.dt.float32, mybir.dt.float32r, mybir.dt.int32,
                                 mybir.dt.uint32, mybir.dt.bfloat16)
    ALU, ACT = mybir.AluOpType, mybir.ActivationFunctionType
    AX = mybir.AxisListType.X

    NT, D = x.shape
    NBATCH = 2
    S = NT // NBATCH
    H = wv_t.shape[1]
    QK = wqk_t.shape[1]
    HALF = QK // 2
    BLK = 512
    TB = BLK // P
    NB = S // BLK
    KD, KH = D // P, H // P
    E = w1.shape[0]
    TOPK = 4
    GRP, EG = 8, E // 8
    CAP = max(1, int(1.25 * NT * TOPK / E))
    ST = CAP // P
    CH = 2
    NCH = ST // CH
    NSLOT = E * CAP
    NROW = NT * TOPK
    REC = 3
    FAR = 1 << 20
    G64 = 64
    ZW = 1024
    NPOS = pos_emb.shape[0]
    MAXREL = (NPOS - 1) // 2
    NBLK = NBATCH * NB

    def dram(name, shape, dt):
        return nc.dram_tensor(name, shape, dt).ap()

    xt_d = dram("xt_d", [NBLK, P, KD * BLK], F32)
    x2_d = dram("x2_d", [NT, D], F32)
    xf_d = dram("xf_d", [NT + P, D], F32)
    slot_d = dram("slot_d", [NSLOT, REC], I32)
    y4_d = dram("y4_d", [NROW, D], F32)
    toep_d = dram("toep_d", [G64 * 2 * G64], F32)

    ctx = ExitStack()
    with ctx:
        def sb(name, shape, dt, c=ctx):
            return c.enter_context(nc.sbuf_tensor(name, shape, dt))

        def sem(name):
            return ctx.enter_context(nc.semaphore(name))

        cst = sb("cst", [P, consts.shape[1]], F32)
        ident = cst[:, 0:P]
        off_block = cst[:, 2 * P:3 * P]
        iota_e = cst[:, 3 * P:3 * P + E]
        eps = sb("eps", [P, 2], F32)
        gate_cell = sb("gate_cell", [P, 1], F32)

        cA = ExitStack()
        tri = sb("tri", [P, P], BF16, cA)
        ones_b = sb("ones_b", [P, P], BF16, cA)
        tok_id = sb("tok_id", [P, TB * TOPK * 2], I32, cA)
        zero = sb("zero", [P, ZW], F32, cA)
        kvh, kvl = sb("kvh", [P, H], F32R, cA), sb("kvl", [P, H], F32R, cA)
        bias_s = sb("bias_s", [P, P], F32, cA)
        wqh, wql = sb("wqh", [P, KD, QK], F32R, cA), sb("wql", [P, KD, QK], F32R, cA)
        wvh, wvl, wgh, wgl = (sb(n, [P, KD, H], F32R, cA) for n in ("wvh", "wvl", "wgh", "wgl"))
        wo = sb("wo", [P, KH, D], F32, cA)
        wr = sb("wr", [P, KD, E], F32, cA)
        ones_r = sb("ones_r", [P, P], F32R, cA)
        qb_r = sb("qb_r", [P, QK], F32R, cA)
        vb_r = sb("vb_r", [P, H], F32R, cA)
        ob_r = sb("ob_r", [P, D], F32R, cA)
        gb = sb("gb", [P, KH], F32, cA)
        gam, bet = sb("gam", [P, 4 * QK], F32, cA), sb("bet", [P, 4 * QK], F32, cA)
        w2b, b2b = sb("w2b", [P, D], F32, cA), sb("b2b", [P, D], F32, cA)
        cos, sin = sb("cos", [P, S // P, HALF], F32, cA), sb("sin", [P, S // P, HALF], F32, cA)
        qo_all = sb("qo_all", [P, KH, S], F32, cA)
        lq_all = sb("lq_all", [P, S], F32, cA)
        xh, xl = sb("xh", [P, KD, BLK], F32R, cA), sb("xl", [P, KD, BLK], F32R, cA)
        hit_all, hit_was = sb("hit_all", [P, E], F32, cA), sb("hit_was", [P, E], BF16, cA)
        base_f = sb("base_f", [P, TB * TOPK * 2], F32, cA)

        c0 = ExitStack()
        wraw = sb("wraw", [P, 2, KD, H], F32, c0)
        wscl = sb("wscl", [P, KD, H], F32, c0)
        qraw, qscl = sb("qraw", [P, KD, QK], F32, c0), sb("qscl", [P, KD, QK], F32, c0)
        l1w, l1b = sb("l1w", [P, KD], F32, c0), sb("l1b", [P, KD], F32, c0)
        bmat = sb("bmat", [P, KD, P], F32, c0)
        vb, vbh, vbl = sb("vb", [P, H], F32, c0), sb("vbh", [P, H], F32R, c0), sb("vbl", [P, H], F32R, c0)
        ob, obh, obl = sb("ob", [P, D], F32, c0), sb("obh", [P, D], F32R, c0), sb("obl", [P, D], F32R, c0)
        qb, qbh, qbl = sb("qb", [P, QK], F32, c0), sb("qbh", [P, QK], F32R, c0), sb("qbl", [P, QK], F32R, c0)
        gbi = sb("gbi", [P, KH], F32, c0)
        pe_row = sb("pe_row", [G64, NPOS], F32, c0)
        ext = sb("ext", [G64, 2 * G64], F32, c0)
        toep = sb("toep", [P, P], F32, c0)
        free_rec = sb("free_rec", [P, NSLOT * REC // P], I32, c0)
        c0.close()

        c1 = ExitStack()
        xa = sb("xa", [P, TB, D], F32, c1)
        xn = sb("xn", [P, TB, D], F32, c1)
        xta = sb("xta", [P, KD, BLK], F32, c1)
        u = sb("u", [P, TB, QK], F32, c1)
        hd = sb("hd", [P, TB, 4, QK], F32, c1)
        prod = [sb(f"prod{i}", [P, TB, 4, HALF], F32, c1) for i in range(4)]
        hr = sb("hr", [P, TB, 4, QK], F32, c1)
        pbh, pbl = sb("pbh", [P, TB, 2 * QK], F32R, c1), sb("pbl", [P, TB, 2 * QK], F32R, c1)
        qqt, kkt = sb("qqt", [QK, BLK], F32, c1), sb("kkt", [QK, BLK], F32, c1)
        vt = [sb(f"vt{i}", [P, H], F32, c1) for i in range(2)]
        vh, vl = sb("vh", [P, TB, H], F32R, c1), sb("vl", [P, TB, H], F32R, c1)
        sc, at = sb("sc", [P, BLK], F32, c1), sb("at", [P, BLK], F32, c1)
        ath, atl = sb("ath", [P, BLK], F32R, c1), sb("atl", [P, BLK], F32R, c1)
        st_a = sb("st_a", [P, TB, 6], F32, c1)
        mv_a = sb("mv_a", [P, TB, 2], F32, c1)
        sd_a, rs_a, nm_a = (sb(n, [P, TB], F32, c1) for n in ("sd_a", "rs_a", "nm_a"))
        c1.close()

        c2 = ExitStack()
        xb = sb("xb", [P, TB, D], F32, c2)
        xtb = sb("xtb", [P, KD, BLK], F32, c2)
        lqh, lql = sb("lqh", [P, BLK], F32R, c2), sb("lql", [P, BLK], F32R, c2)
        gsb = [sb(f"gsb{i}", [P, BLK], F32, c2) for i in range(2)]
        mixed = [sb(f"mixed{i}", [P, BLK], F32, c2) for i in range(2)]
        og = sb("og", [P, KH, BLK], F32, c2)
        yb = sb("yb", [P, TB, D], F32, c2)
        x2b = sb("x2b", [P, TB, D], F32, c2)
        xfb = sb("xfb", [P, TB, D], F32, c2)
        xft = sb("xft", [P, KD, BLK], F32, c2)
        st_b = sb("st_b", [P, TB, 6], F32, c2)
        mv_b = sb("mv_b", [P, TB, 2], F32, c2)
        sd_b, rs_b, nm_b = (sb(n, [P, TB], F32, c2) for n in ("sd_b", "rs_b", "nm_b"))
        lg = sb("lg", [P, TB, E], F32, c2)
        pr = sb("pr", [P, TB, E], F32, c2)
        mx, sm, rsm = (sb(n, [P, TB], F32, c2) for n in ("mx", "sm", "rsm"))
        gs = sb("gs", [P, TB, GRP], F32, c2)
        top_g, top_e = sb("top_g", [P, TB, 8], F32, c2), sb("top_e", [P, TB, 8], F32, c2)
        ix_g, ix_e = sb("ix_g", [P, TB, 8], U32, c2), sb("ix_e", [P, TB, 8], U32, c2)
        fx_g, fx_e = sb("fx_g", [P, TB, 8], F32, c2), sb("fx_e", [P, TB, 8], F32, c2)
        eq_g = sb("eq_g", [P, TB, TOPK, GRP], F32, c2)
        keep, kneg = sb("keep", [P, TB, GRP], F32, c2), sb("kneg", [P, TB, GRP], F32, c2)
        msk = sb("msk", [P, TB, E], F32, c2)
        oh = sb("oh", [P, TB, TOPK, E], F32, c2)
        ohp = sb("ohp", [P, TB, TOPK, E], F32, c2)
        hit = sb("hit", [P, TB, E], BF16, c2)
        hsum = sb("hsum", [P, E], F32, c2)
        wsum, wrec = sb("wsum", [P, TB], F32, c2), sb("wrec", [P, TB], F32, c2)
        pos, dst, over = (sb(n, [P, TB, TOPK], F32, c2) for n in ("pos", "dst", "over"))
        dsti = sb("dsti", [P, TB * TOPK], I32, c2)
        rec = sb("rec", [P, TB * TOPK, REC], I32, c2)
        c2.close()
        cA.close()

        c3 = ExitStack()
        NXB = 5
        wld = sb("wld", [P, 3, KD, D], F32, c3)
        wh = [sb(f"wh{i}", [P, 3, KD, D], F32R, c3) for i in range(2)]
        wl = [sb(f"wl{i}", [P, 3, KD, D], F32R, c3) for i in range(2)]
        gix = [sb(f"gix{i}", [P, ST, REC], I32, c3) for i in range(2)]
        six = [sb(f"six{i}", [P, ST, REC], I32, c3) for i in range(2)]
        xg = [sb(f"xg{i}", [P, CH, D], F32, c3) for i in range(NXB)]
        eh = [sb(f"eh{i}", [P, KD, CH * P], F32R, c3) for i in range(2)]
        el = [sb(f"el{i}", [P, KD, CH * P], F32R, c3) for i in range(2)]
        sa = [sb(f"sa{i}", [P, KD, CH * P], F32, c3) for i in range(2)]
        hf = [sb(f"hf{i}", [P, KD, CH * P], F32, c3) for i in range(2)]
        hh = [sb(f"hh{i}", [P, KD, CH * P], F32R, c3) for i in range(2)]
        hl = [sb(f"hl{i}", [P, KD, CH * P], F32R, c3) for i in range(2)]
        sx = [sb(f"sx{i}", [P, CH, REC], I32, c3) for i in range(NXB)]
        eo = [sb(f"eo{i}", [P, CH, D], F32, c3) for i in range(NXB)]
        GC = 4
        y4 = [sb(f"y4{i}", [P, CH, TOPK, D], F32, c3) for i in range(GC)]
        xr = [sb(f"xr{i}", [P, CH, D], F32, c3) for i in range(GC)]
        ysum = [sb(f"ysum{i}", [P, CH, 2, D], F32, c3) for i in range(2)]
        ytot = [sb(f"ytot{i}", [P, CH, D], F32, c3) for i in range(GC)]
        yout = [sb(f"yout{i}", [P, CH, D], F32, c3) for i in range(GC)]
        st_c = sb("st_c", [P, CH, 6], F32, c3)
        mv_c = sb("mv_c", [P, GC * CH, 2], F32, c3)
        sd_c, rs_c, nm_c = (sb(n, [P, GC * CH], F32, c3) for n in ("sd_c", "rs_c", "nm_c"))
        c3.close()

        bank = [ctx.enter_context(nc.psum_tensor(f"bank{i}", [P, 512], F32)) for i in range(8)]

        s_load, s_pos, s_ext, s_toep, s_tl, s_clear = (sem(n) for n in ("s_load", "s_pos", "s_ext", "s_toep", "s_tl", "s_clear"))
        s_dve, s_act, s_pe, s_zero = sem("s_dve"), sem("s_act"), sem("s_pe"), sem("s_zero")
        ph = {n: sem(f"ph_{n}") for n in ("sp", "act", "dve", "pe", "pool")}
        past = {nc.sync: sem("past_sp"), nc.gpsimd: sem("past_pool")}
        ld_x, st_xt, ld_xt = sem("ld_x"), sem("st_xt"), sem("ld_xt")
        a_sd, a_xt, a_xh, a_u, a_ta, a_v, a_vh, a_pbh, a_ath, a_qo, a_kvh = (sem(n) for n in (
            "a_sd", "a_xt", "a_xh", "a_u", "a_ta", "a_v", "a_vh", "a_pbh", "a_ath", "a_qo", "a_kvh"))
        d_stat, d_rs, d_xl, d_prod, d_head, d_pbl, d_vl, d_tab, d_at, d_atl = (sem(n) for n in (
            "d_stat", "d_rs", "d_xl", "d_prod", "d_head", "d_pbl", "d_vl", "d_tab", "d_at", "d_atl"))
        g_xn, g_gam, g_hd, g_rec = sem("g_xn"), sem("g_gam"), sem("g_hd"), sem("g_rec")
        o_ln, o_rs, o_at, o_kv = sem("o_ln"), sem("o_rs"), sem("o_at"), sem("o_kv")
        p_x, p_u, p_v, p_ta, p_tb, p_kv, p_s, p_qo = (sem(n) for n in (
            "p_x", "p_u", "p_v", "p_ta", "p_tb", "p_kv", "p_s", "p_qo"))
        ld_xb, st_x2, st_xf, st_rec = sem("ld_xb"), sem("st_x2"), sem("st_xf"), sem("st_rec")
        a_bxh, a_lqh, a_gs, a_ln, a_xft, a_exp = (sem(n) for n in ("a_bxh", "a_lqh", "a_gs", "a_ln", "a_xft", "a_exp"))
        d_bxl, d_lql, d_mix, d_og, d_ln, d_lg, d_hit, d_rec = (sem(n) for n in (
            "d_bxl", "d_lql", "d_mix", "d_og", "d_ln", "d_lg", "d_hit", "d_rec"))
        o_ch, o_rt, o_fin = sem("o_ch"), sem("o_rt"), sem("o_fin")
        p_g, p_lo, p_wo, p_xt, p_lg, p_cs = (sem(n) for n in ("p_g", "p_lo", "p_wo", "p_xt", "p_lg", "p_cs"))
        ld_w, ld_gix, ld_six = sem("ld_w"), [sem("ld_gix0"), sem("ld_gix1")], [sem("ld_six0"), sem("ld_six1")]
        ld_xg = [sem(f"ld_xg{i}") for i in range(NXB)]
        st_eo = [sem(f"st_eo{i}") for i in range(NXB)]
        a_wh, a_eh, a_sa, a_hh, a_eo = (sem(n) for n in ("a_wh", "a_eh", "a_sa", "a_hh", "a_eo"))
        d_wl, d_el, d_hf, d_hl, d_sx = (sem(n) for n in ("d_wl", "d_el", "d_hf", "d_hl", "d_sx"))
        p_et, p_up, p_dn = sem("p_et"), sem("p_up"), sem("p_dn")
        ld_c, ld_y, ld_r, st_out = ([sem(f"{n}{i}") for i in range(GC)] for n in ("ld_c", "ld_y", "ld_r", "st_out"))
        g_ys, d_acc, d_tot, d_cst, d_crs, d_out = (sem(n) for n in ("g_ys", "d_acc", "d_tot", "d_cst", "d_crs", "d_out"))
        a_csd, a_cn, o_c, o_cr = sem("a_csd"), sem("a_cn"), sem("o_c"), sem("o_cr")

        block = ctx.enter_context(nc.Block())

        class Own:

            def __init__(self, eng, s, base):
                self.eng, self.s, self.base, self.n = eng, s, base, 0

            def step(self, ins):
                self.n += 1
                ins.then_inc(self.s, 1)

            def wait(self):
                self.eng.wait_ge(self.s, self.base + self.n)

        def settled(eng):
            eng.sem_inc(past[eng], 1)

        def meet(eng, name, n):
            eng.drain().then_inc(ph[name], 1)
            for other in ph:
                if other != name:
                    eng.wait_ge(ph[other], n)
            if eng in past:
                settled(eng)

        def attention(eng, name, pass_a, pass_b):
            with eng.Fori(0, NBATCH) as b:
                pass_a(b)
                meet(eng, name, b * 2 + 2)
                pass_b(b)
                meet(eng, name, b * 2 + 3)

        def blocks(eng, b, body):
            body(b * NB, 0, False, True)
            with eng.Fori(1, NB - 1) as m:
                body(b * NB + m, m, True, True)
            body(b * NB + (NB - 1), NB - 1, True, False)

        def cols(m):
            return bass.ds(m * BLK, BLK)

        QO_BANK = (6, 3, 4, 6)

        @block.sync
        def _(sp):
            for dst_, src in (
                (cst[:, :], consts), (tok_id[:, :], token_ids),
                (cos[:, :, :], rope[0]), (sin[:, :, :], rope[1]),
                (qraw[:, :, :], wqk_t.rearrange("(k p) n -> p k n", p=P)),
                (wraw[:, 0], wv_t.rearrange("(k p) n -> p k n", p=P)),
                (wraw[:, 1], wg_t.rearrange("(k p) n -> p k n", p=P)),
                (wo[:, :, :], wo_t.rearrange("(k p) n -> p k n", p=P)),
                (wr[:, :, :], route_t.rearrange("(k p) n -> p k n", p=P)),
                (l1w[:, :], ln1_w), (l1b[:, :], ln1_b), (gbi[:, :], bg),
                (gam[:, :], gamma.partition_broadcast(P)), (bet[:, :], beta.partition_broadcast(P)),
                (vb[:, :], bv.partition_broadcast(P)), (ob[:, :], bo.partition_broadcast(P)),
                (qb[:, :], bqk.partition_broadcast(P)),
                (w2b[:, :], ln2_w.partition_broadcast(P)), (b2b[:, :], ln2_b.partition_broadcast(P)),
                (pe_row[:, :], pos_emb.partition_broadcast(G64)),
            ):
                sp.dma_start(dst_, src).then_inc(s_load, 16)
            sp.wait_ge(s_ext, 4)
            W = 2 * G64 - 1
            sp.dma_start(toep_d[0:G64 * W].rearrange("(a c) -> a c", c=W), ext[:, 0:W]).then_inc(s_toep, 16)
            sp.wait_ge(s_toep, 16)
            src = toep_d[G64 - 1:G64 - 1 + G64 * (W - 1)].rearrange("(a c) -> a c", c=W - 1)[:, 0:G64]
            for q in range(2):
                sp.dma_start(toep[q * G64:(q + 1) * G64, q * G64:(q + 1) * G64], src).then_inc(s_tl, 16)
            sp.wait_ge(s_zero, 4)
            sp.dma_start(slot_d.rearrange("(p s) r -> p (s r)", p=P), free_rec[:, :]).then_inc(s_clear, 16)
            sp.dma_start(xf_d[NT:NT + P, :], zero[:, 0:D]).then_inc(s_clear, 16)
            sp.wait_ge(s_clear, 32)
            for s in st_out:
                sp.sem_inc(s, 16)
            meet(sp, "sp", 1)

            y4_rows = y4_d.rearrange("(n p r) d -> n p (r d)", p=P, r=ZW // D)   
            clears = y4_rows.shape[0] // NBLK

            def load_x(dst_, g, done):
                sp.dma_start(dst_[:, :, :], x[bass.ds(g * BLK, BLK), :].rearrange("(t p) d -> p t d", p=P)) \
                  .then_inc(done, 16)

            def pass_a(b):
                load_x(xa, b * NB, ld_x)

                def body(g, m, has_prev, has_next):
                    sp.wait_ge(a_xt, g + 1)
                    sp.dma_start(xt_d[g, :, :], xta[:, :, :]).then_inc(st_xt, 16)
                    if has_next:
                        sp.wait_ge(g_xn, g + 1)
                        load_x(xa, g + 1, ld_x)
                    for n in range(clears):
                        sp.dma_start(y4_rows[g * clears + n, :, :], zero[:, :]).then_inc(s_clear, 16)

                blocks(sp, b, body)
                sp.wait_ge(st_xt, (b + 1) * (16 * NB))
                settled(sp)

            def pass_b(b):
                def load_xt(g):
                    sp.dma_start(xtb[:, :, :], xt_d[g, :, :]).then_inc(ld_xt, 16)

                load_xt(b * NB)
                load_x(xb, b * NB, ld_xb)

                def body(g, m, has_prev, has_next):
                    if has_next:
                        sp.wait_ge(d_bxl, g + 1)
                        load_xt(g + 1)
                    sp.wait_ge(d_ln, g * 6 + 5)
                    if has_next:
                        load_x(xb, g + 1, ld_xb)
                    sp.dma_start(x2_d[bass.ds(g * BLK, BLK), :].rearrange("(t p) d -> p t d", p=P), x2b[:, :, :]) \
                      .then_inc(st_x2, 16)
                    sp.wait_ge(a_ln, g * 6 + 6)
                    sp.dma_start(xf_d[bass.ds(g * BLK, BLK), :].rearrange("(t p) d -> p t d", p=P), xfb[:, :, :]) \
                      .then_inc(st_xf, 16)

                blocks(sp, b, body)
                for s in (st_x2, st_xf):
                    sp.wait_ge(s, (b + 1) * (16 * NB))
                settled(sp)

            attention(sp, "sp", pass_a, pass_b)
            sp.wait_ge(s_clear, 32 + 16 * clears * NBLK)
            meet(sp, "sp", 6)

            slots = slot_d.rearrange("(e p s) r -> e p (s r)", p=P, s=ST)

            def load_w(e):
                for j, w in enumerate((w1, w3, w2)):
                    sp.dma_start(wld[:, j], w[e, :, :].rearrange("(k p) n -> p k n", p=P)).then_inc(ld_w, 16)

            def load_gix(e, q):
                sp.dma_start(gix[q][:, :, :], slots[e, :, :]).then_inc(ld_gix[q], 16)

            def load_six(e, q):
                sp.dma_start(six[q][:, :, :], slots[e, :, :]).then_inc(ld_six[q], 16)

            load_gix(0, 0)
            load_w(0)
            load_six(0, 0)

            def pair(i, first, last):
                for q in range(2):
                    e = i * 2 + q
                    if last and q == 1:
                        sp.wait_ge(d_wl, e + 1)
                        for j, w in enumerate((sw1, sw3, sw2)):
                            sp.dma_start(wld[:, j], w.rearrange("(k p) n -> p k n", p=P)).then_inc(ld_w, 16)
                        continue
                    if not (first and q == 0):
                        sp.wait_ge(p_et, e * NCH)
                    load_gix(e + 1, 1 - q)
                    sp.wait_ge(d_wl, e + 1)
                    load_w(e + 1)
                    if not (first and q == 0):
                        sp.wait_ge(d_sx, e * NCH)
                    load_six(e + 1, 1 - q)

            pair(0, True, False)
            with sp.Fori(1, E // 2 - 1) as i:
                pair(i, False, False)
            pair(E // 2 - 1, False, True)
            meet(sp, "sp", 7)

            NC = NT // (CH * P)

            def load_c(n, q):
                sp.dma_start(xg[q][:, :, :], xf_d[bass.ds(n * CH * P, CH * P), :].rearrange("(p t) d -> p t d", t=CH)) \
                  .then_inc(ld_c[q], 16)

            def load_y(n, q):
                sp.dma_start(y4[q][:, :, :, :], y4_d[bass.ds(n * CH * P * TOPK, CH * P * TOPK), :]
                             .rearrange("(p t k) d -> p t k d", t=CH, k=TOPK)).then_inc(ld_y[q], 16)

            def load_r(n, q):
                sp.dma_start(xr[q][:, :, :], x2_d[bass.ds(n * CH * P, CH * P), :].rearrange("(p t) d -> p t d", t=CH)) \
                  .then_inc(ld_r[q], 16)

            def store(n, q):
                sp.wait_ge(d_out, n + 1)
                sp.dma_start(out[bass.ds(n * CH * P, CH * P), :].rearrange("(p t) d -> p t d", t=CH), yout[q][:, :, :]) \
                  .then_inc(st_out[q], 16)

            for q in range(GC):
                load_c(q, q)
                load_y(q, q)

            def group(i, first, last):
                for q in range(GC):
                    n = i * GC + q
                    if not last:
                        sp.wait_ge(p_et, n + (E * NCH + 1))
                        load_c(n + GC, q)
                        sp.wait_ge(g_ys, n + 1)
                        load_y(n + GC, q)
                    if not first:
                        store(n - GC, q)
                    load_r(n, q)

            group(0, True, False)
            with sp.Fori(1, NC // GC - 1) as i:
                group(i, False, False)
            group(NC // GC - 1, False, True)
            for q in range(GC):
                store(NC - GC + q, q)
            for q in range(GC):
                sp.wait_ge(st_out[q], 16 * (NC // GC) + 16)

        @block.gpsimd
        def _(pool):
            nc.gpsimd.memset(zero[:, :], 0.0).then_inc(s_zero, 1)
            fr = free_rec[:, :].rearrange("p (s r) -> p s r", r=REC)
            nc.gpsimd.memset(fr[:, :, 0:1], NT).then_inc(s_zero, 1)
            nc.gpsimd.memset(fr[:, :, 1:2], FAR).then_inc(s_zero, 1)
            nc.gpsimd.memset(fr[:, :, 2:3], 0).then_inc(s_zero, 1)
            pool.sem_inc(g_rec, 1)
            meet(pool, "pool", 1)

            def pass_a(b):
                def normalise(g, has_prev):
                    pool.wait_ge(d_rs, g + 1)
                    if has_prev:
                        pool.wait_ge(p_x, g * KD)
                    settled(pool)
                    for t in range(TB):
                        ins = nc.gpsimd.tensor_scalar(xn[:, t, :], xa[:, t, :], rs_a[:, t:t + 1], nm_a[:, t:t + 1],
                                                      ALU.mult, ALU.add)
                    ins.then_inc(g_xn, 1)

                def heads(g, has_prev):
                    pool.wait_ge(a_u, g + 1)
                    if has_prev:
                        pool.wait_ge(d_prod, g)
                    nc.gpsimd.tensor_tensor(hd[:, :, :, :], u[:, :, :].unsqueeze(2).to_broadcast([P, TB, 4, QK]),
                                            gam[:, :].rearrange("p (h d) -> p h d", h=4).unsqueeze(1)
                                            .to_broadcast([P, TB, 4, QK]), ALU.mult).then_inc(g_gam, 1)
                    pool.wait_ge(g_gam, g + 1)
                    h3 = hd[:, :, :, :].rearrange("p t h d -> p t (h d)")
                    nc.gpsimd.tensor_tensor(h3, h3, bet[:, :].unsqueeze(1).to_broadcast([P, TB, 4 * QK]), ALU.add) \
                        .then_inc(g_hd, 1)

                normalise(b * NB, False)

                def body(g, m, has_prev, has_next):
                    heads(g, has_prev)
                    if has_next:
                        normalise(g + 1, True)

                blocks(pool, b, body)

            def pass_b(b):
                def scatter(g):
                    pool.wait_ge(d_rec, g + 2)
                    settled(pool)
                    for j in range(TB * TOPK):
                        pool.indirect_dma_start(
                            slot_d, bass.IndirectOffsetOnAxis(ap=dsti[:, j:j + 1], axis=0), rec[:, j, :], None,
                            bounds_check=NSLOT - 1, oob_is_err=False).then_inc(st_rec, 16)
                    pool.wait_ge(st_rec, (g + 1) * (16 * TB * TOPK))
                    pool.sem_inc(g_rec, 1)

                with pool.Fori(0, NB) as m:
                    scatter(b * NB + m)

            attention(pool, "pool", pass_a, pass_b)
            meet(pool, "pool", 6)

            def gather(c, i, first):
                i, c = (i + 1, c - 2 * NCH) if c >= 2 * NCH else (i, c)
                e, q, buf = i * 2 + c // NCH, c // NCH, c % NXB
                if c % NCH == 0:
                    pool.wait_ge(ld_gix[q], (i + 1) * 16)
                if not first:
                    pool.wait_ge(p_et, i * (2 * NCH) + (c - NXB + 1))
                settled(pool)
                for t in range(CH):
                    s = (c % NCH) * CH + t
                    pool.indirect_dma_start(xg[buf][:, t, :], None, xf_d,
                                            bass.IndirectOffsetOnAxis(ap=gix[q][:, s, 0:1], axis=0)) \
                        .then_inc(ld_xg[buf], 16)

            def put(c, i):
                buf = c % NXB
                pool.wait_ge(a_eo, i * (2 * NCH) + (c + 1))
                settled(pool)
                for t in range(CH):
                    pool.indirect_dma_start(y4_d, bass.IndirectOffsetOnAxis(ap=sx[buf][:, t, 1:2], axis=0),
                                            eo[buf][:, t, :], None, bounds_check=NROW - 1, oob_is_err=False) \
                        .then_inc(st_eo[buf], 16)

            AHEAD = 3
            for c in range(AHEAD):
                gather(c, 0, True)

            def pair(i, first, last):
                for c in range(2 * NCH):
                    if not (last and c + AHEAD >= 2 * NCH):
                        gather(c + AHEAD, i, first and c + AHEAD < NXB)
                    if c > 0:
                        put(c - 1, i)
                put(2 * NCH - 1, i)

            pair(0, True, False)
            with pool.Fori(1, E // 2 - 1) as i:
                pair(i, False, False)
            pair(E // 2 - 1, False, True)
            for buf in range(NXB):
                pool.wait_ge(st_eo[buf], E * NCH // NXB * 16 * CH)
            meet(pool, "pool", 7)

            def add_rows(n, q, i, first):
                pool.wait_ge(ld_y[q], i * 16 + 16)
                if not first:
                    pool.wait_ge(d_tot, n - 1)
                nc.gpsimd.tensor_tensor(ysum[q % 2][:, :, :, :], y4[q][:, :, 0:2, :], y4[q][:, :, 2:4, :], ALU.add) \
                    .then_inc(g_ys, 1)

            def group(i, first):
                for q in range(GC):
                    add_rows(i * GC + q, q, i, first and q < 2)

            group(0, True)
            with pool.Fori(1, NT // (CH * P) // GC) as i:
                group(i, False)

        @block.scalar
        def _(act):
            act.wait_ge(s_load, 16 * 20)
            act.wait_ge(s_dve, 6)
            nc.scalar.activation(wqh[:, :, :], qscl[:, :, :], ACT.Copy).then_inc(s_act, 1)
            for j, w in enumerate((wvh, wgh)):
                act.wait_ge(s_dve, 8 + 2 * j)
                nc.scalar.activation(w[:, :, :], wscl[:, :, :], ACT.Copy).then_inc(s_act, 1)
            act.wait_ge(s_dve, 17)
            nc.scalar.activation(vbh[:, :], vb[:, :], ACT.Copy).then_inc(s_act, 1)
            nc.scalar.activation(qbh[:, :], qb[:, :], ACT.Copy).then_inc(s_act, 1)
            nc.scalar.activation(obh[:, :], ob[:, :], ACT.Copy).then_inc(s_act, 1)
            meet(act, "act", 1)

            def pass_a(b):
                def sqrt_x(g):
                    act.wait_ge(d_stat, g + 1)
                    nc.scalar.activation(sd_a[:, :], mv_a[:, :, 1], ACT.Sqrt, bias=eps[:, 1:2], scale=1.0 + EPS) \
                        .then_inc(a_sd, 1)

                def x_high(g, m, first):
                    for k in range(KD):
                        act.wait_ge(p_x, g * KD + (k + 1))
                        if k == 0 and not first:
                            act.wait_ge(st_xt, g * 16)
                        ins = nc.scalar.activation(xta[:, k, :], bank[k][:, :], ACT.Copy)
                        if k == KD - 1:
                            ins.then_inc(a_xt, 1)
                        if k == 0 and not first:
                            act.wait_ge(p_v, g * TB)
                        nc.scalar.activation(xh[:, k, :], bank[k][:, :], ACT.Copy).then_inc(a_xh, 1)

                def values_out(g, m):
                    for c in range(KH):
                        act.wait_ge(p_qo, g * KH + (c + 1))
                        nc.scalar.activation(qo_all[:, c, cols(m)], bank[QO_BANK[c]][:, :], ACT.Copy).then_inc(a_qo, 1)

                sqrt_x(b * NB)
                x_high(b * NB, 0, True)

                def body(g, m, has_prev, has_next):
                    act.wait_ge(p_u, g + 1)
                    if has_prev:
                        act.wait_ge(g_gam, g)
                    nc.scalar.activation(u[:, :, :], bank[2][:, 0:TB * QK].rearrange("p (t d) -> p t d", t=TB),
                                         ACT.Silu).then_inc(a_u, 1)
                    if has_next:
                        sqrt_x(g + 1)
                    if has_prev:
                        values_out(g - 1, m - 1)
                    for t in range(TB):
                        act.wait_ge(p_v, g * TB + (t + 1))
                        if t >= 2 or has_prev:
                            act.wait_ge(d_vl, g * TB + (t - 1))
                        nc.scalar.activation(vt[t % 2][:, :], bank[t % 2][:, :], ACT.Silu).then_inc(a_v, 1)
                        act.wait_ge(a_v, g * TB + (t + 1))
                        nc.scalar.activation(vh[:, t, :], vt[t % 2][:, :], ACT.Copy).then_inc(a_vh, 1)
                        if t == 1:
                            act.wait_ge(d_head, g + 1)
                            nc.scalar.activation(pbh[:, :, :], hr[:, :, 2:4, :].rearrange("p t h d -> p t (h d)"), ACT.Copy) \
                                .then_inc(a_pbh, 1)
                    act.wait_ge(p_ta, g + 1)
                    nc.scalar.activation(lq_all[QK:2 * QK, cols(m)], bank[3][QK:2 * QK, :], ACT.Copy).then_inc(a_ta, 1)
                    if has_next:
                        x_high(g + 1, m + 1, False)
                    act.wait_ge(d_at, g + 1)
                    nc.scalar.activation(ath[:, :], at[:, :], ACT.Copy).then_inc(a_ath, 1)

                blocks(act, b, body)
                values_out(b * NB + (NB - 1), NB - 1)
                act.wait_ge(p_kv, (b + 1) * (NB * TB))
                nc.scalar.activation(kvh[QK:2 * QK, :], bank[7][QK:2 * QK, :], ACT.Copy, scale=1.0 / S).then_inc(a_kvh, 1)

            def pass_b(b):
                def highs(g, m, has_prev):
                    if has_prev:
                        act.wait_ge(p_lo, g * KH)
                    act.wait_ge(ld_xt, g * 16 + 16)
                    nc.scalar.activation(xh[:, :, :], xtb[:, :, :], ACT.Copy).then_inc(a_bxh, 1)
                    nc.scalar.activation(lqh[QK:2 * QK, :], lq_all[QK:2 * QK, cols(m)], ACT.Copy).then_inc(a_lqh, 1)

                def gates(g, c, has_prev):
                    act.wait_ge(p_g, g * KH + (c + 1))
                    if c >= 2 or has_prev:
                        act.wait_ge(d_og, g * KH + (c - 1))
                    nc.scalar.activation(gsb[c % 2][:, :], bank[c % 2][:, :], ACT.Silu, bias=gb[:, c:c + 1]).then_inc(a_gs, 1)

                def root(g, n):
                    act.wait_ge(d_ln, g * 6 + n)
                    nc.scalar.activation(sd_b[:, :], mv_b[:, :, 1], ACT.Sqrt, bias=eps[:, 0:1]).then_inc(a_ln, 1)

                def norm(g, n, dst_, src):
                    act.wait_ge(d_ln, g * 6 + n)
                    for t in range(TB):
                        ins = nc.scalar.activation(dst_[:, t, :], src(t), ACT.Identity, bias=nm_b[:, t:t + 1],
                                                   scale=rs_b[:, t:t + 1])
                    ins.then_inc(a_ln, 1)

                def turn(g):
                    for k in range(KD):
                        act.wait_ge(p_xt, g * KD + (k + 1))
                        nc.scalar.activation(xft[:, k, :], bank[6 + k][:, :], ACT.Copy).then_inc(a_xft, 1)

                def expo(g):
                    act.wait_ge(d_lg, g + 1)
                    nc.scalar.activation(pr[:, :, :], lg[:, :, :], ACT.Exp).then_inc(a_exp, 1)

                highs(b * NB, 0, False)

                def body(g, m, has_prev, has_next):
                    for c in range(KH):
                        gates(g, c, has_prev)
                    if has_prev:
                        turn(g - 1)
                    if has_next:
                        highs(g + 1, m + 1, True)
                    if has_prev:
                        expo(g - 1)
                    root(g, 1)
                    norm(g, 2, yb, lambda t: bank[4 + t // 2][:, (t % 2) * D:(t % 2 + 1) * D])
                    root(g, 3)
                    norm(g, 4, yb, lambda t: yb[:, t, :])
                    root(g, 5)
                    if has_prev:
                        act.wait_ge(st_xf, g * 16)
                    norm(g, 6, xfb, lambda t: x2b[:, t, :])

                blocks(act, b, body)
                turn(b * NB + (NB - 1))
                expo(b * NB + (NB - 1))

            attention(act, "act", pass_a, pass_b)
            meet(act, "act", 6)

            def split_w(e, q):
                act.wait_ge(ld_w, (e + 1) * 48)
                for j in range(3):
                    nc.scalar.activation(wh[q][:, j], wld[:, j], ACT.Copy).then_inc(a_wh, 1)

            def e_high(n, q):
                act.wait_ge(p_et, n + 1)
                nc.scalar.activation(eh[q][:, :, :], bank[q][:, :].rearrange("p (k n) -> p k n", k=KD), ACT.Copy) \
                    .then_inc(a_eh, 1)

            def silu(n, q):
                act.wait_ge(p_up, n + 1)
                nc.scalar.activation(sa[q][:, :, :], bank[2 + q][:, :].rearrange("p (k n) -> p k n", k=KD), ACT.Silu) \
                    .then_inc(a_sa, 1)

            def h_high(n, q):
                act.wait_ge(d_hf, n + 1)
                nc.scalar.activation(hh[q][:, :, :], hf[q][:, :, :], ACT.Copy).then_inc(a_hh, 1)

            def weighted(c, i, first):
                buf, n = c % NXB, i * (2 * NCH) + c
                act.wait_ge(p_dn, n + 1)
                act.wait_ge(d_sx, n + 1)
                if not (first and c < NXB):
                    act.wait_ge(st_eo[buf], (i * 2 + c // NXB) * (16 * CH))
                for t in range(CH):
                    ins = nc.scalar.activation(eo[buf][:, t, :], bank[6 + c % 2][:, t * D:(t + 1) * D], ACT.Copy,
                                               scale=sx[buf][:, t, 2:3].bitcast(F32))
                ins.then_inc(a_eo, 1)

            split_w(0, 0)
            e_high(0, 0)

            def pair(i, first, last):
                for c in range(2 * NCH):
                    n = i * (2 * NCH) + c
                    if not (last and c == 2 * NCH - 1):
                        e_high(n + 1, (c + 1) % 2)
                    silu(n, c % 2)
                    h_high(n, c % 2)
                    if c > 0:
                        weighted(c - 1, i, first)
                    if c % NCH == 2:
                        split_w(i * 2 + (c // NCH + 1), (c // NCH + 1) % 2)
                weighted(2 * NCH - 1, i, first)

            pair(0, True, False)
            with act.Fori(1, E // 2 - 1) as i:
                pair(i, False, False)
            pair(E // 2 - 1, False, True)
            meet(act, "act", 7)

            NC, N0 = NT // (CH * P), E * NCH

            def c_root(i):
                act.wait_ge(d_cst, i * GC)
                nc.scalar.activation(sd_c[:, :], mv_c[:, :, 1], ACT.Sqrt, bias=eps[:, 0:1]).then_inc(a_csd, 1)
                act.wait_ge(d_crs, i)

            def c_norm(i, q):
                act.wait_ge(st_out[q], i * 16)
                for t in range(CH):
                    c = q * CH + t
                    ins = nc.scalar.activation(yout[q][:, t, :], ytot[q][:, t, :], ACT.Identity, bias=nm_c[:, c:c + 1],
                                               scale=rs_c[:, c:c + 1])
                ins.then_inc(a_cn, 1)

            e_high(N0, 0)

            def group(i, first, last):
                for q in range(GC):
                    n = i * GC + q
                    if not (last and q == GC - 1):
                        e_high(n + (N0 + 1), 1 - q % 2)
                    silu(n + N0, q % 2)
                    h_high(n + N0, q % 2)
                    if not first:
                        if q == 1:
                            c_root(i)
                            c_norm(i, 0)
                            c_norm(i, 1)
                        if q == 2:
                            c_norm(i, 2)
                            c_norm(i, 3)

            group(0, True, False)
            with act.Fori(1, NC // GC - 1) as i:
                group(i, False, False)
            group(NC // GC - 1, False, True)
            c_root(NC // GC)
            for q in range(GC):
                c_norm(NC // GC, q)

        @block.vector
        def _(dve):
            own = Own(dve, s_dve, 0)
            own.step(nc.vector.memset(eps[:, 0:1], EPS))
            own.step(nc.vector.memset(eps[:, 1:2], EPS * EPS))
            own.step(nc.vector.memset(hit_all[:, :], 0.0))
            own.step(nc.vector.memset(ones_b[:, :], 1.0))
            own.step(nc.vector.memset(ones_r[:, :].bitcast(F32), 1.0))
            dve.wait_ge(s_load, 16 * 20)
            for k in range(KD):
                ins = nc.vector.tensor_scalar(qscl[:, k, :], qraw[:, k, :], l1w[:, k:k + 1], None, ALU.mult)
            own.step(ins)
            dve.wait_ge(s_act, 1)
            own.wait()
            own.step(nc.vector.tensor_tensor(wql[:, :, :], qscl[:, :, :], wqh[:, :, :].bitcast(F32), ALU.subtract))
            for j, (hi, lo) in enumerate(((wvh, wvl), (wgh, wgl))):
                own.wait()
                for k in range(KD):
                    ins = nc.vector.tensor_scalar(wscl[:, k, :], wraw[:, j, k, :], l1w[:, k:k + 1], None, ALU.mult)
                own.step(ins)
                dve.wait_ge(s_act, j + 2)
                own.wait()
                own.step(nc.vector.tensor_tensor(lo[:, :, :], wscl[:, :, :], hi[:, :, :].bitcast(F32), ALU.subtract))
            for k in range(KD):
                own.step(nc.vector.tensor_copy(bmat[:, k, :], l1b[:, k:k + 1].to_broadcast([P, P])))
            dve.wait_ge(s_pe, 1)
            own.step(nc.vector.tensor_tensor(gb[:, :], bank[1][:, 0:KH], gbi[:, :], ALU.add))
            own.step(nc.vector.tensor_tensor(vb[:, :], bank[2][:, :], vb[:, :], ALU.add))
            own.step(nc.vector.tensor_tensor(qb[:, :], bank[0][:, 0:QK], qb[:, :], ALU.add))
            own.step(nc.vector.tensor_copy(tri[:, :], cst[:, P:2 * P]))
            for z in (vb_r, ob_r, qb_r, kvh, kvl):
                own.step(nc.vector.memset(z[:, :].bitcast(F32), 0.0))
            dve.wait_ge(s_act, 6)
            own.wait()
            own.step(nc.vector.tensor_tensor(vbl[:, :], vb[:, :], vbh[:, :].bitcast(F32), ALU.subtract))
            own.step(nc.vector.tensor_tensor(obl[:, :], ob[:, :], obh[:, :].bitcast(F32), ALU.subtract))
            own.step(nc.vector.tensor_tensor(qbl[:, :], qb[:, :], qbh[:, :].bitcast(F32), ALU.subtract))
            own.wait()
            for dst_, hi, lo in ((vb_r, vbh, vbl), (ob_r, obh, obl), (qb_r, qbh, qbl)):
                own.step(nc.vector.tensor_copy(dst_[0:1, :], hi[0:1, :].bitcast(F32)))
                own.step(nc.vector.tensor_copy(dst_[32:33, :], lo[32:33, :].bitcast(F32)))
            own.step(nc.vector.memset(hit_was[:, :], 0.0))
            own.step(nc.vector.memset(toep[:, :], 0.0))
            own.step(nc.vector.tensor_copy(base_f[:, :], tok_id[:, :]))
            M, R = G64 - 1, MAXREL
            edge = pe_row[:, R:R + 1]
            nc.vector.tensor_copy(ext[:, 0:M - R], edge.to_broadcast([G64, M - R])).then_inc(s_ext, 1)
            nc.vector.tensor_copy(ext[:, M:M + R + 1], pe_row[:, 0:R + 1]).then_inc(s_ext, 1)
            nc.vector.tensor_copy(ext[:, M + R + 1:2 * G64], edge.to_broadcast([G64, 2 * G64 - M - R - 1])).then_inc(s_ext, 1)
            nc.vector.tensor_copy(ext[:, M - R:M], pe_row[:, R:0:-1]).then_inc(s_ext, 1)
            dve.wait_ge(s_tl, 32)
            own.wait()
            own.step(nc.vector.tensor_tensor(bias_s[:, :], toep[:, :], off_block, ALU.add))
            dve.sem_inc(d_rec, 1)
            meet(dve, "dve", 1)

            def stats(own_, src, st, mv, tiles, done):
                for t in range(tiles):
                    ins = nc.vector.bn_stats(st[:, t, :], src(t))
                own_.step(ins)
                own_.wait()
                nc.vector.memset(gate_cell[:, :], 0.0)
                for t in range(tiles):
                    ins = nc.vector.bn_aggr(mv[:, t, :], st[:, t, :])
                ins.then_inc(done, 1)

            def inverse(own_, sd, rs, nm, mv, done):
                own_.step(nc.vector.reciprocal(rs[:, :], sd[:, :]))
                own_.wait()
                nc.vector.scalar_tensor_tensor(nm[:, :], mv[:, :, 0], -1.0, rs[:, :], ALU.mult, ALU.mult).then_inc(done, 1)

            def pass_a(b):
                def x_stats(g):
                    dve.wait_ge(ld_x, (g + 1) * 16)
                    stats(Own(dve, o_ln, g), lambda t: xa[:, t, :], st_a, mv_a, TB, d_stat)

                def x_scale(g, has_prev):
                    dve.wait_ge(a_sd, g + 1)
                    if has_prev:
                        dve.wait_ge(g_xn, g)
                    inverse(Own(dve, o_rs, g), sd_a, rs_a, nm_a, mv_a, d_rs)

                def x_low(g):
                    for k in range(KD):
                        dve.wait_ge(a_xh, g * KD + (k + 1))
                        nc.vector.tensor_tensor(xl[:, k, :], bank[k][:, :], xh[:, k, :].bitcast(F32),
                                                ALU.subtract).then_inc(d_xl, 1)

                def rotate(g, m):
                    a1, a2 = hd[:, :, :, 0:HALF], hd[:, :, :, HALF:QK]
                    c_, s_ = (w[:, bass.ds(m * TB, TB), :].unsqueeze(2).to_broadcast([P, TB, 4, HALF]) for w in (cos, sin))
                    dve.wait_ge(g_hd, g + 1)
                    nc.vector.tensor_tensor(prod[0][:, :, :, :], a1, c_, ALU.mult)
                    nc.vector.tensor_tensor(prod[1][:, :, :, :], a2, s_, ALU.mult)
                    nc.vector.tensor_tensor(prod[2][:, :, :, :], a2, c_, ALU.mult)
                    nc.vector.tensor_tensor(prod[3][:, :, :, :], a1, s_, ALU.mult).then_inc(d_prod, 1)
                    dve.wait_ge(d_prod, g + 1)
                    nc.vector.tensor_tensor(hr[:, :, :, 0:HALF], prod[0][:, :, :, :], prod[1][:, :, :, :], ALU.subtract)
                    nc.vector.tensor_tensor(hr[:, :, :, HALF:QK], prod[2][:, :, :, :], prod[3][:, :, :, :], ALU.add) \
                        .then_inc(d_head, 1)

                def kb_low(g):
                    dve.wait_ge(a_pbh, g + 1)
                    nc.vector.tensor_tensor(pbl[:, :, :], hr[:, :, 2:4, :].rearrange("p t h d -> p t (h d)"),
                                            pbh[:, :, :].bitcast(F32), ALU.subtract).then_inc(d_pbl, 1)

                def v_low(g, t):
                    dve.wait_ge(a_vh, g * TB + (t + 1))
                    nc.vector.tensor_tensor(vl[:, t, :], vt[t % 2][:, :], vh[:, t, :].bitcast(F32), ALU.subtract) \
                        .then_inc(d_vl, 1)

                def q_and_k(g):
                    dve.wait_ge(p_ta, g + 1)
                    nc.vector.tensor_copy(qqt[:, :], bank[3][0:QK, :])
                    dve.wait_ge(p_tb, g + 1)
                    nc.vector.tensor_copy(kkt[:, :], bank[4][0:QK, :]).then_inc(d_tab, 1)

                def scores(g):
                    dve.wait_ge(p_s, g + 1)
                    nc.vector.scalar_tensor_tensor(sc[:, :].rearrange("p (t n) -> p t n", t=TB),
                                                   bank[5][:, :].rearrange("p (t n) -> p t n", t=TB), 1.0 / G64,
                                                   bias_s[:, :].unsqueeze(1).to_broadcast([P, TB, P]),
                                                   ALU.mult, ALU.add).then_inc(o_at, 1)
                    dve.wait_ge(o_at, g + 1)
                    nc.vector.scalar_tensor_tensor(at[:, :], sc[:, :], 0.0, sc[:, :], ALU.max, ALU.mult).then_inc(d_at, 1)
                    dve.wait_ge(a_ath, g + 1)
                    nc.vector.tensor_tensor(atl[:, :], at[:, :], ath[:, :].bitcast(F32), ALU.subtract).then_inc(d_atl, 1)

                x_stats(b * NB)
                x_scale(b * NB, False)
                x_low(b * NB)

                def body(g, m, has_prev, has_next):
                    if has_next:
                        x_stats(g + 1)
                        x_scale(g + 1, True)
                    rotate(g, m)
                    v_low(g, 0)
                    v_low(g, 1)
                    kb_low(g)
                    v_low(g, 2)
                    v_low(g, 3)
                    q_and_k(g)
                    if has_next:
                        x_low(g + 1)
                    scores(g)

                blocks(dve, b, body)
                dve.wait_ge(a_kvh, b + 1)
                nc.vector.scalar_tensor_tensor(kvl[QK:2 * QK, :], bank[7][QK:2 * QK, :], 1.0 / S,
                                               kvh[QK:2 * QK, :].bitcast(F32), ALU.mult, ALU.subtract).then_inc(o_kv, 1)

            def pass_b(b):
                for z in (lqh, lql):
                    nc.vector.memset(z[0:QK, :].bitcast(F32), 0.0)

                def lows(g, m):
                    dve.wait_ge(a_bxh, g + 1)
                    nc.vector.tensor_tensor(xl[:, :, :], xtb[:, :, :], xh[:, :, :].bitcast(F32), ALU.subtract) \
                        .then_inc(d_bxl, 1)
                    dve.wait_ge(a_lqh, g + 1)
                    nc.vector.tensor_tensor(lql[QK:2 * QK, :], lq_all[QK:2 * QK, cols(m)],
                                            lqh[QK:2 * QK, :].bitcast(F32), ALU.subtract).then_inc(d_lql, 1)

                def gated(g, m, has_prev):
                    for c in range(KH):
                        dve.wait_ge(p_lo, g * KH + (c + 1))
                        nc.vector.tensor_tensor(mixed[c % 2][:, :], bank[2 + c % 2][:, :], qo_all[:, c, cols(m)], ALU.add) \
                            .then_inc(d_mix, 1)
                        dve.wait_ge(a_gs, g * KH + (c + 1))
                        dve.wait_ge(d_mix, g * KH + (c + 1))
                        if c == 0 and has_prev:
                            dve.wait_ge(p_wo, g * 2)
                        nc.vector.tensor_tensor(og[:, c, :], mixed[c % 2][:, :], gsb[c % 2][:, :], ALU.mult).then_inc(d_og, 1)

                def route(g):
                    own_ = Own(dve, o_rt, g * 16)

                    def wide(ap, n):
                        return ap.unsqueeze(2).to_broadcast([P, TB, n])

                    dve.wait_ge(p_lg, g + 1)
                    z = bank[6][:, 0:TB * E].rearrange("p (t e) -> p t e", t=TB)
                    own_.step(nc.vector.tensor_reduce(mx[:, :], z, AX, ALU.max))
                    own_.wait()
                    nc.vector.tensor_tensor(lg[:, :, :], z, wide(mx[:, :], E), ALU.subtract).then_inc(d_lg, 1)
                    dve.wait_ge(a_exp, g + 1)
                    own_.step(nc.vector.tensor_reduce(sm[:, :], pr[:, :, :], AX, ALU.add))
                    own_.wait()
                    own_.step(nc.vector.reciprocal(rsm[:, :], sm[:, :]))
                    own_.wait()
                    own_.step(nc.vector.tensor_tensor(pr[:, :, :], pr[:, :, :], wide(rsm[:, :], E), ALU.mult))
                    own_.wait()
                    own_.step(nc.vector.tensor_reduce(gs[:, :, :], pr[:, :, :].rearrange("p t (a c) -> p t a c", a=GRP), AX, ALU.max))
                    own_.wait()
                    nc.vector.memset(gate_cell[:, :], 0.0)
                    top4(own_, gs, top_g, ix_g, fx_g)
                    own_.step(nc.vector.tensor_tensor(
                        eq_g[:, :, :, :], iota_e[:, 0:GRP].unsqueeze(1).unsqueeze(1).to_broadcast([P, TB, TOPK, GRP]),
                        fx_g[:, :, 0:TOPK].unsqueeze(3).to_broadcast([P, TB, TOPK, GRP]), ALU.is_equal))
                    own_.wait()
                    own_.step(nc.vector.tensor_reduce(keep[:, :, :], eq_g[:, :, :, :].rearrange("p t k a -> p t a k"), AX, ALU.add))
                    own_.wait()
                    nc.vector.tensor_scalar(kneg[:, :, :], keep[:, :, :], -1.0, None, ALU.add)
                    m4 = msk[:, :, :].rearrange("p t (a c) -> p t a c", a=GRP)
                    own_.step(nc.vector.tensor_tensor(m4, pr[:, :, :].rearrange("p t (a c) -> p t a c", a=GRP),
                                                      keep[:, :, :].unsqueeze(3).to_broadcast([P, TB, GRP, EG]), ALU.mult))
                    own_.wait()
                    own_.step(nc.vector.tensor_tensor(m4, m4, kneg[:, :, :].unsqueeze(3).to_broadcast([P, TB, GRP, EG]), ALU.add))
                    own_.wait()
                    nc.vector.memset(gate_cell[:, :], 0.0)
                    top4(own_, msk, top_e, ix_e, fx_e)
                    own_.step(nc.vector.tensor_tensor(
                        oh[:, :, :, :], iota_e.unsqueeze(1).unsqueeze(1).to_broadcast([P, TB, TOPK, E]),
                        fx_e[:, :, 0:TOPK].unsqueeze(3).to_broadcast([P, TB, TOPK, E]), ALU.is_equal))
                    own_.wait()
                    nc.vector.tensor_reduce(wsum[:, :], top_e[:, :, 0:TOPK], AX, ALU.add)
                    with nc.allow_low_precision("0 and 1 are exact"):
                        nc.vector.tensor_reduce(hit[:, :, :], oh[:, :, :, :].rearrange("p t k e -> p t e k"), AX, ALU.add) \
                            .then_inc(d_hit, 1)
                    assert own_.n == 16, own_.n

                def top4(own_, src, val, ix, fx):
                    for t in range(TB):
                        ins = nc.vector.max(val[:, t, :], src[:, t, :])
                    own_.step(ins)
                    own_.wait()
                    nc.vector.memset(gate_cell[:, :], 0.0)
                    for t in range(TB):
                        ins = nc.vector.max_index(ix[:, t, :], val[:, t, :], src[:, t, :])
                    own_.step(ins)
                    own_.wait()
                    own_.step(nc.vector.tensor_copy(fx[:, :, :], ix[:, :, :]))
                    own_.wait()

                def slots(g):
                    own_ = Own(dve, o_fin, g * 7)
                    dve.wait_ge(p_cs, g + 1)
                    n4 = bank[7][:, 0:TB * E].rearrange("p (t e) -> p t e", t=TB)
                    nc.vector.tensor_reduce(hsum[:, :], hit[:, :, :].rearrange("p t e -> p e t"), AX, ALU.add)
                    nc.vector.tensor_scalar(wrec[:, :], wsum[:, :], 1e-9, None, ALU.add)
                    own_.step(nc.vector.tensor_tensor(ohp[:, :, :, :], oh[:, :, :, :],
                                                      n4.unsqueeze(2).to_broadcast([P, TB, TOPK, E]), ALU.mult))
                    own_.wait()
                    own_.step(nc.vector.tensor_reduce(pos[:, :, :], ohp[:, :, :, :], AX, ALU.add))
                    nc.vector.tensor_tensor(hit_all[:, :], hit_all[:, :], hsum[:, :], ALU.add)
                    own_.step(nc.vector.reciprocal(wrec[:, :], wrec[:, :]))
                    own_.wait()
                    own_.step(nc.vector.tensor_copy(hit_was[:, :], hit_all[:, :]))
                    nc.vector.tensor_scalar(over[:, :, :], pos[:, :, :], float(CAP), float(FAR), ALU.is_ge, ALU.mult)
                    own_.step(nc.vector.scalar_tensor_tensor(dst[:, :, :], fx_e[:, :, 0:TOPK], float(CAP), pos[:, :, :],
                                                             ALU.mult, ALU.add))
                    dve.wait_ge(g_rec, g + 1)
                    own_.wait()
                    own_.step(nc.vector.tensor_tensor(dsti[:, :].rearrange("p (t k) -> p t k", t=TB), dst[:, :, :],
                                                      over[:, :, :], ALU.add))
                    nc.vector.tensor_copy(rec[:, :, 0:2], base_f[:, :].rearrange("p (n r) -> p n r", r=2))
                    own_.step(nc.vector.tensor_tensor(
                        rec[:, :, 2:3].bitcast(F32).rearrange("p (t k) r -> p t (k r)", t=TB), top_e[:, :, 0:TOPK],
                        wrec[:, :].unsqueeze(2).to_broadcast([P, TB, TOPK]), ALU.mult))
                    own_.wait()
                    step_ = base_f[:, :].rearrange("p (n r) -> p n r", r=2)
                    nc.vector.tensor_scalar(step_[:, :, 0:1], step_[:, :, 0:1], float(BLK), None, ALU.add)
                    nc.vector.tensor_scalar(step_[:, :, 1:2], step_[:, :, 1:2], float(BLK * TOPK), None, ALU.add) \
                        .then_inc(d_rec, 1)
                    assert own_.n == 7, own_.n

                def chain(g, has_prev):
                    own_ = Own(dve, o_ch, g * 9)
                    dve.wait_ge(p_wo, g * 2 + 2)
                    stats(own_, lambda t: bank[4 + t // 2][:, (t % 2) * D:(t % 2 + 1) * D], st_b, mv_b, TB, d_ln)
                    dve.wait_ge(a_ln, g * 6 + 1)
                    inverse(own_, sd_b, rs_b, nm_b, mv_b, d_ln)
                    dve.wait_ge(a_ln, g * 6 + 2)
                    own_.step(nc.vector.tensor_tensor(yb[:, :, :], yb[:, :, :], w2b[:, :].unsqueeze(1).to_broadcast([P, TB, D]), ALU.mult))
                    own_.wait()
                    own_.step(nc.vector.tensor_tensor(yb[:, :, :], yb[:, :, :], b2b[:, :].unsqueeze(1).to_broadcast([P, TB, D]), ALU.add))
                    own_.wait()
                    stats(own_, lambda t: yb[:, t, :], st_b, mv_b, TB, d_ln)
                    dve.wait_ge(a_ln, g * 6 + 3)
                    inverse(own_, sd_b, rs_b, nm_b, mv_b, d_ln)
                    dve.wait_ge(a_ln, g * 6 + 4)
                    dve.wait_ge(ld_xb, g * 16 + 16)
                    if has_prev:
                        dve.wait_ge(st_x2, g * 16)
                    own_.step(nc.vector.tensor_tensor(x2b[:, :, :], yb[:, :, :], xb[:, :, :], ALU.add))
                    own_.wait()
                    stats(own_, lambda t: x2b[:, t, :], st_b, mv_b, TB, d_ln)
                    dve.wait_ge(a_ln, g * 6 + 5)
                    if has_prev:
                        dve.wait_ge(p_xt, g * KD)
                    inverse(own_, sd_b, rs_b, nm_b, mv_b, d_ln)
                    assert own_.n == 9, own_.n

                def body(g, m, has_prev, has_next):
                    gated(g, m, has_prev)
                    if has_next:
                        lows(g + 1, m + 1)
                    if has_prev:
                        route(g - 1)
                    chain(g, has_prev)
                    if has_prev:
                        slots(g - 1)

                lows(b * NB, 0)
                blocks(dve, b, body)
                route(b * NB + (NB - 1))
                slots(b * NB + (NB - 1))

            attention(dve, "dve", pass_a, pass_b)
            meet(dve, "dve", 6)

            def split_w(e, q):
                for j in range(3):
                    dve.wait_ge(a_wh, e * 3 + (j + 1))
                    ins = nc.vector.tensor_tensor(wl[q][:, j], wld[:, j], wh[q][:, j].bitcast(F32), ALU.subtract)
                ins.then_inc(d_wl, 1)

            def e_low(n, q):
                dve.wait_ge(a_eh, n + 1)
                nc.vector.tensor_tensor(el[q][:, :, :], bank[q][:, :].rearrange("p (k n) -> p k n", k=KD),
                                        eh[q][:, :, :].bitcast(F32), ALU.subtract).then_inc(d_el, 1)

            def product(n, q):
                dve.wait_ge(a_sa, n + 1)
                nc.vector.tensor_tensor(hf[q][:, :, :], bank[4 + q][:, :].rearrange("p (k n) -> p k n", k=KD),
                                        sa[q][:, :, :], ALU.mult).then_inc(d_hf, 1)

            def h_low(n, q):
                dve.wait_ge(a_hh, n + 1)
                nc.vector.tensor_tensor(hl[q][:, :, :], hf[q][:, :, :], hh[q][:, :, :].bitcast(F32), ALU.subtract) \
                    .then_inc(d_hl, 1)

            split_w(0, 0)
            e_low(0, 0)

            def records(c, i, first):
                q, buf, n = c // NCH, c % NXB, i * (2 * NCH) + c
                if c % NCH == 0:
                    dve.wait_ge(ld_six[q], (i + 1) * 16)
                if not (first and c < NXB):
                    dve.wait_ge(st_eo[buf], (i * 2 + c // NXB) * (16 * CH))
                s = (c % NCH) * CH
                nc.vector.tensor_copy(sx[buf][:, :, :], six[q][:, s:s + CH, :]).then_inc(d_sx, 1)

            def pair(i, first, last):
                for c in range(2 * NCH):
                    n = i * (2 * NCH) + c
                    if not (last and c == 2 * NCH - 1):
                        e_low(n + 1, (c + 1) % 2)
                    records(c, i, first)
                    product(n, c % 2)
                    h_low(n, c % 2)
                    if c % NCH == 2:
                        split_w(i * 2 + (c // NCH + 1), (c // NCH + 1) % 2)

            pair(0, True, False)
            with dve.Fori(1, E // 2 - 1) as i:
                pair(i, False, False)
            pair(E // 2 - 1, False, True)
            meet(dve, "dve", 7)

            NC, N0 = NT // (CH * P), E * NCH

            def total(n, q, first):
                dve.wait_ge(g_ys, n + 1)
                dve.wait_ge(p_dn, n + (N0 + 1))
                if not first:
                    dve.wait_ge(a_cn, n - (GC - 1))
                nc.vector.tensor_tensor(ytot[q][:, :, :], ysum[q % 2][:, :, 0, :],
                                        bank[6 + q % 2][:, :].rearrange("p (t d) -> p t d", t=CH), ALU.add).then_inc(d_acc, 1)
                dve.wait_ge(d_acc, n + 1)
                nc.vector.tensor_tensor(ytot[q][:, :, :], ytot[q][:, :, :], ysum[q % 2][:, :, 1, :], ALU.add).then_inc(d_tot, 1)
                dve.wait_ge(d_tot, n + 1)
                stats(Own(dve, o_c, n), lambda t: ytot[q][:, t, :], st_c, mv_c[:, q * CH:(q + 1) * CH, :], CH, d_cst)

            def c_inverse(i):
                dve.wait_ge(a_csd, i)
                inverse(Own(dve, o_cr, i - 1), sd_c, rs_c, nm_c, mv_c, d_crs)

            def final(i, q):
                dve.wait_ge(a_cn, i * GC + (q + 1 - GC))
                dve.wait_ge(ld_r[q], i * 16)
                nc.vector.tensor_tensor(yout[q][:, :, :], yout[q][:, :, :], xr[q][:, :, :], ALU.add).then_inc(d_out, 1)

            e_low(N0, 0)

            def group(i, first, last):
                for q in range(GC):
                    n = i * GC + q
                    if not (last and q == GC - 1):
                        e_low(n + (N0 + 1), 1 - q % 2)
                    product(n + N0, q % 2)
                    h_low(n + N0, q % 2)
                    if not first:
                        if q == 1:
                            c_inverse(i)
                        if q >= 2:
                            final(i, 2 * q - 4)
                            final(i, 2 * q - 3)
                    if not (first and q == 0):
                        total(n - 1, (q - 1) % GC, first or q == 0)

            group(0, True, False)
            with dve.Fori(1, NC // GC - 1) as i:
                group(i, False, False)
            group(NC // GC - 1, False, True)
            total(NC - 1, GC - 1, False)
            c_inverse(NC // GC)
            for q in range(GC):
                final(NC // GC, q)

        @block.tensor
        def _(pe):
            pe.wait_ge(s_dve, 13)
            pe.wait_ge(s_load, 16 * 20)
            for c in range(KH):
                for k in range(KD):
                    nc.tensor.matmul(bank[1][:, c:c + 1], wraw[:, 1, k, c * P:(c + 1) * P], l1b[:, k:k + 1],
                                     start=(k == 0), stop=(k == KD - 1))
            for k in range(KD):
                nc.tensor.matmul(bank[0][:, 0:QK], bmat[:, k, :], qraw[:, k, :], start=(k == 0), stop=(k == KD - 1))
            for k in range(KD):
                ins = nc.tensor.matmul(bank[2][:, :], bmat[:, k, :], wraw[:, 0, k, :], start=(k == 0), stop=(k == KD - 1))
            ins.then_inc(s_pe, 1)
            meet(pe, "pe", 1)

            def three(dst_, ah, al, bh, bl, start, stop, check=False):
                kw = {"skip_group_check": True} if check else {}
                nc.tensor.matmul(dst_, ah, bh, start=start, stop=False, **kw)
                nc.tensor.matmul(dst_, ah, bl, start=False, stop=False, **kw)
                return nc.tensor.matmul(dst_, al, bh, start=False, stop=stop, **kw)

            def pass_a(b):
                def turn_x(g, first):
                    pe.wait_ge(g_xn, g + 1)
                    for k in range(KD):
                        if not first:
                            pe.wait_ge(a_v, (g - 1) * TB + (k + 3))
                        for t in range(TB):
                            ins = nc.tensor.transpose(bank[k][:, t * P:(t + 1) * P], xn[:, t, k * P:(k + 1) * P], ident)
                        ins.then_inc(p_x, 1)

                def project(dst_, t, bias, w_h, w_l):
                    nc.tensor.matmul(dst_, ones_r[:, :], bias[:, :], start=True, stop=False)
                    for k in range(KD):
                        ins = three(dst_, xh[:, k, t * P:(t + 1) * P], xl[:, k, t * P:(t + 1) * P], w_h[:, k, :], w_l[:, k, :],
                                    False, k == KD - 1)
                    return ins

                def weigh(g):
                    pe.wait_ge(d_atl, g + 1)
                    for c in range(KH):
                        if c == 1:
                            pe.wait_ge(a_ta, g + 1)
                        if c == 3:
                            pe.wait_ge(a_qo, g * KH + 1)
                        for t in range(TB):
                            dst_ = bank[QO_BANK[c]][:, t * P:(t + 1) * P]
                            ins = three(dst_, vh[:, t, c * P:(c + 1) * P], vl[:, t, c * P:(c + 1) * P],
                                        ath[:, t * P:(t + 1) * P], atl[:, t * P:(t + 1) * P], True, True)
                        ins.then_inc(p_qo, 1)

                def add_kv(g, t):
                    pe.wait_ge(d_vl, g * TB + (t + 1))
                    three(bank[7][:, :], pbh[:, t, :], pbl[:, t, :], vh[:, t, :], vl[:, t, :], False, False, True) \
                        .then_inc(p_kv, 1)

                nc.tensor.matmul(bank[7][:, :], zero[:, 0:P], zero[:, 0:H], start=True, stop=True, skip_group_check=True)
                turn_x(b * NB, True)

                def body(g, m, has_prev, has_next):
                    pe.wait_ge(d_xl, g * KD + KD)
                    if has_prev:
                        pe.wait_ge(a_u, g)
                    for t in range(TB):
                        ins = project(bank[2][:, t * QK:(t + 1) * QK], t, qb_r, wqh, wql)
                    ins.then_inc(p_u, 1)
                    if has_prev:
                        weigh(g - 1)
                    for t in range(TB):
                        if t >= 2:
                            pe.wait_ge(a_v, g * TB + (t - 1))
                        project(bank[t % 2][:, :], t, vb_r, wvh, wvl).then_inc(p_v, 1)
                    pe.wait_ge(d_head, g + 1)
                    for h, (bk, done) in enumerate(((3, p_ta), (4, p_tb))):
                        if has_prev:
                            pe.wait_ge(a_qo, (g - 1) * KH + (h + 2))
                        for t in range(TB):
                            ins = nc.tensor.transpose(bank[bk][:, t * P:(t + 1) * P],
                                                      hr[:, t, 2 * h:2 * h + 2, :].rearrange("p h d -> p (h d)"), ident)
                        ins.then_inc(done, 1)
                    pe.wait_ge(d_pbl, g + 1)
                    add_kv(g, 0)
                    add_kv(g, 1)
                    pe.wait_ge(d_tab, g + 1)
                    for t in range(TB):
                        ins = nc.tensor.matmul(bank[5][:, t * P:(t + 1) * P], kkt[:, t * P:(t + 1) * P],
                                               qqt[:, t * P:(t + 1) * P], start=True, stop=True)
                    ins.then_inc(p_s, 1)
                    add_kv(g, 2)
                    add_kv(g, 3)
                    if has_next:
                        turn_x(g + 1, False)

                blocks(pe, b, body)
                weigh(b * NB + (NB - 1))

            def pass_b(b):
                def mix(g, c, has_prev):
                    if c == 0:
                        pe.wait_ge(d_bxl, g + 1)
                        pe.wait_ge(d_lql, g + 1)
                    if has_prev or c >= 2:
                        pe.wait_ge(a_gs, g * KH + (c - 1))
                    for k in range(KD):
                        ins = three(bank[c % 2][:, :], wgh[:, k, c * P:(c + 1) * P], wgl[:, k, c * P:(c + 1) * P],
                                    xh[:, k, :], xl[:, k, :], k == 0, k == KD - 1)
                    ins.then_inc(p_g, 1)
                    if has_prev or c >= 2:
                        pe.wait_ge(d_mix, g * KH + (c - 1))
                    three(bank[2 + c % 2][:, :], kvh[:, c * P:(c + 1) * P], kvl[:, c * P:(c + 1) * P], lqh[:, :], lql[:, :],
                          True, True).then_inc(p_lo, 1)

                def turn_xf(g, has_prev):
                    pe.wait_ge(a_ln, g * 6 + 6)
                    for k in range(KD):
                        for t in range(TB):
                            ins = nc.tensor.transpose(bank[6 + k][:, t * P:(t + 1) * P], xfb[:, t, k * P:(k + 1) * P], ident)
                        ins.then_inc(p_xt, 1)

                def logits(g):
                    pe.wait_ge(a_xft, g * KD + KD)
                    for t in range(TB):
                        for k in range(KD):
                            ins = nc.tensor.matmul(bank[6][:, t * E:(t + 1) * E], xft[:, k, t * P:(t + 1) * P], wr[:, k, :],
                                                   start=(k == 0), stop=(k == KD - 1))
                    ins.then_inc(p_lg, 1)

                def wo_(g, has_prev):
                    pe.wait_ge(d_og, g * KH + KH)
                    if has_prev:
                        pe.wait_ge(a_ln, (g - 1) * 6 + 2)
                    for t in range(TB):
                        dst_ = bank[4 + t // 2][:, (t % 2) * D:(t % 2 + 1) * D]
                        nc.tensor.matmul(dst_, ones_r[:, :], ob_r[:, :], start=True, stop=False)
                        for k in range(KH):
                            ins = nc.tensor.matmul(dst_, og[:, k, t * P:(t + 1) * P], wo[:, k, :], start=False,
                                                   stop=(k == KH - 1))
                        if t % 2:
                            ins.then_inc(p_wo, 1)

                def count(g):
                    pe.wait_ge(d_hit, g + 1)
                    for t in range(TB):
                        dst_ = bank[7][:, t * E:(t + 1) * E]
                        nc.tensor.matmul(dst_, ones_b[:, :], hit_was[:, :], start=True, stop=False)
                        for s in range(t):
                            nc.tensor.matmul(dst_, ones_b[:, :], hit[:, s, :], start=False, stop=False)
                        ins = nc.tensor.matmul(dst_, tri[:, :], hit[:, t, :], start=False, stop=True)
                    ins.then_inc(p_cs, 1)

                def body(g, m, has_prev, has_next):
                    for c in range(KH - 1):
                        mix(g, c, has_prev)
                    if has_prev:
                        pe.wait_ge(d_rec, g)
                        turn_xf(g - 1, True)
                    mix(g, KH - 1, has_prev)
                    if has_prev:
                        logits(g - 1)
                    wo_(g, has_prev)
                    if has_prev:
                        count(g - 1)

                blocks(pe, b, body)
                g = b * NB + (NB - 1)
                pe.wait_ge(d_rec, g + 1)
                turn_xf(g, True)
                logits(g)
                count(g)

            attention(pe, "pe", pass_a, pass_b)
            meet(pe, "pe", 6)

            def turn_e(n, q, src, arrived):
                arrived()
                for k in range(KD):
                    for t in range(CH):
                        ins = nc.tensor.transpose(bank[q][:, (k * CH + t) * P:(k * CH + t + 1) * P],
                                                  src[:, t, k * P:(k + 1) * P], ident)
                ins.then_inc(p_et, 1)

            def up(n, q, wq, e, first):
                pe.wait_ge(d_el, n + 1)
                if not first:
                    pe.wait_ge(d_hf, n - 1)
                for j in range(2):
                    for c in range(KD):
                        for k in range(KD):
                            ins = three(bank[2 + 2 * j + q][:, c * CH * P:(c + 1) * CH * P],
                                        wh[wq][:, j, k, c * P:(c + 1) * P], wl[wq][:, j, k, c * P:(c + 1) * P],
                                        eh[q][:, k, :], el[q][:, k, :], k == 0, k == KD - 1)
                ins.then_inc(p_up, 1)

            def down(n, q, wq, free):
                pe.wait_ge(d_hl, n + 1)
                free()
                for t in range(CH):
                    for k in range(KD):
                        ins = three(bank[6 + q][:, t * D:(t + 1) * D], hh[q][:, k, t * P:(t + 1) * P],
                                    hl[q][:, k, t * P:(t + 1) * P], wh[wq][:, 2, k, :], wl[wq][:, 2, k, :],
                                    k == 0, k == KD - 1)
                ins.then_inc(p_dn, 1)

            def turn_g(c, i, first):
                i, c = (i + 1, c - 2 * NCH) if c >= 2 * NCH else (i, c)
                n = i * (2 * NCH) + c

                def arrived():
                    pe.wait_ge(ld_xg[c % NXB], (i * 2 + (c // NXB + 1)) * (16 * CH))
                    if not first:
                        pe.wait_ge(d_el, n - 1)

                turn_e(n, c % 2, xg[c % NXB], arrived)

            turn_g(0, 0, True)

            def pair(i, first, last):
                for c in range(2 * NCH):
                    n = i * (2 * NCH) + c
                    if not (last and c == 2 * NCH - 1):
                        turn_g(c + 1, i, first and c + 1 < 2)
                    if c % NCH == 0:
                        pe.wait_ge(d_wl, i * 2 + (c // NCH + 1))
                    up(n, c % 2, c // NCH, None, first and c < 2)
                    if c > 0:
                        m = c - 1
                        down(n - 1, m % 2, m // NCH, lambda: None if first and m < 2 else pe.wait_ge(a_eo, n - 2))
                m = 2 * NCH - 1
                n = i * (2 * NCH) + m
                down(n, m % 2, m // NCH, lambda: pe.wait_ge(a_eo, n - 1))

            pair(0, True, False)
            with pe.Fori(1, E // 2 - 1) as i:
                pair(i, False, False)
            pair(E // 2 - 1, False, True)
            meet(pe, "pe", 7)

            NC, N0 = NT // (CH * P), E * NCH

            def turn_c(n, q, i):
                def arrived():
                    pe.wait_ge(ld_c[q], i * 16 + 16)
                    pe.wait_ge(d_el, n + (N0 - 1))

                turn_e(n + N0, q % 2, xg[q], arrived)

            turn_c(0, 0, 0)
            pe.wait_ge(d_wl, E + 1)

            def group(i, first, last):
                for q in range(GC):
                    n = i * GC + q
                    if not (last and q == GC - 1):
                        turn_c(n + 1, (q + 1) % GC, i + (q + 1) // GC)
                    up(n + N0, q % 2, 0, None, False)
                    if not (first and q == 0):
                        down(n + (N0 - 1), 1 - q % 2, 0, lambda: None if first and q < 3 else pe.wait_ge(d_acc, n - 2))

            group(0, True, False)
            with pe.Fori(1, NC // GC - 1) as i:
                group(i, False, False)
            group(NC // GC - 1, False, True)
            down(N0 + NC - 1, 1, 0, lambda: pe.wait_ge(d_acc, NC - 2))


_OUT = (2, 4096, 256)


def kernel(L0_attn_x, L0_attn_ln1_w, L0_attn_ln1_b, L0_attn_Wqk, L0_attn_bqk, L0_attn_Wv, L0_attn_bv, L0_attn_Wg,
           L0_attn_bg, L0_attn_Wo, L0_attn_bo, L0_attn_ln2_w, L0_attn_ln2_b, L0_attn_gamma, L0_attn_beta,
           L0_attn_pos_emb, L0_ffn_wg, L0_ffn_w1, L0_ffn_w2, L0_ffn_w3, L0_ffn_sw1, L0_ffn_sw2, L0_ffn_sw3):
    import numpy as np
    import concourse.bacc as bacc
    from concourse import mybir
    from concourse.bass_utils import run_bass_kernel_spmd

    def rows(a):
        return np.ascontiguousarray(a)

    def columns(a):
        return rows(np.asarray(a).reshape(-1, 128).T)

    n, half = 4096, 32
    inv_freq = np.power(np.float32(10000.0), -(np.arange(half, dtype=np.float32) / np.float32(half)))
    angle = np.arange(n, dtype=np.float32)[:, None] * inv_freq[None, :]
    rope = np.stack([np.cos(angle), np.sin(angle)]).reshape(2, n // 128, 128, half).transpose(0, 2, 1, 3)
    p = np.arange(128)
    ident = np.eye(128, dtype=np.float32)
    before = (p[:, None] < p[None, :]).astype(np.float32)
    off_block = np.where(p[:, None] // 64 == p[None, :] // 64, 0.0, -1e30).astype(np.float32)
    experts = np.broadcast_to(np.arange(32, dtype=np.float32), (128, 32))
    tok = np.arange(4)[None, :, None] * 128 + p[:, None, None] + np.zeros((1, 1, 4), np.int64)
    token_ids = np.stack([tok, tok * 4 + np.arange(4)], -1).reshape(128, 32).astype(np.int32)

    arrays = {
        "x": rows(np.asarray(L0_attn_x).reshape(8192, 256)),
        "wqk_t": rows(np.asarray(L0_attn_Wqk).T), "wv_t": rows(np.asarray(L0_attn_Wv).T),
        "wg_t": rows(np.asarray(L0_attn_Wg).T), "wo_t": rows(np.asarray(L0_attn_Wo).T),
        "ln1_w": columns(L0_attn_ln1_w), "ln1_b": columns(L0_attn_ln1_b),
        "bqk": rows(L0_attn_bqk), "bg": columns(L0_attn_bg),
        "bv": rows(L0_attn_bv), "bo": rows(L0_attn_bo),
        "ln2_w": rows(L0_attn_ln2_w), "ln2_b": rows(L0_attn_ln2_b),
        "gamma": rows(np.asarray(L0_attn_gamma).reshape(-1)), "beta": rows(np.asarray(L0_attn_beta).reshape(-1)), "pos_emb": rows(L0_attn_pos_emb),
        "rope": rows(rope), "consts": rows(np.concatenate([ident, before, off_block, experts], 1)),
        "token_ids": token_ids, "route_t": rows(np.asarray(L0_ffn_wg).T),
        "w1": rows(L0_ffn_w1), "w2": rows(L0_ffn_w2), "w3": rows(L0_ffn_w3),
        "sw1": rows(L0_ffn_sw1), "sw2": rows(L0_ffn_sw2), "sw3": rows(L0_ffn_sw3),
    }
    nc = bacc.Bacc("TRN2", target_bir_lowering=False, num_devices=1)
    args = {k: nc.dram_tensor("in_" + k, a.shape, mybir.dt.from_np(a.dtype), kind="ExternalInput").ap()
            for k, a in arrays.items()}
    args["out"] = nc.dram_tensor("out", (8192, 256), mybir.dt.float32, kind="ExternalOutput").ap()
    build_program(nc, **args)
    r = run_bass_kernel_spmd(nc, [{"in_" + k: a for k, a in arrays.items()}], core_ids=[0])
    return r.results[0]["out"].reshape(_OUT)
```

```python
import concourse.bass as bass
from concourse import mybir
from contextlib import ExitStack

P = 128
EPS = 1e-5


def build_program(nc, x, wqk_t, wv_t, wg_t, wo_t, ln1_w, ln1_b, bqk, bg, bv, bo, ln2_w, ln2_b,
                  gamma, beta, pos_emb, rope, consts, token_ids, route_t, w1, w2, w3, sw1, sw2, sw3, out):
    F32, F32R, I32, U32, BF16 = (mybir.dt.float32, mybir.dt.float32r, mybir.dt.int32,
                                 mybir.dt.uint32, mybir.dt.bfloat16)
    ALU, ACT = mybir.AluOpType, mybir.ActivationFunctionType
    AX = mybir.AxisListType.X

    NT, D = x.shape
    NBATCH = 2
    S = NT // NBATCH
    H = wv_t.shape[1]
    QK = wqk_t.shape[1]
    HALF = QK // 2
    BLK = 512
    TB = BLK // P
    NB = S // BLK
    KD, KH = D // P, H // P
    E = w1.shape[0]
    TOPK = 4
    GRP, EG = 8, E // 8
    CAP = max(1, int(1.25 * NT * TOPK / E))
    ST = CAP // P
    CH = 2
    NCH = ST // CH
    NSLOT = E * CAP
    NROW = NT * TOPK
    REC = 3
    FAR = 1 << 20
    G64 = 64
    ZW = 512
    NPOS = pos_emb.shape[0]
    MAXREL = (NPOS - 1) // 2
    NBLK = NBATCH * NB

    def dram(name, shape, dt):
        return nc.dram_tensor(name, shape, dt).ap()

    xh_d, xl_d = dram("xh_d", [NBLK, P, KD * BLK], F32R), dram("xl_d", [NBLK, P, KD * BLK], F32R)
    x2_d = dram("x2_d", [NT, D], F32)
    xf_d = dram("xf_d", [NT + P, D], F32)
    slot_d = dram("slot_d", [NSLOT, REC], I32)
    y4_d = dram("y4_d", [NROW, D], F32)
    toep_d = dram("toep_d", [G64 * 2 * G64], F32)

    ctx = ExitStack()
    with ctx:
        def sb(name, shape, dt, c=ctx):
            return c.enter_context(nc.sbuf_tensor(name, shape, dt))

        def sem(name):
            return ctx.enter_context(nc.semaphore(name))

        cst = sb("cst", [P, consts.shape[1]], F32)
        ident = cst[:, 0:P]
        off_block = cst[:, 2 * P:3 * P]
        iota_e = cst[:, 3 * P:3 * P + E]
        eps = sb("eps", [P, 2], F32)
        gate_cell = sb("gate_cell", [P, 1], F32)

        cA = ExitStack()
        tri = sb("tri", [P, P], BF16, cA)
        ones_b = sb("ones_b", [P, P], BF16, cA)
        tok_id = sb("tok_id", [P, TB * TOPK * 2], I32, cA)
        zero = sb("zero", [P, ZW], F32, cA)
        kvh, kvl = sb("kvh", [P, H], F32R, cA), sb("kvl", [P, H], F32R, cA)
        bias_s = sb("bias_s", [P, P], F32, cA)
        wq = sb("wq", [P, KD, QK], F32, cA)
        wvh, wvl, wgh, wgl = (sb(n, [P, KD, H], F32R, cA) for n in ("wvh", "wvl", "wgh", "wgl"))
        wo = sb("wo", [P, KH, D], F32, cA)
        wr = sb("wr", [P, KD, E], F32, cA)
        ones_r = sb("ones_r", [P, P], F32R, cA)
        qb_f = sb("qb_f", [P, QK], F32, cA)
        vb_r = sb("vb_r", [P, H], F32R, cA)
        ob_r = sb("ob_r", [P, D], F32R, cA)
        ones_f = ones_r[:, :].bitcast(F32)
        gb = sb("gb", [P, KH], F32, cA)
        gam, bet = sb("gam", [P, 4 * QK], F32, cA), sb("bet", [P, 4 * QK], F32, cA)
        cos, sin = sb("cos", [P, S // P, HALF], F32, cA), sb("sin", [P, S // P, HALF], F32, cA)
        qo_all = sb("qo_all", [P, KH, S], F32, cA)
        lqh, lql = sb("lqh", [P, S], F32R, cA), sb("lql", [P, S], F32R, cA)
        xh, xl = sb("xh", [P, KD, BLK], F32R, cA), sb("xl", [P, KD, BLK], F32R, cA)
        hit_all, hit_was = sb("hit_all", [P, E], F32, cA), sb("hit_was", [P, E], BF16, cA)
        base_f = sb("base_f", [P, TB * TOPK * 2], F32, cA)

        c0 = ExitStack()
        wraw = sb("wraw", [P, 2, KD, H], F32, c0)
        wscl = sb("wscl", [P, KD, H], F32, c0)
        qraw = sb("qraw", [P, KD, QK], F32, c0)
        l1w, l1b = sb("l1w", [P, KD], F32, c0), sb("l1b", [P, KD], F32, c0)
        bmat = sb("bmat", [P, KD, P], F32, c0)
        vb, vbh, vbl = sb("vb", [P, H], F32, c0), sb("vbh", [P, H], F32R, c0), sb("vbl", [P, H], F32R, c0)
        ob, obh, obl = sb("ob", [P, D], F32, c0), sb("obh", [P, D], F32R, c0), sb("obl", [P, D], F32R, c0)
        qb = sb("qb", [P, QK], F32, c0)
        gbi = sb("gbi", [P, KH], F32, c0)
        pe_row = sb("pe_row", [G64, NPOS], F32, c0)
        ext = sb("ext", [G64, 2 * G64], F32, c0)
        toep = sb("toep", [P, P], F32, c0)
        free_rec = sb("free_rec", [P, NSLOT * REC // P], I32, c0)
        c0.close()

        c1 = ExitStack()
        xa = sb("xa", [P, TB, D], F32, c1)
        xn = sb("xn", [P, TB, D], F32, c1)
        xta = sb("xta", [P, KD, BLK], F32, c1)
        u = sb("u", [P, TB, QK], F32, c1)
        hd = sb("hd", [P, TB, 4, QK], F32, c1)
        prod = [sb(f"prod{i}", [P, TB, 4, HALF], F32, c1) for i in range(2)]
        hr = sb("hr", [P, TB, 4, QK], F32, c1)
        pbh, pbl = sb("pbh", [P, TB, 2 * QK], F32R, c1), sb("pbl", [P, TB, 2 * QK], F32R, c1)
        qqt, kkt = sb("qqt", [QK, BLK], F32, c1), sb("kkt", [QK, BLK], F32, c1)
        vt = sb("vt", [P, TB, H], F32, c1)
        vh, vl = sb("vh", [P, TB, H], F32R, c1), sb("vl", [P, TB, H], F32R, c1)
        at = sb("at", [P, BLK], F32, c1)
        st_a = sb("st_a", [P, TB, 6], F32, c1)
        mv_a = sb("mv_a", [P, TB, 2], F32, c1)
        sd_a, rs_a, nm_a = (sb(n, [P, TB], F32, c1) for n in ("sd_a", "rs_a", "nm_a"))
        c1.close()

        c2 = ExitStack()
        w2b, b2b = sb("w2b", [P, D], F32, c2), sb("b2b", [P, D], F32, c2)
        xb = sb("xb", [P, TB, D], F32, c2)
        gsb = [sb(f"gsb{i}", [P, BLK], F32, c2) for i in range(2)]
        mixed = [sb(f"mixed{i}", [P, BLK], F32, c2) for i in range(2)]
        og = sb("og", [P, KH, BLK], F32, c2)
        yo = sb("yo", [P, TB, D], F32, c2)
        yb = sb("yb", [P, TB, D], F32, c2)
        x2b = sb("x2b", [P, TB, D], F32, c2)
        xfb = sb("xfb", [P, TB, D], F32, c2)
        xft = sb("xft", [P, KD, BLK], F32, c2)
        st_1, st_2, st_3 = (sb(n, [P, TB, 6], F32, c2) for n in ("st_1", "st_2", "st_3"))
        mv_b, mv_m = sb("mv_b", [P, 2 * TB, 2], F32, c2), sb("mv_m", [P, TB, 2], F32, c2)
        sd_b, rs_b, nm_b = (sb(n, [P, 2 * TB], F32, c2) for n in ("sd_b", "rs_b", "nm_b"))
        sd_m, rs_m, nm_m = (sb(n, [P, TB], F32, c2) for n in ("sd_m", "rs_m", "nm_m"))
        lg = sb("lg", [P, TB, E], F32, c2)
        pr = sb("pr", [P, TB, E], F32, c2)
        mx, sm, rsm = (sb(n, [P, TB], F32, c2) for n in ("mx", "sm", "rsm"))
        gs = sb("gs", [P, TB, GRP], F32, c2)
        top_g, top_e = sb("top_g", [P, TB, 8], F32, c2), sb("top_e", [P, TB, 8], F32, c2)
        ix_g, ix_e = sb("ix_g", [P, TB, 8], U32, c2), sb("ix_e", [P, TB, 8], U32, c2)
        fx_g, fx_e = sb("fx_g", [P, TB, 8], F32, c2), sb("fx_e", [P, TB, 8], F32, c2)
        eq_g = sb("eq_g", [P, TB, TOPK, GRP], F32, c2)
        keep, kneg = sb("keep", [P, TB, GRP], F32, c2), sb("kneg", [P, TB, GRP], F32, c2)
        msk = sb("msk", [P, TB, E], F32, c2)
        oh = sb("oh", [P, TB, TOPK, E], F32, c2)
        ohp = sb("ohp", [P, TB, TOPK, E], F32, c2)
        hit = sb("hit", [P, TB, E], BF16, c2)
        hsum = sb("hsum", [P, E], F32, c2)
        wsum, wrec = sb("wsum", [P, TB], F32, c2), sb("wrec", [P, TB], F32, c2)
        pos, dst, over = (sb(n, [P, TB, TOPK], F32, c2) for n in ("pos", "dst", "over"))
        dsti = sb("dsti", [P, TB * TOPK], I32, c2)
        rec = sb("rec", [P, TB * TOPK, REC], I32, c2)
        c2.close()
        cA.close()

        c3 = ExitStack()
        NXB = 5
        wld = sb("wld", [P, 3, KD, D], F32, c3)
        wh = [sb(f"wh{i}", [P, 3, KD, D], F32R, c3) for i in range(2)]
        wl = [sb(f"wl{i}", [P, 3, KD, D], F32R, c3) for i in range(2)]
        gix = [sb(f"gix{i}", [P, ST, REC], I32, c3) for i in range(2)]
        six = [sb(f"six{i}", [P, ST, REC], I32, c3) for i in range(2)]
        xg = [sb(f"xg{i}", [P, CH, D], F32, c3) for i in range(NXB)]
        eh = [sb(f"eh{i}", [P, KD, CH * P], F32R, c3) for i in range(2)]
        el = [sb(f"el{i}", [P, KD, CH * P], F32R, c3) for i in range(2)]
        sa = [sb(f"sa{i}", [P, KD, CH * P], F32, c3) for i in range(2)]
        hf = [sb(f"hf{i}", [P, KD, CH * P], F32, c3) for i in range(2)]
        hh = [sb(f"hh{i}", [P, KD, CH * P], F32R, c3) for i in range(2)]
        hl = [sb(f"hl{i}", [P, KD, CH * P], F32R, c3) for i in range(2)]
        sx = [sb(f"sx{i}", [P, CH, REC], I32, c3) for i in range(NXB)]
        eo = [sb(f"eo{i}", [P, CH, D], F32, c3) for i in range(NXB)]
        GC = 4
        y4 = [sb(f"y4{i}", [P, CH, TOPK, D], F32, c3) for i in range(GC)]
        xr = [sb(f"xr{i}", [P, CH, D], F32, c3) for i in range(GC)]
        ysum = [sb(f"ysum{i}", [P, CH, 2, D], F32, c3) for i in range(2)]
        ytot = [sb(f"ytot{i}", [P, CH, D], F32, c3) for i in range(GC)]
        yout = [sb(f"yout{i}", [P, CH, D], F32, c3) for i in range(GC)]
        st_c = sb("st_c", [P, CH, 6], F32, c3)
        mv_c = sb("mv_c", [P, GC * CH, 2], F32, c3)
        sd_c, rs_c, nm_c = (sb(n, [P, GC * CH], F32, c3) for n in ("sd_c", "rs_c", "nm_c"))
        c3.close()

        bank = [ctx.enter_context(nc.psum_tensor(f"bank{i}", [P, 512], F32)) for i in range(8)]

        s_load, s_pos, s_ext, s_toep, s_tl, s_clear = (sem(n) for n in ("s_load", "s_pos", "s_ext", "s_toep", "s_tl", "s_clear"))
        s_dve, s_act, s_pe, s_zero = sem("s_dve"), sem("s_act"), sem("s_pe"), sem("s_zero")
        ph = {n: sem(f"ph_{n}") for n in ("sp", "act", "dve", "pe", "pool")}
        past = {nc.sync: sem("past_sp"), nc.gpsimd: sem("past_pool")}
        ld_x, st_xh, st_xl, ld_xh = sem("ld_x"), sem("st_xh"), sem("st_xl"), sem("ld_xh")
        a_sd, a_xt, a_xh, a_u, a_ta, a_v, a_vh, a_pbh, a_qo, a_kvh = (sem(n) for n in (
            "a_sd", "a_xt", "a_xh", "a_u", "a_ta", "a_v", "a_vh", "a_pbh", "a_qo", "a_kvh"))
        d_stat, d_rs, d_xl, d_prod, d_head, d_pbl, d_vl, d_tab, d_at = (sem(n) for n in (
            "d_stat", "d_rs", "d_xl", "d_prod", "d_head", "d_pbl", "d_vl", "d_tab", "d_at"))
        g_xn, g_gam, g_hd, g_rec = sem("g_xn"), sem("g_gam"), sem("g_hd"), sem("g_rec")
        o_ln, o_rs, o_at, o_kv = sem("o_ln"), sem("o_rs"), sem("o_at"), sem("o_kv")
        p_x, p_u, p_v, p_ta, p_tb, p_kv, p_s, p_qo = (sem(n) for n in (
            "p_x", "p_u", "p_v", "p_ta", "p_tb", "p_kv", "p_s", "p_qo"))
        ld_w2, ld_xb, st_x2, st_xf, st_rec = sem("ld_w2"), sem("ld_xb"), sem("st_x2"), sem("st_xf"), sem("st_rec")
        a_gs, a_root, a_rootm, a_n1, a_n2, a_n3, a_yo, a_xft, a_exp = (sem(n) for n in (
            "a_gs", "a_root", "a_rootm", "a_n1", "a_n2", "a_n3", "a_yo", "a_xft", "a_exp"))
        d_lql, d_mix, d_og, d_st1, d_st2, d_st3, d_inv, d_invm, d_x2, d_lg, d_hit, d_rec = (sem(n) for n in (
            "d_lql", "d_mix", "d_og", "d_st1", "d_st2", "d_st3", "d_inv", "d_invm", "d_x2", "d_lg", "d_hit", "d_rec"))
        o_s1, o_s2, o_s3, o_inv, o_invm, o_wb, o_rt, o_fin = (sem(n) for n in (
            "o_s1", "o_s2", "o_s3", "o_inv", "o_invm", "o_wb", "o_rt", "o_fin"))
        p_g, p_lo, p_wo, p_xt, p_lg, p_cs = (sem(n) for n in ("p_g", "p_lo", "p_wo", "p_xt", "p_lg", "p_cs"))
        ld_w, ld_gix, ld_six = sem("ld_w"), [sem("ld_gix0"), sem("ld_gix1")], [sem("ld_six0"), sem("ld_six1")]
        ld_xg = [sem(f"ld_xg{i}") for i in range(NXB)]
        st_eo = [sem(f"st_eo{i}") for i in range(NXB)]
        a_wh, a_eh, a_sa, a_hh, a_eo = (sem(n) for n in ("a_wh", "a_eh", "a_sa", "a_hh", "a_eo"))
        d_wl, d_el, d_hf, d_hl, d_sx = (sem(n) for n in ("d_wl", "d_el", "d_hf", "d_hl", "d_sx"))
        p_et, p_up, p_dn = sem("p_et"), sem("p_up"), sem("p_dn")
        ld_c, ld_y, ld_r, st_out = ([sem(f"{n}{i}") for i in range(GC)] for n in ("ld_c", "ld_y", "ld_r", "st_out"))
        g_ys, d_acc, d_tot, d_cst, d_crs, d_out = (sem(n) for n in ("g_ys", "d_acc", "d_tot", "d_cst", "d_crs", "d_out"))
        a_csd, a_cn, o_c, o_cr = sem("a_csd"), sem("a_cn"), sem("o_c"), sem("o_cr")

        block = ctx.enter_context(nc.Block())

        class Own:

            def __init__(self, eng, s, base):
                self.eng, self.s, self.base, self.n = eng, s, base, 0

            def step(self, ins):
                self.n += 1
                ins.then_inc(self.s, 1)

            def wait(self):
                self.eng.wait_ge(self.s, self.base + self.n)

        def settled(eng):
            eng.sem_inc(past[eng], 1)

        def meet(eng, name, n):
            eng.drain().then_inc(ph[name], 1)
            for other in ph:
                if other != name:
                    eng.wait_ge(ph[other], n)
            if eng in past:
                settled(eng)

        def attention(eng, name, pass_a, pass_b):
            with eng.Fori(0, NBATCH) as b:
                pass_a(b)
                meet(eng, name, b * 2 + 2)
                pass_b(b)
                meet(eng, name, b * 2 + 3)

        LAG = 3

        def blocks_b(eng, b, body):
            def on(m):
                return [0 <= m - s < NB for s in range(LAG + 1)]

            for m in range(LAG):
                body(b * NB + m, m, on(m))
            with eng.Fori(LAG, NB) as m:
                body(b * NB + m, m, on(LAG))
            for m in range(NB, NB + LAG):
                body(b * NB + m, m, on(m))

        def blocks_a(eng, b, body):
            body(b * NB, 0, False, 2)
            with eng.Fori(1, NB - 2) as m:
                body(b * NB + m, m, True, 2)
            for m in (NB - 2, NB - 1):
                body(b * NB + m, m, True, NB - 1 - m)

        def cols(m):
            return bass.ds(m * BLK, BLK)

        QO_BANK = (6, 3, 4, 2)

        @block.sync
        def _(sp):
            for dst_, src in (
                (cst[:, :], consts), (tok_id[:, :], token_ids),
                (cos[:, :, :], rope[0]), (sin[:, :, :], rope[1]),
                (qraw[:, :, :], wqk_t.rearrange("(k p) n -> p k n", p=P)),
                (wraw[:, 0], wv_t.rearrange("(k p) n -> p k n", p=P)),
                (wraw[:, 1], wg_t.rearrange("(k p) n -> p k n", p=P)),
                (wo[:, :, :], wo_t.rearrange("(k p) n -> p k n", p=P)),
                (wr[:, :, :], route_t.rearrange("(k p) n -> p k n", p=P)),
                (l1w[:, :], ln1_w), (l1b[:, :], ln1_b), (gbi[:, :], bg),
                (gam[:, :], gamma.partition_broadcast(P)), (bet[:, :], beta.partition_broadcast(P)),
                (vb[:, :], bv.partition_broadcast(P)), (ob[:, :], bo.partition_broadcast(P)),
                (qb[:, :], bqk.partition_broadcast(P)),
                (pe_row[:, :], pos_emb.partition_broadcast(G64)),
            ):
                sp.dma_start(dst_, src).then_inc(s_load, 16)
            sp.wait_ge(s_ext, 4)
            W = 2 * G64 - 1
            sp.dma_start(toep_d[0:G64 * W].rearrange("(a c) -> a c", c=W), ext[:, 0:W]).then_inc(s_toep, 16)
            sp.wait_ge(s_toep, 16)
            src = toep_d[G64 - 1:G64 - 1 + G64 * (W - 1)].rearrange("(a c) -> a c", c=W - 1)[:, 0:G64]
            for q in range(2):
                sp.dma_start(toep[q * G64:(q + 1) * G64, q * G64:(q + 1) * G64], src).then_inc(s_tl, 16)
            sp.wait_ge(s_zero, 4)
            sp.dma_start(slot_d.rearrange("(p s) r -> p (s r)", p=P), free_rec[:, :]).then_inc(s_clear, 16)
            sp.dma_start(xf_d[NT:NT + P, :], zero[:, 0:D]).then_inc(s_clear, 16)
            sp.wait_ge(s_clear, 32)
            for s in st_out:
                sp.sem_inc(s, 16)
            meet(sp, "sp", 1)

            y4_rows = y4_d.rearrange("(n p r) d -> n p (r d)", p=P, r=ZW // D)   
            clears = y4_rows.shape[0] // NBLK

            def load_x(dst_, g, done):
                sp.dma_start(dst_[:, :, :], x[bass.ds(g * BLK, BLK), :].rearrange("(t p) d -> p t d", p=P)) \
                  .then_inc(done, 16)

            def pass_a(b):
                def next_x(g):
                    sp.wait_ge(g_xn, g)
                    load_x(xa, g, ld_x)

                def store_parts(g):
                    sp.wait_ge(a_xh, g * KD + KD)
                    sp.dma_start(xh_d[g, :, :].bitcast(F32), xh[:, :, :].bitcast(F32)).then_inc(st_xh, 16)
                    sp.wait_ge(d_xl, g * KD + KD)
                    sp.dma_start(xl_d[g, :, :].bitcast(F32), xl[:, :, :].bitcast(F32)).then_inc(st_xl, 16)

                load_x(xa, b * NB, ld_x)
                next_x(b * NB + 1)
                store_parts(b * NB)

                def body(g, m, has_prev, ahead):
                    if ahead >= 2:
                        next_x(g + 2)
                    if ahead >= 1:
                        store_parts(g + 1)
                    for n in range(clears):
                        sp.dma_start(y4_rows[g * clears + n, :, :], zero[:, :]).then_inc(s_clear, 16)

                blocks_a(sp, b, body)
                for s in (st_xh, st_xl):
                    sp.wait_ge(s, (b + 1) * (16 * NB))
                settled(sp)

            def pass_b(b):
                def rows_of(t, g):
                    return t[bass.ds(g * BLK, BLK), :].rearrange("(t p) d -> p t d", p=P)

                load_x(xb, b * NB, ld_xb)
                sp.dma_start(w2b[:, :], ln2_w.partition_broadcast(P)).then_inc(ld_w2, 16)
                sp.dma_start(b2b[:, :], ln2_b.partition_broadcast(P)).then_inc(ld_w2, 16)

                def body(g, m, on):
                    if on[2]:
                        sp.wait_ge(a_n3, g - 1)
                        sp.dma_start(rows_of(xf_d, g - 2), xfb[:, :, :]).then_inc(st_xf, 16)
                    if on[1]:
                        sp.wait_ge(d_x2, g)
                        sp.dma_start(rows_of(x2_d, g - 1), x2b[:, :, :]).then_inc(st_x2, 16)
                        if on[0]:
                            load_x(xb, g, ld_xb)

                blocks_b(sp, b, body)
                for s in (st_x2, st_xf):
                    sp.wait_ge(s, (b + 1) * (16 * NB))
                settled(sp)

            attention(sp, "sp", pass_a, pass_b)
            sp.wait_ge(s_clear, 32 + 16 * clears * NBLK)
            meet(sp, "sp", 6)

            slots = slot_d.rearrange("(e p s) r -> e p (s r)", p=P, s=ST)

            def load_w(e):
                for j, w in enumerate((w1, w3, w2)):
                    sp.dma_start(wld[:, j], w[e, :, :].rearrange("(k p) n -> p k n", p=P)).then_inc(ld_w, 16)

            def load_gix(e, q):
                sp.dma_start(gix[q][:, :, :], slots[e, :, :]).then_inc(ld_gix[q], 16)

            def load_six(e, q):
                sp.dma_start(six[q][:, :, :], slots[e, :, :]).then_inc(ld_six[q], 16)

            load_gix(0, 0)
            load_w(0)
            load_six(0, 0)

            def pair(i, first, last):
                for q in range(2):
                    e = i * 2 + q
                    if last and q == 1:
                        sp.wait_ge(d_wl, e + 1)
                        for j, w in enumerate((sw1, sw3, sw2)):
                            sp.dma_start(wld[:, j], w.rearrange("(k p) n -> p k n", p=P)).then_inc(ld_w, 16)
                        continue
                    if not (first and q == 0):
                        sp.wait_ge(p_et, e * NCH)
                    load_gix(e + 1, 1 - q)
                    sp.wait_ge(d_wl, e + 1)
                    load_w(e + 1)
                    if not (first and q == 0):
                        sp.wait_ge(d_sx, e * NCH)
                    load_six(e + 1, 1 - q)

            pair(0, True, False)
            with sp.Fori(1, E // 2 - 1) as i:
                pair(i, False, False)
            pair(E // 2 - 1, False, True)
            meet(sp, "sp", 7)

            NC = NT // (CH * P)

            def load_c(n, q):
                sp.dma_start(xg[q][:, :, :], xf_d[bass.ds(n * CH * P, CH * P), :].rearrange("(p t) d -> p t d", t=CH)) \
                  .then_inc(ld_c[q], 16)

            def load_y(n, q):
                sp.dma_start(y4[q][:, :, :, :], y4_d[bass.ds(n * CH * P * TOPK, CH * P * TOPK), :]
                             .rearrange("(p t k) d -> p t k d", t=CH, k=TOPK)).then_inc(ld_y[q], 16)

            def load_r(n, q):
                sp.dma_start(xr[q][:, :, :], x2_d[bass.ds(n * CH * P, CH * P), :].rearrange("(p t) d -> p t d", t=CH)) \
                  .then_inc(ld_r[q], 16)

            def store(n, q):
                sp.wait_ge(d_out, n + 1)
                sp.dma_start(out[bass.ds(n * CH * P, CH * P), :].rearrange("(p t) d -> p t d", t=CH), yout[q][:, :, :]) \
                  .then_inc(st_out[q], 16)

            for q in range(GC):
                load_c(q, q)
                load_y(q, q)

            def group(i, first, last):
                for q in range(GC):
                    n = i * GC + q
                    if not last:
                        sp.wait_ge(p_et, n + (E * NCH + 1))
                        load_c(n + GC, q)
                        sp.wait_ge(g_ys, n + 1)
                        load_y(n + GC, q)
                    if not first:
                        store(n - GC, q)
                    load_r(n, q)

            group(0, True, False)
            with sp.Fori(1, NC // GC - 1) as i:
                group(i, False, False)
            group(NC // GC - 1, False, True)
            for q in range(GC):
                store(NC - GC + q, q)
            for q in range(GC):
                sp.wait_ge(st_out[q], 16 * (NC // GC) + 16)

        @block.gpsimd
        def _(pool):
            nc.gpsimd.memset(zero[:, :], 0.0).then_inc(s_zero, 1)
            fr = free_rec[:, :].rearrange("p (s r) -> p s r", r=REC)
            nc.gpsimd.memset(fr[:, :, 0:1], NT).then_inc(s_zero, 1)
            nc.gpsimd.memset(fr[:, :, 1:2], FAR).then_inc(s_zero, 1)
            nc.gpsimd.memset(fr[:, :, 2:3], 0).then_inc(s_zero, 1)
            pool.sem_inc(g_rec, 1)
            meet(pool, "pool", 1)

            def pass_a(b):
                def normalise(g, has_prev):
                    pool.wait_ge(d_rs, g + 1)
                    if has_prev:
                        pool.wait_ge(p_x, g * KD)
                    settled(pool)
                    for t in range(TB):
                        ins = nc.gpsimd.tensor_scalar(xn[:, t, :], xa[:, t, :], rs_a[:, t:t + 1], nm_a[:, t:t + 1],
                                                      ALU.mult, ALU.add)
                    ins.then_inc(g_xn, 1)

                def heads(g, has_prev):
                    pool.wait_ge(a_u, g + 1)
                    if has_prev:
                        pool.wait_ge(d_prod, g)
                    nc.gpsimd.tensor_tensor(hd[:, :, :, :], u[:, :, :].unsqueeze(2).to_broadcast([P, TB, 4, QK]),
                                            gam[:, :].rearrange("p (h d) -> p h d", h=4).unsqueeze(1)
                                            .to_broadcast([P, TB, 4, QK]), ALU.mult).then_inc(g_gam, 1)
                    pool.wait_ge(g_gam, g + 1)
                    h3 = hd[:, :, :, :].rearrange("p t h d -> p t (h d)")
                    nc.gpsimd.tensor_tensor(h3, h3, bet[:, :].unsqueeze(1).to_broadcast([P, TB, 4 * QK]), ALU.add) \
                        .then_inc(g_hd, 1)

                normalise(b * NB, False)

                heads(b * NB, False)

                def body(g, m, has_prev, ahead):
                    if ahead >= 1:
                        normalise(g + 1, True)
                        heads(g + 1, True)

                blocks_a(pool, b, body)

            def pass_b(b):
                def load_parts(g):
                    pool.dma_start(xh[:, :, :], xh_d[g, :, :]).then_inc(ld_xh, 16)
                    pool.dma_start(xl[:, :, :], xl_d[g, :, :]).then_inc(ld_xh, 16)

                def next_parts(g):
                    pool.wait_ge(p_g, g * KH)
                    settled(pool)
                    load_parts(g)

                def scatter(g, loads):
                    pool.wait_ge(d_rec, g + 2)
                    settled(pool)
                    for j in range(TB * TOPK):
                        if loads and j == TB * TOPK // 2:
                            next_parts(g + AHEAD)
                        pool.indirect_dma_start(
                            slot_d, bass.IndirectOffsetOnAxis(ap=dsti[:, j:j + 1], axis=0), rec[:, j, :], None,
                            bounds_check=NSLOT - 1, oob_is_err=False).then_inc(st_rec, 16)
                    pool.wait_ge(st_rec, (g + 1) * (16 * TB * TOPK))
                    pool.sem_inc(g_rec, 1)

                AHEAD = LAG + 2
                load_parts(b * NB)
                for m in range(1, AHEAD):
                    next_parts(b * NB + m)
                with pool.Fori(0, NB - AHEAD) as m:
                    scatter(b * NB + m, True)
                with pool.Fori(NB - AHEAD, NB) as m:
                    scatter(b * NB + m, False)

            attention(pool, "pool", pass_a, pass_b)
            meet(pool, "pool", 6)

            def gather(c, i, first):
                i, c = (i + 1, c - 2 * NCH) if c >= 2 * NCH else (i, c)
                e, q, buf = i * 2 + c // NCH, c // NCH, c % NXB
                if c % NCH == 0:
                    pool.wait_ge(ld_gix[q], (i + 1) * 16)
                if not first:
                    pool.wait_ge(p_et, i * (2 * NCH) + (c - NXB + 1))
                settled(pool)
                for t in range(CH):
                    s = (c % NCH) * CH + t
                    pool.indirect_dma_start(xg[buf][:, t, :], None, xf_d,
                                            bass.IndirectOffsetOnAxis(ap=gix[q][:, s, 0:1], axis=0)) \
                        .then_inc(ld_xg[buf], 16)

            def put(c, i):
                buf = c % NXB
                pool.wait_ge(a_eo, i * (2 * NCH) + (c + 1))
                settled(pool)
                for t in range(CH):
                    pool.indirect_dma_start(y4_d, bass.IndirectOffsetOnAxis(ap=sx[buf][:, t, 1:2], axis=0),
                                            eo[buf][:, t, :], None, bounds_check=NROW - 1, oob_is_err=False) \
                        .then_inc(st_eo[buf], 16)

            AHEAD = 3
            for c in range(AHEAD):
                gather(c, 0, True)

            def pair(i, first, last):
                for c in range(2 * NCH):
                    if not (last and c + AHEAD >= 2 * NCH):
                        gather(c + AHEAD, i, first and c + AHEAD < NXB)
                    if c > 0:
                        put(c - 1, i)
                put(2 * NCH - 1, i)

            pair(0, True, False)
            with pool.Fori(1, E // 2 - 1) as i:
                pair(i, False, False)
            pair(E // 2 - 1, False, True)
            for buf in range(NXB):
                pool.wait_ge(st_eo[buf], E * NCH // NXB * 16 * CH)
            meet(pool, "pool", 7)

            def add_rows(n, q, i, first):
                pool.wait_ge(ld_y[q], i * 16 + 16)
                if not first:
                    pool.wait_ge(d_tot, n - 1)
                nc.gpsimd.tensor_tensor(ysum[q % 2][:, :, :, :], y4[q][:, :, 0:2, :], y4[q][:, :, 2:4, :], ALU.add) \
                    .then_inc(g_ys, 1)

            def group(i, first):
                for q in range(GC):
                    add_rows(i * GC + q, q, i, first and q < 2)

            group(0, True)
            with pool.Fori(1, NT // (CH * P) // GC) as i:
                group(i, False)

        @block.scalar
        def _(act):
            act.wait_ge(s_load, 16 * 18)
            for j, w in enumerate((wvh, wgh)):
                act.wait_ge(s_dve, 8 + 2 * j)
                nc.scalar.activation(w[:, :, :], wscl[:, :, :], ACT.Copy).then_inc(s_act, 1)
            act.wait_ge(s_dve, 17)
            nc.scalar.activation(vbh[:, :], vb[:, :], ACT.Copy).then_inc(s_act, 1)
            nc.scalar.activation(obh[:, :], ob[:, :], ACT.Copy).then_inc(s_act, 1)
            meet(act, "act", 1)

            def pass_a(b):
                def sqrt_x(g):
                    act.wait_ge(d_stat, g + 1)
                    nc.scalar.activation(sd_a[:, :], mv_a[:, :, 1], ACT.Sqrt, bias=eps[:, 1:2], scale=1.0 + EPS) \
                        .then_inc(a_sd, 1)

                def x_high(g, first):
                    for k in range(KD):
                        act.wait_ge(p_x, g * KD + (k + 1))
                        ins = nc.scalar.activation(xta[:, k, :], bank[k][:, :], ACT.Copy)
                    ins.then_inc(a_xt, 1)
                    if not first:
                        act.wait_ge(st_xh, g * 16)
                    for k in range(KD):
                        nc.scalar.activation(xh[:, k, :], bank[k][:, :], ACT.Copy).then_inc(a_xh, 1)

                def silu_u(g, first):
                    act.wait_ge(p_u, g + 1)
                    if not first:
                        act.wait_ge(g_gam, g)
                    nc.scalar.activation(u[:, :, :], bank[2][:, 0:TB * QK].rearrange("p (t d) -> p t d", t=TB),
                                         ACT.Silu).then_inc(a_u, 1)

                def values_out(g, m):
                    for c in range(KH):
                        act.wait_ge(p_qo, g * KH + (c + 1))
                        nc.scalar.activation(qo_all[:, c, cols(m)], bank[QO_BANK[c]][:, :], ACT.Copy).then_inc(a_qo, 1)

                sqrt_x(b * NB)
                x_high(b * NB, True)
                silu_u(b * NB, True)
                sqrt_x(b * NB + 1)

                def body(g, m, has_prev, ahead):
                    if has_prev:
                        values_out(g - 1, m - 1)
                    for t in range(TB):
                        act.wait_ge(p_v, g * TB + (t + 1))
                        nc.scalar.activation(vt[:, t, :], bank[t % 2][:, :], ACT.Silu).then_inc(a_v, 1)
                        act.wait_ge(a_v, g * TB + (t + 1))
                        nc.scalar.activation(vh[:, t, :], vt[:, t, :], ACT.Copy).then_inc(a_vh, 1)
                        if t == 1:
                            act.wait_ge(d_head, g + 1)
                            nc.scalar.activation(pbh[:, :, :], hr[:, :, 2:4, :].rearrange("p t h d -> p t (h d)"), ACT.Copy) \
                                .then_inc(a_pbh, 1)
                    act.wait_ge(p_ta, g + 1)
                    nc.scalar.activation(lqh[QK:2 * QK, cols(m)], bank[3][QK:2 * QK, :], ACT.Copy).then_inc(a_ta, 1)
                    if ahead >= 1:
                        x_high(g + 1, False)
                        silu_u(g + 1, False)
                    if ahead >= 2:
                        sqrt_x(g + 2)

                blocks_a(act, b, body)
                values_out(b * NB + (NB - 1), NB - 1)
                act.wait_ge(p_kv, (b + 1) * (NB * TB))
                nc.scalar.activation(kvh[QK:2 * QK, :], bank[7][QK:2 * QK, :], ACT.Copy, scale=1.0 / S).then_inc(a_kvh, 1)

            def pass_b(b):
                def gates(g, c, has_prev):
                    act.wait_ge(p_g, g * KH + (c + 1))
                    if c >= 2 or has_prev:
                        act.wait_ge(d_og, g * KH + (c - 1))
                    nc.scalar.activation(gsb[c % 2][:, :], bank[c % 2][:, :], ACT.Silu, bias=gb[:, c:c + 1]).then_inc(a_gs, 1)

                def norm(dst_, src, rs, nm, first, done):
                    for t in range(TB):
                        ins = nc.scalar.activation(dst_[:, t, :], src[:, t, :], ACT.Identity,
                                                   bias=nm[:, first + t:first + t + 1], scale=rs[:, first + t:first + t + 1])
                    ins.then_inc(done, 1)

                def roots(g, on):
                    if on[1]:
                        act.wait_ge(d_st1, g)
                    if on[2]:
                        act.wait_ge(d_st3, g - 1)
                    nc.scalar.activation(sd_b[:, :], mv_b[:, :, 1], ACT.Sqrt, bias=eps[:, 0:1]).then_inc(a_root, 1)

                def root_m(g):
                    act.wait_ge(d_st2, g + 1)
                    nc.scalar.activation(sd_m[:, :], mv_m[:, :, 1], ACT.Sqrt, bias=eps[:, 0:1]).then_inc(a_rootm, 1)

                def turn(g, has_prev):
                    if has_prev:
                        act.wait_ge(p_lg, g)
                    for k in range(KD):
                        act.wait_ge(p_xt, g * KD + (k + 1))
                        nc.scalar.activation(xft[:, k, :], bank[6 + k][:, :], ACT.Copy).then_inc(a_xft, 1)

                def expo(g):
                    act.wait_ge(d_lg, g + 1)
                    nc.scalar.activation(pr[:, :, :], lg[:, :, :], ACT.Exp).then_inc(a_exp, 1)

                def body(g, m, on):
                    if on[3]:
                        expo(g - 3)
                    if on[0]:
                        for c in range(KH):
                            gates(g, c, on[1])
                    if on[1] or on[2]:
                        roots(g, on)
                        act.wait_ge(d_inv, g + b)
                    if on[1]:
                        if on[2]:
                            act.wait_ge(d_x2, g - 1)
                        norm(yb, yo, rs_b, nm_b, 0, a_n1)
                    if on[2]:
                        if on[3]:
                            act.wait_ge(st_xf, (g - 2) * 16)
                            act.wait_ge(p_xt, (g - 2) * KD)
                        norm(xfb, x2b, rs_b, nm_b, TB, a_n3)
                    if on[1]:
                        root_m(g - 1)
                        act.wait_ge(d_invm, g)
                        norm(yb, yb, rs_m, nm_m, 0, a_n2)
                    if on[2]:
                        turn(g - 2, on[3])
                    if on[0]:
                        for h in range(2):
                            act.wait_ge(p_wo, g * 2 + (h + 1))
                            nc.scalar.activation(yo[:, 2 * h:2 * h + 2, :],
                                                 bank[4 + h][:, :].rearrange("p (t d) -> p t d", t=2), ACT.Copy) \
                                .then_inc(a_yo, 1)

                blocks_b(act, b, body)

            attention(act, "act", pass_a, pass_b)
            meet(act, "act", 6)

            def split_w(e, q):
                act.wait_ge(ld_w, (e + 1) * 48)
                for j in range(3):
                    nc.scalar.activation(wh[q][:, j], wld[:, j], ACT.Copy).then_inc(a_wh, 1)

            def e_high(n, q):
                act.wait_ge(p_et, n + 1)
                nc.scalar.activation(eh[q][:, :, :], bank[q][:, :].rearrange("p (k n) -> p k n", k=KD), ACT.Copy) \
                    .then_inc(a_eh, 1)

            def silu(n, q):
                act.wait_ge(p_up, n + 1)
                nc.scalar.activation(sa[q][:, :, :], bank[2 + q][:, :].rearrange("p (k n) -> p k n", k=KD), ACT.Silu) \
                    .then_inc(a_sa, 1)

            def h_high(n, q):
                act.wait_ge(d_hf, n + 1)
                nc.scalar.activation(hh[q][:, :, :], hf[q][:, :, :], ACT.Copy).then_inc(a_hh, 1)

            def weighted(c, i, first):
                buf, n = c % NXB, i * (2 * NCH) + c
                act.wait_ge(p_dn, n + 1)
                act.wait_ge(d_sx, n + 1)
                if not (first and c < NXB):
                    act.wait_ge(st_eo[buf], (i * 2 + c // NXB) * (16 * CH))
                for t in range(CH):
                    ins = nc.scalar.activation(eo[buf][:, t, :], bank[6 + c % 2][:, t * D:(t + 1) * D], ACT.Copy,
                                               scale=sx[buf][:, t, 2:3].bitcast(F32))
                ins.then_inc(a_eo, 1)

            split_w(0, 0)
            e_high(0, 0)

            def pair(i, first, last):
                for c in range(2 * NCH):
                    n = i * (2 * NCH) + c
                    if not (last and c == 2 * NCH - 1):
                        e_high(n + 1, (c + 1) % 2)
                    silu(n, c % 2)
                    h_high(n, c % 2)
                    if c > 0:
                        weighted(c - 1, i, first)
                    if c % NCH == 2:
                        split_w(i * 2 + (c // NCH + 1), (c // NCH + 1) % 2)
                weighted(2 * NCH - 1, i, first)

            pair(0, True, False)
            with act.Fori(1, E // 2 - 1) as i:
                pair(i, False, False)
            pair(E // 2 - 1, False, True)
            meet(act, "act", 7)

            NC, N0 = NT // (CH * P), E * NCH

            def c_root(i):
                act.wait_ge(d_cst, i * GC)
                nc.scalar.activation(sd_c[:, :], mv_c[:, :, 1], ACT.Sqrt, bias=eps[:, 0:1]).then_inc(a_csd, 1)
                act.wait_ge(d_crs, i)

            def c_norm(i, q):
                act.wait_ge(st_out[q], i * 16)
                for t in range(CH):
                    c = q * CH + t
                    ins = nc.scalar.activation(yout[q][:, t, :], ytot[q][:, t, :], ACT.Identity, bias=nm_c[:, c:c + 1],
                                               scale=rs_c[:, c:c + 1])
                ins.then_inc(a_cn, 1)

            e_high(N0, 0)

            def group(i, first, last):
                for q in range(GC):
                    n = i * GC + q
                    if not (last and q == GC - 1):
                        e_high(n + (N0 + 1), 1 - q % 2)
                    silu(n + N0, q % 2)
                    h_high(n + N0, q % 2)
                    if not first:
                        if q == 1:
                            c_root(i)
                            c_norm(i, 0)
                            c_norm(i, 1)
                        if q == 2:
                            c_norm(i, 2)
                            c_norm(i, 3)

            group(0, True, False)
            with act.Fori(1, NC // GC - 1) as i:
                group(i, False, False)
            group(NC // GC - 1, False, True)
            c_root(NC // GC)
            for q in range(GC):
                c_norm(NC // GC, q)

        @block.vector
        def _(dve):
            own = Own(dve, s_dve, 0)
            own.step(nc.vector.memset(eps[:, 0:1], EPS))
            own.step(nc.vector.memset(eps[:, 1:2], EPS * EPS))
            own.step(nc.vector.memset(hit_all[:, :], 0.0))
            own.step(nc.vector.memset(ones_b[:, :], 1.0))
            own.step(nc.vector.memset(ones_r[:, :].bitcast(F32), 1.0))
            own.step(nc.vector.memset(qb_f[:, :], 0.0))
            dve.wait_ge(s_load, 16 * 18)
            for k in range(KD):
                ins = nc.vector.tensor_scalar(wq[:, k, :], qraw[:, k, :], l1w[:, k:k + 1], None, ALU.mult)
            own.step(ins)
            for j, (hi, lo) in enumerate(((wvh, wvl), (wgh, wgl))):
                own.wait()
                for k in range(KD):
                    ins = nc.vector.tensor_scalar(wscl[:, k, :], wraw[:, j, k, :], l1w[:, k:k + 1], None, ALU.mult)
                own.step(ins)
                dve.wait_ge(s_act, j + 1)
                own.wait()
                own.step(nc.vector.tensor_tensor(lo[:, :, :], wscl[:, :, :], hi[:, :, :].bitcast(F32), ALU.subtract))
            for k in range(KD):
                own.step(nc.vector.tensor_copy(bmat[:, k, :], l1b[:, k:k + 1].to_broadcast([P, P])))
            dve.wait_ge(s_pe, 1)
            own.step(nc.vector.tensor_tensor(gb[:, :], bank[1][:, 0:KH], gbi[:, :], ALU.add))
            own.step(nc.vector.tensor_tensor(vb[:, :], bank[2][:, :], vb[:, :], ALU.add))
            own.step(nc.vector.tensor_tensor(qb[:, :], bank[0][:, 0:QK], qb[:, :], ALU.add))
            own.step(nc.vector.tensor_copy(tri[:, :], cst[:, P:2 * P]))
            for z in (vb_r, ob_r, kvh, kvl, lqh, lql):
                own.step(nc.vector.memset(z[:, :].bitcast(F32), 0.0))
            dve.wait_ge(s_act, 4)
            own.wait()
            own.step(nc.vector.tensor_tensor(vbl[:, :], vb[:, :], vbh[:, :].bitcast(F32), ALU.subtract))
            own.step(nc.vector.tensor_tensor(obl[:, :], ob[:, :], obh[:, :].bitcast(F32), ALU.subtract))
            own.wait()
            own.step(nc.vector.tensor_copy(qb_f[0:1, :], qb[0:1, :]))
            for dst_, hi, lo in ((vb_r, vbh, vbl), (ob_r, obh, obl)):
                own.step(nc.vector.tensor_copy(dst_[0:1, :], hi[0:1, :].bitcast(F32)))
                own.step(nc.vector.tensor_copy(dst_[32:33, :], lo[32:33, :].bitcast(F32)))
            own.step(nc.vector.memset(hit_was[:, :], 0.0))
            own.step(nc.vector.memset(toep[:, :], 0.0))
            own.step(nc.vector.tensor_copy(base_f[:, :], tok_id[:, :]))
            M, R = G64 - 1, MAXREL
            edge = pe_row[:, R:R + 1]
            nc.vector.tensor_copy(ext[:, 0:M - R], edge.to_broadcast([G64, M - R])).then_inc(s_ext, 1)
            nc.vector.tensor_copy(ext[:, M:M + R + 1], pe_row[:, 0:R + 1]).then_inc(s_ext, 1)
            nc.vector.tensor_copy(ext[:, M + R + 1:2 * G64], edge.to_broadcast([G64, 2 * G64 - M - R - 1])).then_inc(s_ext, 1)
            nc.vector.tensor_copy(ext[:, M - R:M], pe_row[:, R:0:-1]).then_inc(s_ext, 1)
            dve.wait_ge(s_tl, 32)
            own.wait()
            own.step(nc.vector.tensor_tensor(bias_s[:, :], toep[:, :], off_block, ALU.add))
            dve.sem_inc(d_rec, 1)
            meet(dve, "dve", 1)

            def stats(own_, src, st, mv, tiles, done):
                for t in range(tiles):
                    ins = nc.vector.bn_stats(st[:, t, :], src(t))
                own_.step(ins)
                own_.wait()
                nc.vector.memset(gate_cell[:, :], 0.0)
                for t in range(tiles):
                    ins = nc.vector.bn_aggr(mv[:, t, :], st[:, t, :])
                ins.then_inc(done, 1)

            def inverse(own_, sd, rs, nm, mv, done):
                own_.step(nc.vector.reciprocal(rs[:, :], sd[:, :]))
                own_.wait()
                nc.vector.scalar_tensor_tensor(nm[:, :], mv[:, :, 0], -1.0, rs[:, :], ALU.mult, ALU.mult).then_inc(done, 1)

            def pass_a(b):
                def x_stats(g):
                    dve.wait_ge(ld_x, (g + 1) * 16)
                    stats(Own(dve, o_ln, g), lambda t: xa[:, t, :], st_a, mv_a, TB, d_stat)

                def x_scale(g, has_prev):
                    dve.wait_ge(a_sd, g + 1)
                    if has_prev:
                        dve.wait_ge(g_xn, g)
                    inverse(Own(dve, o_rs, g), sd_a, rs_a, nm_a, mv_a, d_rs)

                def x_low(g, first):
                    if not first:
                        dve.wait_ge(st_xl, g * 16)
                    for k in range(KD):
                        dve.wait_ge(a_xh, g * KD + (k + 1))
                        nc.vector.tensor_tensor(xl[:, k, :], bank[k][:, :], xh[:, k, :].bitcast(F32),
                                                ALU.subtract).then_inc(d_xl, 1)

                def rotate(g, m):
                    a1, a2 = hd[:, :, :, 0:HALF], hd[:, :, :, HALF:QK]
                    c_, s_ = (w[:, bass.ds(m * TB, TB), :].unsqueeze(2).to_broadcast([P, TB, 4, HALF]) for w in (cos, sin))
                    dve.wait_ge(g_hd, g + 1)
                    h1, h2 = hr[:, :, :, 0:HALF], hr[:, :, :, HALF:QK]
                    nc.vector.tensor_tensor(h1, a1, c_, ALU.mult)
                    nc.vector.tensor_tensor(prod[0][:, :, :, :], a2, s_, ALU.mult)
                    nc.vector.tensor_tensor(h2, a2, c_, ALU.mult)
                    nc.vector.tensor_tensor(prod[1][:, :, :, :], a1, s_, ALU.mult).then_inc(d_prod, 1)
                    dve.wait_ge(d_prod, g + 1)
                    nc.vector.tensor_tensor(h1, h1, prod[0][:, :, :, :], ALU.subtract)
                    nc.vector.tensor_tensor(h2, h2, prod[1][:, :, :, :], ALU.add) \
                        .then_inc(d_head, 1)

                def kb_low(g):
                    dve.wait_ge(a_pbh, g + 1)
                    nc.vector.tensor_tensor(pbl[:, :, :], hr[:, :, 2:4, :].rearrange("p t h d -> p t (h d)"),
                                            pbh[:, :, :].bitcast(F32), ALU.subtract).then_inc(d_pbl, 1)

                def v_low(g, t):
                    dve.wait_ge(a_vh, g * TB + (t + 1))
                    nc.vector.tensor_tensor(vl[:, t, :], vt[:, t, :], vh[:, t, :].bitcast(F32), ALU.subtract) \
                        .then_inc(d_vl, 1)

                def q_and_k(g):
                    dve.wait_ge(p_ta, g + 1)
                    nc.vector.tensor_copy(qqt[:, :], bank[3][0:QK, :])
                    dve.wait_ge(p_tb, g + 1)
                    nc.vector.tensor_copy(kkt[:, :], bank[4][0:QK, :]).then_inc(d_tab, 1)

                def q_low(g, m):
                    dve.wait_ge(a_ta, g + 1)
                    nc.vector.tensor_tensor(lql[QK:2 * QK, cols(m)], bank[3][QK:2 * QK, :],
                                            lqh[QK:2 * QK, cols(m)].bitcast(F32), ALU.subtract).then_inc(d_lql, 1)

                def scores(g):
                    dve.wait_ge(p_s, g + 1)
                    nc.vector.scalar_tensor_tensor(at[:, :].rearrange("p (t n) -> p t n", t=TB),
                                                   bank[5][:, :].rearrange("p (t n) -> p t n", t=TB), 1.0 / G64,
                                                   bias_s[:, :].unsqueeze(1).to_broadcast([P, TB, P]),
                                                   ALU.mult, ALU.add).then_inc(o_at, 1)
                    dve.wait_ge(o_at, g + 1)
                    nc.vector.scalar_tensor_tensor(at[:, :], at[:, :], 0.0, at[:, :], ALU.max, ALU.mult).then_inc(d_at, 1)

                g0 = b * NB
                x_stats(g0)
                x_scale(g0, False)
                x_stats(g0 + 1)
                x_low(g0, True)
                x_scale(g0 + 1, True)

                def body(g, m, has_prev, ahead):
                    rotate(g, m)
                    v_low(g, 0)
                    v_low(g, 1)
                    kb_low(g)
                    v_low(g, 2)
                    v_low(g, 3)
                    q_and_k(g)
                    if ahead >= 2:
                        x_stats(g + 2)
                    q_low(g, m)
                    scores(g)
                    if ahead >= 1:
                        x_low(g + 1, False)
                    if ahead >= 2:
                        x_scale(g + 2, True)

                blocks_a(dve, b, body)
                dve.wait_ge(a_kvh, b + 1)
                nc.vector.scalar_tensor_tensor(kvl[QK:2 * QK, :], bank[7][QK:2 * QK, :], 1.0 / S,
                                               kvh[QK:2 * QK, :].bitcast(F32), ALU.mult, ALU.subtract).then_inc(o_kv, 1)

            def pass_b(b):
                nc.vector.memset(mv_b[:, :, :], 0.0)

                def gated(g, c, m, has_prev):
                    dve.wait_ge(p_lo, g * KH + (c + 1))
                    nc.vector.tensor_tensor(mixed[c % 2][:, :], bank[2 + c % 2][:, :], qo_all[:, c, cols(m)], ALU.add) \
                        .then_inc(d_mix, 1)
                    dve.wait_ge(a_gs, g * KH + (c + 1))
                    dve.wait_ge(d_mix, g * KH + (c + 1))
                    if c == 0 and has_prev:
                        dve.wait_ge(p_wo, g * 2)
                    nc.vector.tensor_tensor(og[:, c, :], mixed[c % 2][:, :], gsb[c % 2][:, :], ALU.mult).then_inc(d_og, 1)

                def wide(ap, n):
                    return ap.unsqueeze(2).to_broadcast([P, TB, n])

                def less_max(g, own_):
                    dve.wait_ge(p_lg, g + 1)
                    z = bank[6][:, 0:TB * E].rearrange("p (t e) -> p t e", t=TB)
                    own_.step(nc.vector.tensor_reduce(mx[:, :], z, AX, ALU.max))
                    own_.wait()
                    nc.vector.tensor_tensor(lg[:, :, :], z, wide(mx[:, :], E), ALU.subtract).then_inc(d_lg, 1)

                def softmax(g, own_):
                    dve.wait_ge(a_exp, g + 1)
                    own_.step(nc.vector.tensor_reduce(sm[:, :], pr[:, :, :], AX, ALU.add))
                    own_.wait()
                    own_.step(nc.vector.reciprocal(rsm[:, :], sm[:, :]))
                    own_.wait()
                    own_.step(nc.vector.tensor_tensor(pr[:, :, :], pr[:, :, :], wide(rsm[:, :], E), ALU.mult))
                    own_.wait()
                    own_.step(nc.vector.tensor_reduce(gs[:, :, :], pr[:, :, :].rearrange("p t (a c) -> p t a c", a=GRP), AX, ALU.max))
                    own_.wait()
                    nc.vector.memset(gate_cell[:, :], 0.0)

                def groups(own_):
                    top4(own_, gs, top_g, ix_g, fx_g)

                def masked(own_):
                    own_.step(nc.vector.tensor_tensor(
                        eq_g[:, :, :, :], iota_e[:, 0:GRP].unsqueeze(1).unsqueeze(1).to_broadcast([P, TB, TOPK, GRP]),
                        fx_g[:, :, 0:TOPK].unsqueeze(3).to_broadcast([P, TB, TOPK, GRP]), ALU.is_equal))
                    own_.wait()
                    own_.step(nc.vector.tensor_reduce(keep[:, :, :], eq_g[:, :, :, :].rearrange("p t k a -> p t a k"), AX, ALU.add))
                    own_.wait()
                    nc.vector.tensor_scalar(kneg[:, :, :], keep[:, :, :], -1.0, None, ALU.add)
                    m4 = msk[:, :, :].rearrange("p t (a c) -> p t a c", a=GRP)
                    own_.step(nc.vector.tensor_tensor(m4, pr[:, :, :].rearrange("p t (a c) -> p t a c", a=GRP),
                                                      keep[:, :, :].unsqueeze(3).to_broadcast([P, TB, GRP, EG]), ALU.mult))
                    own_.wait()
                    own_.step(nc.vector.tensor_tensor(m4, m4, kneg[:, :, :].unsqueeze(3).to_broadcast([P, TB, GRP, EG]), ALU.add))
                    own_.wait()
                    nc.vector.memset(gate_cell[:, :], 0.0)

                def experts(own_):
                    top4(own_, msk, top_e, ix_e, fx_e)

                def hits(own_):
                    own_.step(nc.vector.tensor_tensor(
                        oh[:, :, :, :], iota_e.unsqueeze(1).unsqueeze(1).to_broadcast([P, TB, TOPK, E]),
                        fx_e[:, :, 0:TOPK].unsqueeze(3).to_broadcast([P, TB, TOPK, E]), ALU.is_equal))
                    own_.wait()
                    nc.vector.tensor_reduce(wsum[:, :], top_e[:, :, 0:TOPK], AX, ALU.add)
                    with nc.allow_low_precision("0 and 1 are exact"):
                        nc.vector.tensor_reduce(hit[:, :, :], oh[:, :, :, :].rearrange("p t k e -> p t e k"), AX, ALU.add) \
                            .then_inc(d_hit, 1)
                    assert own_.n == 16, own_.n

                def top4(own_, src, val, ix, fx):
                    for t in range(TB):
                        ins = nc.vector.max(val[:, t, :], src[:, t, :])
                    own_.step(ins)
                    own_.wait()
                    nc.vector.memset(gate_cell[:, :], 0.0)
                    for t in range(TB):
                        ins = nc.vector.max_index(ix[:, t, :], val[:, t, :], src[:, t, :])
                    own_.step(ins)
                    own_.wait()
                    own_.step(nc.vector.tensor_copy(fx[:, :, :], ix[:, :, :]))
                    own_.wait()

                def slots(g):
                    own_ = Own(dve, o_fin, g * 7)
                    dve.wait_ge(p_cs, g + 1)
                    n4 = bank[7][:, 0:TB * E].rearrange("p (t e) -> p t e", t=TB)
                    nc.vector.tensor_reduce(hsum[:, :], hit[:, :, :].rearrange("p t e -> p e t"), AX, ALU.add)
                    nc.vector.tensor_scalar(wrec[:, :], wsum[:, :], 1e-9, None, ALU.add)
                    own_.step(nc.vector.tensor_tensor(ohp[:, :, :, :], oh[:, :, :, :],
                                                      n4.unsqueeze(2).to_broadcast([P, TB, TOPK, E]), ALU.mult))
                    own_.wait()
                    own_.step(nc.vector.tensor_reduce(pos[:, :, :], ohp[:, :, :, :], AX, ALU.add))
                    nc.vector.tensor_tensor(hit_all[:, :], hit_all[:, :], hsum[:, :], ALU.add)
                    own_.step(nc.vector.reciprocal(wrec[:, :], wrec[:, :]))
                    own_.wait()
                    own_.step(nc.vector.tensor_copy(hit_was[:, :], hit_all[:, :]))
                    nc.vector.tensor_scalar(over[:, :, :], pos[:, :, :], float(CAP), float(FAR), ALU.is_ge, ALU.mult)
                    own_.step(nc.vector.scalar_tensor_tensor(dst[:, :, :], fx_e[:, :, 0:TOPK], float(CAP), pos[:, :, :],
                                                             ALU.mult, ALU.add))
                    dve.wait_ge(g_rec, g + 1)
                    own_.wait()
                    own_.step(nc.vector.tensor_tensor(dsti[:, :].rearrange("p (t k) -> p t k", t=TB), dst[:, :, :],
                                                      over[:, :, :], ALU.add))
                    nc.vector.tensor_copy(rec[:, :, 0:2], base_f[:, :].rearrange("p (n r) -> p n r", r=2))
                    own_.step(nc.vector.tensor_tensor(
                        rec[:, :, 2:3].bitcast(F32).rearrange("p (t k) r -> p t (k r)", t=TB), top_e[:, :, 0:TOPK],
                        wrec[:, :].unsqueeze(2).to_broadcast([P, TB, TOPK]), ALU.mult))
                    own_.wait()
                    step_ = base_f[:, :].rearrange("p (n r) -> p n r", r=2)
                    nc.vector.tensor_scalar(step_[:, :, 0:1], step_[:, :, 0:1], float(BLK), None, ALU.add)
                    nc.vector.tensor_scalar(step_[:, :, 1:2], step_[:, :, 1:2], float(BLK * TOPK), None, ALU.add) \
                        .then_inc(d_rec, 1)
                    assert own_.n == 7, own_.n

                def weight_bias(g):
                    own_ = Own(dve, o_wb, g * 2)
                    dve.wait_ge(a_n1, g + 1)
                    dve.wait_ge(ld_w2, b * 32 + 32)
                    for w, op in ((w2b, ALU.mult), (b2b, ALU.add)):
                        own_.step(nc.vector.tensor_tensor(yb[:, :, :], yb[:, :, :],
                                                          w[:, :].unsqueeze(1).to_broadcast([P, TB, D]), op))
                        own_.wait()

                def add_x(g, has_prev):
                    dve.wait_ge(a_n2, g + 1)
                    dve.wait_ge(ld_xb, g * 16 + 16)
                    if has_prev:
                        dve.wait_ge(st_x2, g * 16)
                        dve.wait_ge(a_n3, g)
                    nc.vector.tensor_tensor(x2b[:, :, :], yb[:, :, :], xb[:, :, :], ALU.add).then_inc(d_x2, 1)

                def body(g, m, on):
                    routing = Own(dve, o_rt, (g - 3) * 16)
                    if on[3]:
                        less_max(g - 3, routing)
                    if on[0]:
                        gated(g, 0, m, on[1])
                    if on[2]:
                        dve.wait_ge(d_x2, g - 1)
                        stats(Own(dve, o_s3, g - 2), lambda t: x2b[:, t, :], st_3, mv_b[:, TB:2 * TB, :], TB, d_st3)
                    if on[0]:
                        gated(g, 1, m, on[1])
                    if on[1]:
                        dve.wait_ge(a_yo, g * 2)
                        stats(Own(dve, o_s1, g - 1), lambda t: yo[:, t, :], st_1, mv_b[:, 0:TB, :], TB, d_st1)
                    if on[0]:
                        gated(g, 2, m, on[1])
                    if on[3]:
                        softmax(g - 3, routing)
                    if on[0]:
                        gated(g, 3, m, on[1])
                    if on[3]:
                        groups(routing)
                    if on[1] or on[2]:
                        dve.wait_ge(a_root, g + b)
                        inverse(Own(dve, o_inv, g + b - 1), sd_b, rs_b, nm_b, mv_b, d_inv)
                    if on[3]:
                        masked(routing)
                    if on[1]:
                        weight_bias(g - 1)
                        stats(Own(dve, o_s2, g - 1), lambda t: yb[:, t, :], st_2, mv_m, TB, d_st2)
                    if on[3] and not on[1]:
                        experts(routing)
                    if on[1]:
                        dve.wait_ge(a_rootm, g)
                        inverse(Own(dve, o_invm, g - 1), sd_m, rs_m, nm_m, mv_m, d_invm)
                        if on[3]:
                            experts(routing)
                    if on[3]:
                        hits(routing)
                    if on[1]:
                        add_x(g - 1, on[2])
                    if on[3]:
                        slots(g - 3)

                blocks_b(dve, b, body)

            attention(dve, "dve", pass_a, pass_b)
            meet(dve, "dve", 6)

            def split_w(e, q):
                for j in range(3):
                    dve.wait_ge(a_wh, e * 3 + (j + 1))
                    ins = nc.vector.tensor_tensor(wl[q][:, j], wld[:, j], wh[q][:, j].bitcast(F32), ALU.subtract)
                ins.then_inc(d_wl, 1)

            def e_low(n, q):
                dve.wait_ge(a_eh, n + 1)
                nc.vector.tensor_tensor(el[q][:, :, :], bank[q][:, :].rearrange("p (k n) -> p k n", k=KD),
                                        eh[q][:, :, :].bitcast(F32), ALU.subtract).then_inc(d_el, 1)

            def product(n, q):
                dve.wait_ge(a_sa, n + 1)
                nc.vector.tensor_tensor(hf[q][:, :, :], bank[4 + q][:, :].rearrange("p (k n) -> p k n", k=KD),
                                        sa[q][:, :, :], ALU.mult).then_inc(d_hf, 1)

            def h_low(n, q):
                dve.wait_ge(a_hh, n + 1)
                nc.vector.tensor_tensor(hl[q][:, :, :], hf[q][:, :, :], hh[q][:, :, :].bitcast(F32), ALU.subtract) \
                    .then_inc(d_hl, 1)

            split_w(0, 0)
            e_low(0, 0)

            def records(c, i, first):
                q, buf, n = c // NCH, c % NXB, i * (2 * NCH) + c
                if c % NCH == 0:
                    dve.wait_ge(ld_six[q], (i + 1) * 16)
                if not (first and c < NXB):
                    dve.wait_ge(st_eo[buf], (i * 2 + c // NXB) * (16 * CH))
                s = (c % NCH) * CH
                nc.vector.tensor_copy(sx[buf][:, :, :], six[q][:, s:s + CH, :]).then_inc(d_sx, 1)

            def pair(i, first, last):
                for c in range(2 * NCH):
                    n = i * (2 * NCH) + c
                    if not (last and c == 2 * NCH - 1):
                        e_low(n + 1, (c + 1) % 2)
                    records(c, i, first)
                    product(n, c % 2)
                    h_low(n, c % 2)
                    if c % NCH == 2:
                        split_w(i * 2 + (c // NCH + 1), (c // NCH + 1) % 2)

            pair(0, True, False)
            with dve.Fori(1, E // 2 - 1) as i:
                pair(i, False, False)
            pair(E // 2 - 1, False, True)
            meet(dve, "dve", 7)

            NC, N0 = NT // (CH * P), E * NCH

            def total(n, q, first):
                dve.wait_ge(g_ys, n + 1)
                dve.wait_ge(p_dn, n + (N0 + 1))
                if not first:
                    dve.wait_ge(a_cn, n - (GC - 1))
                nc.vector.tensor_tensor(ytot[q][:, :, :], ysum[q % 2][:, :, 0, :],
                                        bank[6 + q % 2][:, :].rearrange("p (t d) -> p t d", t=CH), ALU.add).then_inc(d_acc, 1)
                dve.wait_ge(d_acc, n + 1)
                nc.vector.tensor_tensor(ytot[q][:, :, :], ytot[q][:, :, :], ysum[q % 2][:, :, 1, :], ALU.add).then_inc(d_tot, 1)
                dve.wait_ge(d_tot, n + 1)
                stats(Own(dve, o_c, n), lambda t: ytot[q][:, t, :], st_c, mv_c[:, q * CH:(q + 1) * CH, :], CH, d_cst)

            def c_inverse(i):
                dve.wait_ge(a_csd, i)
                inverse(Own(dve, o_cr, i - 1), sd_c, rs_c, nm_c, mv_c, d_crs)

            def final(i, q):
                dve.wait_ge(a_cn, i * GC + (q + 1 - GC))
                dve.wait_ge(ld_r[q], i * 16)
                nc.vector.tensor_tensor(yout[q][:, :, :], yout[q][:, :, :], xr[q][:, :, :], ALU.add).then_inc(d_out, 1)

            e_low(N0, 0)

            def group(i, first, last):
                for q in range(GC):
                    n = i * GC + q
                    if not (last and q == GC - 1):
                        e_low(n + (N0 + 1), 1 - q % 2)
                    product(n + N0, q % 2)
                    h_low(n + N0, q % 2)
                    if not first:
                        if q == 1:
                            c_inverse(i)
                        if q >= 2:
                            final(i, 2 * q - 4)
                            final(i, 2 * q - 3)
                    if not (first and q == 0):
                        total(n - 1, (q - 1) % GC, first or q == 0)

            group(0, True, False)
            with dve.Fori(1, NC // GC - 1) as i:
                group(i, False, False)
            group(NC // GC - 1, False, True)
            total(NC - 1, GC - 1, False)
            c_inverse(NC // GC)
            for q in range(GC):
                final(NC // GC, q)

        @block.tensor
        def _(pe):
            pe.wait_ge(s_dve, 13)
            pe.wait_ge(s_load, 16 * 18)
            for c in range(KH):
                for k in range(KD):
                    nc.tensor.matmul(bank[1][:, c:c + 1], wraw[:, 1, k, c * P:(c + 1) * P], l1b[:, k:k + 1],
                                     start=(k == 0), stop=(k == KD - 1))
            for k in range(KD):
                nc.tensor.matmul(bank[0][:, 0:QK], bmat[:, k, :], qraw[:, k, :], start=(k == 0), stop=(k == KD - 1))
            for k in range(KD):
                ins = nc.tensor.matmul(bank[2][:, :], bmat[:, k, :], wraw[:, 0, k, :], start=(k == 0), stop=(k == KD - 1))
            ins.then_inc(s_pe, 1)
            meet(pe, "pe", 1)

            def three(dst_, ah, al, bh, bl, start, stop, check=False):
                kw = {"skip_group_check": True} if check else {}
                nc.tensor.matmul(dst_, ah, bh, start=start, stop=False, **kw)
                nc.tensor.matmul(dst_, ah, bl, start=False, stop=False, **kw)
                return nc.tensor.matmul(dst_, al, bh, start=False, stop=stop, **kw)

            def pass_a(b):
                def turn_x(g, first):
                    pe.wait_ge(g_xn, g + 1)
                    for k in range(KD):
                        if not first:
                            pe.wait_ge(a_v, (g - 1) * TB + (k + 3))
                        for t in range(TB):
                            ins = nc.tensor.transpose(bank[k][:, t * P:(t + 1) * P], xn[:, t, k * P:(k + 1) * P], ident)
                        ins.then_inc(p_x, 1)

                def project(dst_, t, bias, w_h, w_l):
                    nc.tensor.matmul(dst_, ones_r[:, :], bias[:, :], start=True, stop=False)
                    for k in range(KD):
                        ins = three(dst_, xh[:, k, t * P:(t + 1) * P], xl[:, k, t * P:(t + 1) * P], w_h[:, k, :], w_l[:, k, :],
                                    False, k == KD - 1)
                    return ins

                def queries(g):
                    pe.wait_ge(a_xt, g + 1)
                    for t in range(TB):
                        dst_ = bank[2][:, t * QK:(t + 1) * QK]
                        nc.tensor.matmul(dst_, ones_f, qb_f[:, :], start=True, stop=False)
                        for k in range(KD):
                            ins = nc.tensor.matmul(dst_, xta[:, k, t * P:(t + 1) * P], wq[:, k, :], start=False,
                                                   stop=(k == KD - 1))
                    ins.then_inc(p_u, 1)

                def weigh(g):
                    pe.wait_ge(d_at, g + 1)
                    for c in range(KH):
                        if c == 1:
                            pe.wait_ge(d_lql, g + 1)
                        for t in range(TB):
                            ins = nc.tensor.matmul(bank[QO_BANK[c]][:, t * P:(t + 1) * P], vt[:, t, c * P:(c + 1) * P],
                                                   at[:, t * P:(t + 1) * P], start=True, stop=True)
                        ins.then_inc(p_qo, 1)

                def add_kv(g, t):
                    pe.wait_ge(d_vl, g * TB + (t + 1))
                    three(bank[7][:, :], pbh[:, t, :], pbl[:, t, :], vh[:, t, :], vl[:, t, :], False, False, True) \
                        .then_inc(p_kv, 1)

                nc.tensor.matmul(bank[7][:, :], zero[:, 0:P], zero[:, 0:H], start=True, stop=True, skip_group_check=True)
                turn_x(b * NB, True)
                queries(b * NB)

                def body(g, m, has_prev, ahead):
                    pe.wait_ge(a_u, g + 1)
                    if has_prev:
                        weigh(g - 1)
                    pe.wait_ge(d_xl, g * KD + KD)
                    for t in range(TB):
                        if t >= 2:
                            pe.wait_ge(a_v, g * TB + (t - 1))
                        project(bank[t % 2][:, :], t, vb_r, wvh, wvl).then_inc(p_v, 1)
                    pe.wait_ge(d_head, g + 1)
                    for h, (bk, done) in enumerate(((3, p_ta), (4, p_tb))):
                        if has_prev:
                            pe.wait_ge(a_qo, (g - 1) * KH + (h + 2))
                        for t in range(TB):
                            ins = nc.tensor.transpose(bank[bk][:, t * P:(t + 1) * P],
                                                      hr[:, t, 2 * h:2 * h + 2, :].rearrange("p h d -> p (h d)"), ident)
                        ins.then_inc(done, 1)
                    pe.wait_ge(d_pbl, g + 1)
                    add_kv(g, 0)
                    add_kv(g, 1)
                    pe.wait_ge(d_tab, g + 1)
                    for t in range(TB):
                        ins = nc.tensor.matmul(bank[5][:, t * P:(t + 1) * P], kkt[:, t * P:(t + 1) * P],
                                               qqt[:, t * P:(t + 1) * P], start=True, stop=True)
                    ins.then_inc(p_s, 1)
                    if ahead >= 1:
                        turn_x(g + 1, False)
                    add_kv(g, 2)
                    add_kv(g, 3)
                    if ahead >= 1:
                        if has_prev:
                            pe.wait_ge(a_qo, g * KH)
                        queries(g + 1)

                blocks_a(pe, b, body)
                weigh(b * NB + (NB - 1))

            def pass_b(b):
                def mix(g, c, m, has_prev):
                    if c == 0:
                        pe.wait_ge(ld_xh, g * 32 + 32)
                    if has_prev or c >= 2:
                        pe.wait_ge(a_gs, g * KH + (c - 1))
                    for k in range(KD):
                        ins = three(bank[c % 2][:, :], wgh[:, k, c * P:(c + 1) * P], wgl[:, k, c * P:(c + 1) * P],
                                    xh[:, k, :], xl[:, k, :], k == 0, k == KD - 1)
                    ins.then_inc(p_g, 1)
                    if has_prev or c >= 2:
                        pe.wait_ge(d_mix, g * KH + (c - 1))
                    three(bank[2 + c % 2][:, :], kvh[:, c * P:(c + 1) * P], kvl[:, c * P:(c + 1) * P],
                          lqh[:, cols(m)], lql[:, cols(m)],
                          True, True).then_inc(p_lo, 1)

                def turn_xf(g, has_prev):
                    pe.wait_ge(a_n3, g + 1)
                    if has_prev:
                        pe.wait_ge(d_lg, g)
                        pe.wait_ge(d_rec, g)
                    for k in range(KD):
                        for t in range(TB):
                            ins = nc.tensor.transpose(bank[6 + k][:, t * P:(t + 1) * P], xfb[:, t, k * P:(k + 1) * P], ident)
                        ins.then_inc(p_xt, 1)

                def logits(g):
                    pe.wait_ge(a_xft, g * KD + KD)
                    for t in range(TB):
                        for k in range(KD):
                            ins = nc.tensor.matmul(bank[6][:, t * E:(t + 1) * E], xft[:, k, t * P:(t + 1) * P], wr[:, k, :],
                                                   start=(k == 0), stop=(k == KD - 1))
                    ins.then_inc(p_lg, 1)

                def wo_(g, has_prev):
                    pe.wait_ge(d_og, g * KH + KH)
                    if has_prev:
                        pe.wait_ge(a_yo, g * 2)
                    for t in range(TB):
                        dst_ = bank[4 + t // 2][:, (t % 2) * D:(t % 2 + 1) * D]
                        nc.tensor.matmul(dst_, ones_r[:, :], ob_r[:, :], start=True, stop=False)
                        for k in range(KH):
                            ins = nc.tensor.matmul(dst_, og[:, k, t * P:(t + 1) * P], wo[:, k, :], start=False,
                                                   stop=(k == KH - 1))
                        if t % 2:
                            ins.then_inc(p_wo, 1)

                def count(g):
                    pe.wait_ge(d_hit, g + 1)
                    for t in range(TB):
                        dst_ = bank[7][:, t * E:(t + 1) * E]
                        nc.tensor.matmul(dst_, ones_b[:, :], hit_was[:, :], start=True, stop=False)
                        for s in range(t):
                            nc.tensor.matmul(dst_, ones_b[:, :], hit[:, s, :], start=False, stop=False)
                        ins = nc.tensor.matmul(dst_, tri[:, :], hit[:, t, :], start=False, stop=True)
                    ins.then_inc(p_cs, 1)

                def body(g, m, on):
                    if on[0]:
                        for c in range(KH):
                            mix(g, c, m, on[1])
                        wo_(g, on[1])
                    if on[2]:
                        turn_xf(g - 2, on[3])
                        logits(g - 2)
                    if on[3]:
                        count(g - 3)

                blocks_b(pe, b, body)

            attention(pe, "pe", pass_a, pass_b)
            meet(pe, "pe", 6)

            def turn_e(n, q, src, arrived):
                arrived()
                for k in range(KD):
                    for t in range(CH):
                        ins = nc.tensor.transpose(bank[q][:, (k * CH + t) * P:(k * CH + t + 1) * P],
                                                  src[:, t, k * P:(k + 1) * P], ident)
                ins.then_inc(p_et, 1)

            def up(n, q, wq, e, first):
                pe.wait_ge(d_el, n + 1)
                if not first:
                    pe.wait_ge(d_hf, n - 1)
                for j in range(2):
                    for c in range(KD):
                        for k in range(KD):
                            ins = three(bank[2 + 2 * j + q][:, c * CH * P:(c + 1) * CH * P],
                                        wh[wq][:, j, k, c * P:(c + 1) * P], wl[wq][:, j, k, c * P:(c + 1) * P],
                                        eh[q][:, k, :], el[q][:, k, :], k == 0, k == KD - 1)
                ins.then_inc(p_up, 1)

            def down(n, q, wq, free):
                pe.wait_ge(d_hl, n + 1)
                free()
                for t in range(CH):
                    for k in range(KD):
                        ins = three(bank[6 + q][:, t * D:(t + 1) * D], hh[q][:, k, t * P:(t + 1) * P],
                                    hl[q][:, k, t * P:(t + 1) * P], wh[wq][:, 2, k, :], wl[wq][:, 2, k, :],
                                    k == 0, k == KD - 1)
                ins.then_inc(p_dn, 1)

            def turn_g(c, i, first):
                i, c = (i + 1, c - 2 * NCH) if c >= 2 * NCH else (i, c)
                n = i * (2 * NCH) + c

                def arrived():
                    pe.wait_ge(ld_xg[c % NXB], (i * 2 + (c // NXB + 1)) * (16 * CH))
                    if not first:
                        pe.wait_ge(d_el, n - 1)

                turn_e(n, c % 2, xg[c % NXB], arrived)

            turn_g(0, 0, True)

            def pair(i, first, last):
                for c in range(2 * NCH):
                    n = i * (2 * NCH) + c
                    if not (last and c == 2 * NCH - 1):
                        turn_g(c + 1, i, first and c + 1 < 2)
                    if c % NCH == 0:
                        pe.wait_ge(d_wl, i * 2 + (c // NCH + 1))
                    up(n, c % 2, c // NCH, None, first and c < 2)
                    if c > 0:
                        m = c - 1
                        down(n - 1, m % 2, m // NCH, lambda: None if first and m < 2 else pe.wait_ge(a_eo, n - 2))
                m = 2 * NCH - 1
                n = i * (2 * NCH) + m
                down(n, m % 2, m // NCH, lambda: pe.wait_ge(a_eo, n - 1))

            pair(0, True, False)
            with pe.Fori(1, E // 2 - 1) as i:
                pair(i, False, False)
            pair(E // 2 - 1, False, True)
            meet(pe, "pe", 7)

            NC, N0 = NT // (CH * P), E * NCH

            def turn_c(n, q, i):
                def arrived():
                    pe.wait_ge(ld_c[q], i * 16 + 16)
                    pe.wait_ge(d_el, n + (N0 - 1))

                turn_e(n + N0, q % 2, xg[q], arrived)

            turn_c(0, 0, 0)
            pe.wait_ge(d_wl, E + 1)

            def group(i, first, last):
                for q in range(GC):
                    n = i * GC + q
                    if not (last and q == GC - 1):
                        turn_c(n + 1, (q + 1) % GC, i + (q + 1) // GC)
                    up(n + N0, q % 2, 0, None, False)
                    if not (first and q == 0):
                        down(n + (N0 - 1), 1 - q % 2, 0, lambda: None if first and q < 3 else pe.wait_ge(d_acc, n - 2))

            group(0, True, False)
            with pe.Fori(1, NC // GC - 1) as i:
                group(i, False, False)
            group(NC // GC - 1, False, True)
            down(N0 + NC - 1, 1, 0, lambda: pe.wait_ge(d_acc, NC - 2))


_OUT = (2, 4096, 256)


def kernel(L0_attn_x, L0_attn_ln1_w, L0_attn_ln1_b, L0_attn_Wqk, L0_attn_bqk, L0_attn_Wv, L0_attn_bv, L0_attn_Wg,
           L0_attn_bg, L0_attn_Wo, L0_attn_bo, L0_attn_ln2_w, L0_attn_ln2_b, L0_attn_gamma, L0_attn_beta,
           L0_attn_pos_emb, L0_ffn_wg, L0_ffn_w1, L0_ffn_w2, L0_ffn_w3, L0_ffn_sw1, L0_ffn_sw2, L0_ffn_sw3):
    import numpy as np
    import concourse.bacc as bacc
    from concourse import mybir
    from concourse.bass_utils import run_bass_kernel_spmd

    def rows(a):
        return np.ascontiguousarray(a)

    def columns(a):
        return rows(np.asarray(a).reshape(-1, 128).T)

    n, half = 4096, 32
    inv_freq = np.power(np.float32(10000.0), -(np.arange(half, dtype=np.float32) / np.float32(half)))
    angle = np.arange(n, dtype=np.float32)[:, None] * inv_freq[None, :]
    rope = np.stack([np.cos(angle), np.sin(angle)]).reshape(2, n // 128, 128, half).transpose(0, 2, 1, 3)
    p = np.arange(128)
    ident = np.eye(128, dtype=np.float32)
    before = (p[:, None] < p[None, :]).astype(np.float32)
    off_block = np.where(p[:, None] // 64 == p[None, :] // 64, 0.0, -1e30).astype(np.float32)
    experts = np.broadcast_to(np.arange(32, dtype=np.float32), (128, 32))
    tok = np.arange(4)[None, :, None] * 128 + p[:, None, None] + np.zeros((1, 1, 4), np.int64)
    token_ids = np.stack([tok, tok * 4 + np.arange(4)], -1).reshape(128, 32).astype(np.int32)

    arrays = {
        "x": rows(np.asarray(L0_attn_x).reshape(8192, 256)),
        "wqk_t": rows(np.asarray(L0_attn_Wqk).T), "wv_t": rows(np.asarray(L0_attn_Wv).T),
        "wg_t": rows(np.asarray(L0_attn_Wg).T), "wo_t": rows(np.asarray(L0_attn_Wo).T),
        "ln1_w": columns(L0_attn_ln1_w), "ln1_b": columns(L0_attn_ln1_b),
        "bqk": rows(L0_attn_bqk), "bg": columns(L0_attn_bg),
        "bv": rows(L0_attn_bv), "bo": rows(L0_attn_bo),
        "ln2_w": rows(L0_attn_ln2_w), "ln2_b": rows(L0_attn_ln2_b),
        "gamma": rows(np.asarray(L0_attn_gamma).reshape(-1)), "beta": rows(np.asarray(L0_attn_beta).reshape(-1)), "pos_emb": rows(L0_attn_pos_emb),
        "rope": rows(rope), "consts": rows(np.concatenate([ident, before, off_block, experts], 1)),
        "token_ids": token_ids, "route_t": rows(np.asarray(L0_ffn_wg).T),
        "w1": rows(L0_ffn_w1), "w2": rows(L0_ffn_w2), "w3": rows(L0_ffn_w3),
        "sw1": rows(L0_ffn_sw1), "sw2": rows(L0_ffn_sw2), "sw3": rows(L0_ffn_sw3),
    }
    nc = bacc.Bacc("TRN2", target_bir_lowering=False, num_devices=1)
    args = {k: nc.dram_tensor("in_" + k, a.shape, mybir.dt.from_np(a.dtype), kind="ExternalInput").ap()
            for k, a in arrays.items()}
    args["out"] = nc.dram_tensor("out", (8192, 256), mybir.dt.float32, kind="ExternalOutput").ap()
    build_program(nc, **args)
    r = run_bass_kernel_spmd(nc, [{"in_" + k: a for k, a in arrays.items()}], core_ids=[0])
    return r.results[0]["out"].reshape(_OUT)
```

```python
import concourse.bass as bass
from concourse import mybir
from contextlib import ExitStack

P = 128
EPS = 1e-5


def build_program(nc, x, wqk_t, wv_t, wg_t, wo_t, ln1_w, ln1_b, bqk, bg, bv, bo, ln2_w, ln2_b,
                  gamma, beta, pos_emb, rope, consts, token_ids, route_t, w1, w2, w3, sw1, sw2, sw3, out):
    F32, F32R, I32, U32, BF16 = (mybir.dt.float32, mybir.dt.float32r, mybir.dt.int32,
                                 mybir.dt.uint32, mybir.dt.bfloat16)
    ALU, ACT = mybir.AluOpType, mybir.ActivationFunctionType
    AX = mybir.AxisListType.X

    NT, D = x.shape
    NBATCH = 2
    S = NT // NBATCH
    H = wv_t.shape[1]
    QK = wqk_t.shape[1]
    HALF = QK // 2
    BLK = 512
    TB = BLK // P
    NB = S // BLK
    KD, KH = D // P, H // P
    E = w1.shape[0]
    TOPK = 4
    GRP, EG = 8, E // 8
    CAP = max(1, int(1.25 * NT * TOPK / E))
    ST = CAP // P
    CH = 2
    NCH = ST // CH
    NSLOT = E * CAP
    NROW = NT * TOPK
    REC = 3
    FAR = 1 << 20
    G64 = 64
    ZW = 512
    NPOS = pos_emb.shape[0]
    MAXREL = (NPOS - 1) // 2
    NBLK = NBATCH * NB

    def dram(name, shape, dt):
        return nc.dram_tensor(name, shape, dt).ap()

    xh_d, xl_d = dram("xh_d", [NBLK, P, KD * BLK], F32R), dram("xl_d", [NBLK, P, KD * BLK], F32R)
    x2_d = dram("x2_d", [NT, D], F32)
    xf_d = dram("xf_d", [NT + P, D], F32)
    slot_d = dram("slot_d", [NSLOT, REC], I32)
    y4_d = dram("y4_d", [NROW, D], F32)
    toep_d = dram("toep_d", [G64 * 2 * G64], F32)

    ctx = ExitStack()
    with ctx:
        def sb(name, shape, dt, c=ctx):
            return c.enter_context(nc.sbuf_tensor(name, shape, dt))

        def sem(name):
            return ctx.enter_context(nc.semaphore(name))

        cst = sb("cst", [P, consts.shape[1]], F32)
        ident = cst[:, 0:P]
        off_block = cst[:, 2 * P:3 * P]
        iota_e = cst[:, 3 * P:3 * P + E]
        eps = sb("eps", [P, 2], F32)
        gate_cell = sb("gate_cell", [P, 1], F32)
        rec, dsti = sb("rec", [P, TB * TOPK, REC], I32), sb("dsti", [P, TB * TOPK], I32)

        cA = ExitStack()
        tri = sb("tri", [P, P], BF16, cA)
        ones_b = sb("ones_b", [P, P], BF16, cA)
        tok_id = sb("tok_id", [P, TB * TOPK * 2], I32, cA)
        zero = sb("zero", [P, ZW], F32, cA)
        kvh, kvl = sb("kvh", [P, H], F32R, cA), sb("kvl", [P, H], F32R, cA)
        bias_s = sb("bias_s", [P, P], F32, cA)
        wq = sb("wq", [P, KD, QK], F32, cA)
        wvh, wvl, wgh, wgl = (sb(n, [P, KD, H], F32R, cA) for n in ("wvh", "wvl", "wgh", "wgl"))
        wo = sb("wo", [P, KH, D], F32, cA)
        wr = sb("wr", [P, KD, E], F32, cA)
        ones_r = sb("ones_r", [P, P], F32R, cA)
        qb_f = sb("qb_f", [P, QK], F32, cA)
        vb_r = sb("vb_r", [P, H], F32R, cA)
        ob_r = sb("ob_r", [P, D], F32R, cA)
        ones_f = ones_r[:, :].bitcast(F32)
        gb = sb("gb", [P, KH], F32, cA)
        gam, bet = sb("gam", [P, 4 * QK], F32, cA), sb("bet", [P, 4 * QK], F32, cA)
        cos, sin = sb("cos", [P, S // P, HALF], F32, cA), sb("sin", [P, S // P, HALF], F32, cA)
        qo_all = sb("qo_all", [P, KH, S], F32, cA)
        lqh, lql = sb("lqh", [P, S], F32R, cA), sb("lql", [P, S], F32R, cA)
        xh, xl = sb("xh", [P, KD, BLK], F32R, cA), sb("xl", [P, KD, BLK], F32R, cA)
        hit_all, hit_was = sb("hit_all", [P, E], F32, cA), sb("hit_was", [P, E], BF16, cA)
        base_f = sb("base_f", [P, TB * TOPK * 2], F32, cA)

        c0 = ExitStack()
        wraw = sb("wraw", [P, 2, KD, H], F32, c0)
        wscl = sb("wscl", [P, KD, H], F32, c0)
        qraw = sb("qraw", [P, KD, QK], F32, c0)
        l1w, l1b = sb("l1w", [P, KD], F32, c0), sb("l1b", [P, KD], F32, c0)
        bmat = sb("bmat", [P, KD, P], F32, c0)
        vb, vbh, vbl = sb("vb", [P, H], F32, c0), sb("vbh", [P, H], F32R, c0), sb("vbl", [P, H], F32R, c0)
        ob, obh, obl = sb("ob", [P, D], F32, c0), sb("obh", [P, D], F32R, c0), sb("obl", [P, D], F32R, c0)
        qb = sb("qb", [P, QK], F32, c0)
        gbi = sb("gbi", [P, KH], F32, c0)
        pe_row = sb("pe_row", [G64, NPOS], F32, c0)
        ext = sb("ext", [G64, 2 * G64], F32, c0)
        toep = sb("toep", [P, P], F32, c0)
        free_rec = sb("free_rec", [P, NSLOT * REC // P], I32, c0)
        c0.close()

        c1 = ExitStack()
        xa = sb("xa", [P, TB, D], F32, c1)
        xn = sb("xn", [P, TB, D], F32, c1)
        xta = sb("xta", [P, KD, BLK], F32, c1)
        u = sb("u", [P, TB, QK], F32, c1)
        hd = sb("hd", [P, TB, 4, QK], F32, c1)
        prod = [sb(f"prod{i}", [P, TB, 4, HALF], F32, c1) for i in range(2)]
        hr = sb("hr", [P, TB, 4, QK], F32, c1)
        pbh, pbl = sb("pbh", [P, TB, 2 * QK], F32R, c1), sb("pbl", [P, TB, 2 * QK], F32R, c1)
        qqt, kkt = sb("qqt", [QK, BLK], F32, c1), sb("kkt", [QK, BLK], F32, c1)
        vt = sb("vt", [P, TB, H], F32, c1)
        vh, vl = sb("vh", [P, TB, H], F32R, c1), sb("vl", [P, TB, H], F32R, c1)
        at = sb("at", [P, BLK], F32, c1)
        st_a = sb("st_a", [P, TB, 6], F32, c1)
        mv_a = sb("mv_a", [P, TB, 2], F32, c1)
        sd_a, rs_a, nm_a = (sb(n, [P, TB], F32, c1) for n in ("sd_a", "rs_a", "nm_a"))
        c1.close()

        c2 = ExitStack()
        w2b, b2b = sb("w2b", [P, D], F32, c2), sb("b2b", [P, D], F32, c2)
        xb = sb("xb", [P, TB, D], F32, c2)
        gsb = [sb(f"gsb{i}", [P, BLK], F32, c2) for i in range(2)]
        mixed = sb("mixed", [P, BLK], F32, c2)
        og = sb("og", [P, KH, BLK], F32, c2)
        yo = sb("yo", [P, TB, D], F32, c2)
        yb, yn = sb("yb", [P, TB, D], F32, c2), sb("yn", [P, TB, D], F32, c2)
        x2b = sb("x2b", [P, TB, D], F32, c2)
        xfb = sb("xfb", [P, TB, D], F32, c2)
        xft = sb("xft", [P, KD, BLK], F32, c2)
        st_1, st_2, st_3 = (sb(n, [P, TB, 6], F32, c2) for n in ("st_1", "st_2", "st_3"))
        mv_b = sb("mv_b", [P, 3 * TB, 2], F32, c2)
        sd_b, rs_b, nm_b = (sb(n, [P, 3 * TB], F32, c2) for n in ("sd_b", "rs_b", "nm_b"))
        lg = sb("lg", [P, TB, E], F32, c2)
        pr = sb("pr", [P, TB, E], F32, c2)
        mx, sm, rsm = (sb(n, [P, TB], F32, c2) for n in ("mx", "sm", "rsm"))
        gs = sb("gs", [P, TB, GRP], F32, c2)
        top_g, top_e = sb("top_g", [P, TB, 8], F32, c2), sb("top_e", [P, TB, 8], F32, c2)
        ix_g, ix_e = sb("ix_g", [P, TB, 8], U32, c2), sb("ix_e", [P, TB, 8], U32, c2)
        fx_g, fx_e = sb("fx_g", [P, TB, 8], F32, c2), sb("fx_e", [P, TB, 8], F32, c2)
        eq_g = sb("eq_g", [P, TB, TOPK, GRP], F32, c2)
        keep, kneg = sb("keep", [P, TB, GRP], F32, c2), sb("kneg", [P, TB, GRP], F32, c2)
        msk = sb("msk", [P, TB, E], F32, c2)
        oh = sb("oh", [P, TB, TOPK, E], F32, c2)
        ohp = sb("ohp", [P, TB, TOPK, E], F32, c2)
        hit = sb("hit", [P, TB, E], BF16, c2)
        hsum = sb("hsum", [P, E], F32, c2)
        wsum, wrec = sb("wsum", [P, TB], F32, c2), sb("wrec", [P, TB], F32, c2)
        pos, dst, over = (sb(n, [P, TB, TOPK], F32, c2) for n in ("pos", "dst", "over"))
        c2.close()
        cA.close()

        c3 = ExitStack()
        NXB = 5
        wld = sb("wld", [P, 3, KD, D], F32, c3)
        wh = [sb(f"wh{i}", [P, 3, KD, D], F32R, c3) for i in range(2)]
        wl = [sb(f"wl{i}", [P, 3, KD, D], F32R, c3) for i in range(2)]
        gix = [sb(f"gix{i}", [P, ST, REC], I32, c3) for i in range(2)]
        six = [sb(f"six{i}", [P, ST, REC], I32, c3) for i in range(2)]
        xg = [sb(f"xg{i}", [P, CH, D], F32, c3) for i in range(NXB)]
        eh = [sb(f"eh{i}", [P, KD, CH * P], F32R, c3) for i in range(2)]
        el = [sb(f"el{i}", [P, KD, CH * P], F32R, c3) for i in range(2)]
        sa = [sb(f"sa{i}", [P, KD, CH * P], F32, c3) for i in range(2)]
        hf = [sb(f"hf{i}", [P, KD, CH * P], F32, c3) for i in range(2)]
        hh = [sb(f"hh{i}", [P, KD, CH * P], F32R, c3) for i in range(2)]
        hl = [sb(f"hl{i}", [P, KD, CH * P], F32R, c3) for i in range(2)]
        sx = [sb(f"sx{i}", [P, CH, REC], I32, c3) for i in range(NXB)]
        eo = [sb(f"eo{i}", [P, CH, D], F32, c3) for i in range(NXB)]
        GC = 4
        y4 = [sb(f"y4{i}", [P, CH, TOPK, D], F32, c3) for i in range(GC)]
        xr = [sb(f"xr{i}", [P, CH, D], F32, c3) for i in range(GC)]
        ysum = [sb(f"ysum{i}", [P, CH, 2, D], F32, c3) for i in range(2)]
        ytot = [sb(f"ytot{i}", [P, CH, D], F32, c3) for i in range(GC)]
        yout = [sb(f"yout{i}", [P, CH, D], F32, c3) for i in range(GC)]
        st_c = sb("st_c", [P, CH, 6], F32, c3)
        mv_c = sb("mv_c", [P, GC * CH, 2], F32, c3)
        sd_c, rs_c, nm_c = (sb(n, [P, GC * CH], F32, c3) for n in ("sd_c", "rs_c", "nm_c"))
        c3.close()

        bank = [ctx.enter_context(nc.psum_tensor(f"bank{i}", [P, 512], F32)) for i in range(8)]

        s_load, s_loada, s_free, s_pos, s_ext, s_toep, s_tl, s_clear = (sem(n) for n in ("s_load", "s_loada", "s_free", "s_pos", "s_ext", "s_toep", "s_tl", "s_clear"))
        s_dve, s_act, s_pe, s_zero = sem("s_dve"), sem("s_act"), sem("s_pe"), sem("s_zero")
        ph = {n: sem(f"ph_{n}") for n in ("sp", "act", "dve", "pe", "pool")}
        past = {nc.sync: sem("past_sp"), nc.gpsimd: sem("past_pool")}
        ld_x, st_xh, st_xl, ld_xh = sem("ld_x"), sem("st_xh"), sem("st_xl"), sem("ld_xh")
        a_sd, a_xt, a_xh, a_u, a_ta, a_v, a_vh, a_pbh, a_qo, a_kvh = (sem(n) for n in (
            "a_sd", "a_xt", "a_xh", "a_u", "a_ta", "a_v", "a_vh", "a_pbh", "a_qo", "a_kvh"))
        d_stat, d_rs, d_xl, d_prod, d_head, d_pbl, d_vl, d_tab, d_at = (sem(n) for n in (
            "d_stat", "d_rs", "d_xl", "d_prod", "d_head", "d_pbl", "d_vl", "d_tab", "d_at"))
        g_xn, g_gam, g_hd, g_rec = sem("g_xn"), sem("g_gam"), sem("g_hd"), sem("g_rec")
        o_ln, o_rs, o_at, o_kv = sem("o_ln"), sem("o_rs"), sem("o_at"), sem("o_kv")
        p_x, p_u, p_v, p_ta, p_tb, p_kv, p_s, p_qo = (sem(n) for n in (
            "p_x", "p_u", "p_v", "p_ta", "p_tb", "p_kv", "p_s", "p_qo"))
        ld_w2, ld_xb, st_x2, st_xf, st_rec = sem("ld_w2"), sem("ld_xb"), sem("st_x2"), sem("st_xf"), sem("st_rec")
        g_w2 = sem("g_w2")
        a_gs, a_root, a_n1, a_n2, a_n3, a_yo, a_xft, a_exp = (sem(n) for n in (
            "a_gs", "a_root", "a_n1", "a_n2", "a_n3", "a_yo", "a_xft", "a_exp"))
        d_lql, d_mix, d_og, d_st1, d_st2, d_st3, d_inv, d_x2, d_lg, d_hit, d_rec = (sem(n) for n in (
            "d_lql", "d_mix", "d_og", "d_st1", "d_st2", "d_st3", "d_inv", "d_x2", "d_lg", "d_hit", "d_rec"))
        o_s1, o_s2, o_s3, o_inv, o_wb, o_rt, o_fin = (sem(n) for n in (
            "o_s1", "o_s2", "o_s3", "o_inv", "o_wb", "o_rt", "o_fin"))
        p_g, p_lo, p_wo, p_xt, p_lg, p_cs = (sem(n) for n in ("p_g", "p_lo", "p_wo", "p_xt", "p_lg", "p_cs"))
        ld_w, ld_gix, ld_six = sem("ld_w"), [sem("ld_gix0"), sem("ld_gix1")], [sem("ld_six0"), sem("ld_six1")]
        ld_xg = [sem(f"ld_xg{i}") for i in range(NXB)]
        st_eo = [sem(f"st_eo{i}") for i in range(NXB)]
        a_wh, a_eh, a_sa, a_hh, a_eo = (sem(n) for n in ("a_wh", "a_eh", "a_sa", "a_hh", "a_eo"))
        d_wl, d_el, d_hf, d_hl, d_sx = (sem(n) for n in ("d_wl", "d_el", "d_hf", "d_hl", "d_sx"))
        p_et, p_up, p_dn = sem("p_et"), sem("p_up"), sem("p_dn")
        ld_c, ld_y, ld_r, st_out = ([sem(f"{n}{i}") for i in range(GC)] for n in ("ld_c", "ld_y", "ld_r", "st_out"))
        g_y2, g_ys, d_acc, d_cst, d_crs, d_out = (sem(n) for n in ("g_y2", "g_ys", "d_acc", "d_cst", "d_crs", "d_out"))
        a_csd, a_cn, o_c, o_cr = sem("a_csd"), sem("a_cn"), sem("o_c"), sem("o_cr")

        block = ctx.enter_context(nc.Block())

        class Own:

            def __init__(self, eng, s, base):
                self.eng, self.s, self.base, self.n = eng, s, base, 0

            def step(self, ins):
                self.n += 1
                ins.then_inc(self.s, 1)

            def wait(self):
                self.eng.wait_ge(self.s, self.base + self.n)

        def settled(eng):
            eng.sem_inc(past[eng], 1)

        def meet(eng, name, n):
            eng.drain().then_inc(ph[name], 1)
            for other in ph:
                if other != name:
                    eng.wait_ge(ph[other], n)
            if eng in past:
                settled(eng)

        def attention(eng, name, pass_a, pass_b):
            with eng.Fori(0, NBATCH) as b:
                pass_a(b)
                meet(eng, name, b * 2 + 2)
                pass_b(b)
                meet(eng, name, b * 2 + 3)

        LAG = 4
        PE_ADDS = (1, 3)

        def blocks_b(eng, b, body, split=False):
            def on(m):
                return [0 <= m - s < NB for s in range(LAG + 1)] + [m + 2 < NB]

            for m in range(LAG):
                body(b * NB + m, m, on(m))
            for lo, hi in ((LAG, NB - 2), (NB - 2, NB)) if split else ((LAG, NB),):
                with eng.Fori(lo, hi) as m:
                    body(b * NB + m, m, on(lo))
            for m in range(NB, NB + LAG):
                body(b * NB + m, m, on(m))

        def blocks_a(eng, b, body):
            body(b * NB, 0, False, 2)
            with eng.Fori(1, NB - 2) as m:
                body(b * NB + m, m, True, 2)
            for m in (NB - 2, NB - 1):
                body(b * NB + m, m, True, NB - 1 - m)

        def cols(m):
            return bass.ds(m * BLK, BLK)

        QO_BANK = (6, 3, 4, 2)

        @block.sync
        def _(sp):
            sp.dma_start(pe_row[:, :], pos_emb.partition_broadcast(G64)).then_inc(s_pos, 16)
            for dst_, src in (
                (l1w[:, :], ln1_w), (l1b[:, :], ln1_b),
                (wraw[:, 0], wv_t.rearrange("(k p) n -> p k n", p=P)),
                (wraw[:, 1], wg_t.rearrange("(k p) n -> p k n", p=P)),
                (gbi[:, :], bg), (vb[:, :], bv.partition_broadcast(P)), (ob[:, :], bo.partition_broadcast(P)),
                (cst[:, :], consts),
            ):
                sp.dma_start(dst_, src).then_inc(s_load, 16)
            sp.wait_ge(s_zero, 4)
            sp.dma_start(slot_d.rearrange("(p s) r -> p (s r)", p=P), free_rec[:, :]).then_inc(s_free, 16)
            sp.dma_start(xf_d[NT:NT + P, :], zero[:, 0:D]).then_inc(s_free, 16)
            sp.wait_ge(s_ext, 5)
            W = 2 * G64 - 1
            sp.dma_start(toep_d[0:G64 * W].rearrange("(a c) -> a c", c=W), ext[:, 0:W]).then_inc(s_toep, 16)
            sp.wait_ge(s_toep, 16)
            src = toep_d[G64 - 1:G64 - 1 + G64 * (W - 1)].rearrange("(a c) -> a c", c=W - 1)[:, 0:G64]
            for q in range(2):
                sp.dma_start(toep[q * G64:(q + 1) * G64, q * G64:(q + 1) * G64], src).then_inc(s_tl, 16)
            sp.wait_ge(s_free, 32)
            for s in st_out:
                sp.sem_inc(s, 16)
            meet(sp, "sp", 1)

            y4_rows = y4_d.rearrange("(n p r) d -> n p (r d)", p=P, r=ZW // D)
            clears = y4_rows.shape[0] // NBLK

            def load_x(dst_, g, done):
                sp.dma_start(dst_[:, :, :], x[bass.ds(g * BLK, BLK), :].rearrange("(t p) d -> p t d", p=P)) \
                  .then_inc(done, 16)

            def pass_a(b):
                def next_x(g):
                    sp.wait_ge(g_xn, g)
                    load_x(xa, g, ld_x)

                def store_parts(g):
                    sp.wait_ge(a_xh, g * KD + KD)
                    sp.dma_start(xh_d[g, :, :].bitcast(F32), xh[:, :, :].bitcast(F32)).then_inc(st_xh, 16)
                    sp.wait_ge(d_xl, g * KD + KD)
                    sp.dma_start(xl_d[g, :, :].bitcast(F32), xl[:, :, :].bitcast(F32)).then_inc(st_xl, 16)

                load_x(xa, b * NB, ld_x)
                next_x(b * NB + 1)
                store_parts(b * NB)

                def body(g, m, has_prev, ahead):
                    if ahead >= 2:
                        next_x(g + 2)
                    if ahead >= 1:
                        store_parts(g + 1)
                    for n in range(clears):
                        sp.dma_start(y4_rows[g * clears + n, :, :], zero[:, :]).then_inc(s_clear, 16)

                blocks_a(sp, b, body)
                for s in (st_xh, st_xl):
                    sp.wait_ge(s, (b + 1) * (16 * NB))
                settled(sp)

            def pass_b(b):
                def rows_of(t, g):
                    return t[bass.ds(g * BLK, BLK), :].rearrange("(t p) d -> p t d", p=P)

                load_x(xb, b * NB, ld_xb)
                sp.dma_start(w2b[:, :], ln2_w.partition_broadcast(P)).then_inc(ld_w2, 16)
                sp.dma_start(b2b[:, :], ln2_b.partition_broadcast(P)).then_inc(ld_w2, 16)

                def body(g, m, on):
                    if on[3]:
                        sp.wait_ge(a_n3, g - 2)
                        sp.dma_start(rows_of(xf_d, g - 3), xfb[:, :, :]).then_inc(st_xf, 16)
                    if on[2]:
                        sp.wait_ge(d_x2, g - 1)
                        sp.dma_start(rows_of(x2_d, g - 2), x2b[:, :, :]).then_inc(st_x2, 16)
                        if on[1]:
                            load_x(xb, g - 1, ld_xb)

                blocks_b(sp, b, body)
                for s in (st_x2, st_xf):
                    sp.wait_ge(s, (b + 1) * (16 * NB))
                settled(sp)

            attention(sp, "sp", pass_a, pass_b)
            def load_w(e):
                for j, w in enumerate((w1, w3, w2)):
                    sp.dma_start(wld[:, j], w[e, :, :].rearrange("(k p) n -> p k n", p=P)).then_inc(ld_w, 16)

            load_w(0)
            sp.wait_ge(s_clear, 16 * clears * NBLK)
            meet(sp, "sp", 6)

            slots = slot_d.rearrange("(e p s) r -> e p (s r)", p=P, s=ST)

            def load_gix(e, q):
                sp.dma_start(gix[q][:, :, :], slots[e, :, :]).then_inc(ld_gix[q], 16)

            def load_six(e, q):
                sp.dma_start(six[q][:, :, :], slots[e, :, :]).then_inc(ld_six[q], 16)

            load_gix(0, 0)
            load_six(0, 0)

            def pair(i, first, last):
                for q in range(2):
                    e = i * 2 + q
                    if last and q == 1:
                        sp.wait_ge(d_wl, e + 1)
                        for j, w in enumerate((sw1, sw3, sw2)):
                            sp.dma_start(wld[:, j], w.rearrange("(k p) n -> p k n", p=P)).then_inc(ld_w, 16)
                        continue
                    if not (first and q == 0):
                        sp.wait_ge(p_et, e * NCH)
                    load_gix(e + 1, 1 - q)
                    sp.wait_ge(d_wl, e + 1)
                    load_w(e + 1)
                    if not (first and q == 0):
                        sp.wait_ge(d_sx, e * NCH)
                    load_six(e + 1, 1 - q)

            pair(0, True, False)
            with sp.Fori(1, E // 2 - 1) as i:
                pair(i, False, False)
            pair(E // 2 - 1, False, True)

            NC = NT // (CH * P)

            def load_c(n, q):
                sp.dma_start(xg[q][:, :, :], xf_d[bass.ds(n * CH * P, CH * P), :].rearrange("(p t) d -> p t d", t=CH)) \
                  .then_inc(ld_c[q], 16)

            def load_y(n, q):
                sp.dma_start(y4[q][:, :, :, :], y4_d[bass.ds(n * CH * P * TOPK, CH * P * TOPK), :]
                             .rearrange("(p t k) d -> p t k d", t=CH, k=TOPK)).then_inc(ld_y[q], 16)

            def load_r(n, q):
                sp.dma_start(xr[q][:, :, :], x2_d[bass.ds(n * CH * P, CH * P), :].rearrange("(p t) d -> p t d", t=CH)) \
                  .then_inc(ld_r[q], 16)

            def store(n, q):
                sp.wait_ge(d_out, n + 1)
                sp.dma_start(out[bass.ds(n * CH * P, CH * P), :].rearrange("(p t) d -> p t d", t=CH), yout[q][:, :, :]) \
                  .then_inc(st_out[q], 16)

            sp.wait_ge(p_et, E * NCH)
            for q in range(GC):
                load_c(q, q)
            for buf in range(NXB):
                sp.wait_ge(st_eo[buf], E * NCH // NXB * 16 * CH)
            for q in range(GC):
                load_y(q, q)

            def group(i, first, last):
                for q in range(GC):
                    n = i * GC + q
                    if not last:
                        sp.wait_ge(p_et, n + (E * NCH + 1))
                        load_c(n + GC, q)
                        sp.wait_ge(g_y2, n + 1)
                        load_y(n + GC, q)
                    if not first:
                        store(n - GC, q)
                    load_r(n, q)

            group(0, True, False)
            with sp.Fori(1, NC // GC - 1) as i:
                group(i, False, False)
            group(NC // GC - 1, False, True)
            for q in range(GC):
                store(NC - GC + q, q)
            for q in range(GC):
                sp.wait_ge(st_out[q], 16 * (NC // GC) + 16)

        @block.gpsimd
        def _(pool):
            nc.gpsimd.memset(zero[:, :], 0.0).then_inc(s_zero, 1)
            fr = free_rec[:, :].rearrange("p (s r) -> p s r", r=REC)
            nc.gpsimd.memset(fr[:, :, 0:1], NT).then_inc(s_zero, 1)
            nc.gpsimd.memset(fr[:, :, 1:2], FAR).then_inc(s_zero, 1)
            nc.gpsimd.memset(fr[:, :, 2:3], 0).then_inc(s_zero, 1)
            meet(pool, "pool", 1)

            def scatter(g, half):
                if half == 0:
                    pool.wait_ge(d_rec, g + 2)
                    settled(pool)
                HJ = TB * TOPK // 2
                for j in range(half * HJ, (half + 1) * HJ):
                    pool.indirect_dma_start(
                        slot_d, bass.IndirectOffsetOnAxis(ap=dsti[:, j:j + 1], axis=0), rec[:, j, :], None,
                        bounds_check=NSLOT - 1, oob_is_err=False).then_inc(st_rec, 16)
                if half == 1:
                    pool.wait_ge(st_rec, (g + 2) * (16 * TB * TOPK))
                    pool.sem_inc(g_rec, 1)

            def load_parts(g):
                pool.dma_start(xh[:, :, :], xh_d[g, :, :]).then_inc(ld_xh, 16)
                pool.dma_start(xl[:, :, :], xl_d[g, :, :]).then_inc(ld_xh, 16)

            def pass_a(b):
                def normalise(g, has_prev):
                    pool.wait_ge(d_rs, g + 1)
                    if has_prev:
                        pool.wait_ge(p_x, g * KD)
                    settled(pool)
                    for t in range(TB):
                        ins = nc.gpsimd.tensor_scalar(xn[:, t, :], xa[:, t, :], rs_a[:, t:t + 1], nm_a[:, t:t + 1],
                                                      ALU.mult, ALU.add)
                    ins.then_inc(g_xn, 1)

                def heads(g, has_prev):
                    pool.wait_ge(a_u, g + 1)
                    if has_prev:
                        pool.wait_ge(d_prod, g)
                    nc.gpsimd.tensor_tensor(hd[:, :, :, :], u[:, :, :].unsqueeze(2).to_broadcast([P, TB, 4, QK]),
                                            gam[:, :].rearrange("p (h d) -> p h d", h=4).unsqueeze(1)
                                            .to_broadcast([P, TB, 4, QK]), ALU.mult).then_inc(g_gam, 1)
                    pool.wait_ge(g_gam, g + 1)
                    h3 = hd[:, :, :, :].rearrange("p t h d -> p t (h d)")
                    nc.gpsimd.tensor_tensor(h3, h3, bet[:, :].unsqueeze(1).to_broadcast([P, TB, 4 * QK]), ALU.add) \
                        .then_inc(g_hd, 1)

                normalise(b * NB, False)

                heads(b * NB, False)

                def body(g, m, has_prev, ahead):
                    if ahead >= 1:
                        normalise(g + 1, True)
                        heads(g + 1, True)
                    if not has_prev:
                        scatter(b * NB - 1, 0)
                    if ahead == 0:
                        scatter(b * NB - 1, 1)

                blocks_a(pool, b, body)
                for s in (st_xh, st_xl):
                    pool.wait_ge(s, (b + 1) * (16 * NB))
                pool.wait_ge(p_v, (b + 1) * (NB * TB))
                settled(pool)
                load_parts(b * NB)

            def pass_b(b):
                def next_parts(g):
                    pool.wait_ge(p_g, g * KH)
                    settled(pool)
                    load_parts(g)

                def weigh_rows(g):
                    pool.wait_ge(ld_w2, b * 32 + 32)
                    pool.wait_ge(a_n1, g + 1)
                    nc.gpsimd.tensor_tensor(yb[:, :, :], yb[:, :, :], w2b[:, :].unsqueeze(1).to_broadcast([P, TB, D]),
                                            ALU.mult).then_inc(g_w2, 1)

                next_parts(b * NB + 1)

                def body(g, m, on):
                    if on[1]:
                        weigh_rows(g - 1)
                    scatters = on[4] and on[3]
                    if scatters:
                        scatter(g - 4, 0)
                    if on[-1]:
                        next_parts(g + 2)
                    if scatters:
                        scatter(g - 4, 1)

                blocks_b(pool, b, body, True)

            attention(pool, "pool", pass_a, pass_b)
            scatter(NBLK - 1, 0)
            scatter(NBLK - 1, 1)
            meet(pool, "pool", 6)

            def gather(c, i, first):
                i, c = (i + 1, c - 2 * NCH) if c >= 2 * NCH else (i, c)
                e, q, buf = i * 2 + c // NCH, c // NCH, c % NXB
                if c % NCH == 0:
                    pool.wait_ge(ld_gix[q], (i + 1) * 16)
                if not first:
                    pool.wait_ge(p_et, i * (2 * NCH) + (c - NXB + 1))
                settled(pool)
                for t in range(CH):
                    s = (c % NCH) * CH + t
                    pool.indirect_dma_start(xg[buf][:, t, :], None, xf_d,
                                            bass.IndirectOffsetOnAxis(ap=gix[q][:, s, 0:1], axis=0)) \
                        .then_inc(ld_xg[buf], 16)

            def put(c, i):
                buf = c % NXB
                pool.wait_ge(a_eo, i * (2 * NCH) + (c + 1))
                settled(pool)
                for t in range(CH):
                    pool.indirect_dma_start(y4_d, bass.IndirectOffsetOnAxis(ap=sx[buf][:, t, 1:2], axis=0),
                                            eo[buf][:, t, :], None, bounds_check=NROW - 1, oob_is_err=False) \
                        .then_inc(st_eo[buf], 16)

            AHEAD = 3
            for c in range(AHEAD):
                gather(c, 0, True)

            def pair(i, first, last):
                for c in range(2 * NCH):
                    if not (last and c + AHEAD >= 2 * NCH):
                        gather(c + AHEAD, i, first and c + AHEAD < NXB)
                    if c > 0:
                        put(c - 1, i)
                put(2 * NCH - 1, i)

            pair(0, True, False)
            with pool.Fori(1, E // 2 - 1) as i:
                pair(i, False, False)
            pair(E // 2 - 1, False, True)

            def add_rows(n, q, i, first):
                pool.wait_ge(ld_y[q], i * 16 + 16)
                if not first:
                    pool.wait_ge(d_acc, n - 1)
                nc.gpsimd.tensor_tensor(ysum[q % 2][:, :, :, :], y4[q][:, :, 0:2, :], y4[q][:, :, 2:4, :], ALU.add) \
                    .then_inc(g_y2, 1)
                pool.wait_ge(g_y2, n + 1)
                nc.gpsimd.tensor_tensor(ysum[q % 2][:, :, 0, :], ysum[q % 2][:, :, 0, :], ysum[q % 2][:, :, 1, :], ALU.add) \
                    .then_inc(g_ys, 1)

            def group(i, first):
                for q in range(GC):
                    add_rows(i * GC + q, q, i, first and q < 2)

            group(0, True)
            with pool.Fori(1, NT // (CH * P) // GC) as i:
                group(i, False)

        @block.scalar
        def _(act):
            for dst_, src in (
                (qraw[:, :, :], wqk_t.rearrange("(k p) n -> p k n", p=P)), (qb[:, :], bqk.partition_broadcast(P)),
                (wr[:, :, :], route_t.rearrange("(k p) n -> p k n", p=P)),
                (wo[:, :, :], wo_t.rearrange("(k p) n -> p k n", p=P)),
                (gam[:, :], gamma.partition_broadcast(P)), (bet[:, :], beta.partition_broadcast(P)),
                (cos[:, :, :], rope[0]), (sin[:, :, :], rope[1]), (tok_id[:, :], token_ids),
            ):
                act.dma_start(dst_, src).then_inc(s_loada, 16)
            for j, w in enumerate((wvh, wgh)):
                act.wait_ge(s_dve, 10 + 2 * j)
                nc.scalar.activation(w[:, :, :], wscl[:, :, :], ACT.Copy).then_inc(s_act, 1)
            act.wait_ge(s_dve, 17)
            nc.scalar.activation(vbh[:, :], vb[:, :], ACT.Copy).then_inc(s_act, 1)
            nc.scalar.activation(obh[:, :], ob[:, :], ACT.Copy).then_inc(s_act, 1)
            meet(act, "act", 1)

            def pass_a(b):
                def sqrt_x(g):
                    act.wait_ge(d_stat, g + 1)
                    nc.scalar.activation(sd_a[:, :], mv_a[:, :, 1], ACT.Sqrt, bias=eps[:, 1:2], scale=1.0 + EPS) \
                        .then_inc(a_sd, 1)

                def x_high(g, first):
                    for k in range(KD):
                        act.wait_ge(p_x, g * KD + (k + 1))
                        ins = nc.scalar.activation(xta[:, k, :], bank[k][:, :], ACT.Copy)
                    ins.then_inc(a_xt, 1)
                    if not first:
                        act.wait_ge(st_xh, g * 16)
                    for k in range(KD):
                        nc.scalar.activation(xh[:, k, :], bank[k][:, :], ACT.Copy).then_inc(a_xh, 1)

                def silu_u(g, first):
                    act.wait_ge(p_u, g + 1)
                    if not first:
                        act.wait_ge(g_gam, g)
                    nc.scalar.activation(u[:, :, :], bank[2][:, 0:TB * QK].rearrange("p (t d) -> p t d", t=TB),
                                         ACT.Silu).then_inc(a_u, 1)

                def values_out(g, m):
                    for c in range(KH):
                        act.wait_ge(p_qo, g * KH + (c + 1))
                        nc.scalar.activation(qo_all[:, c, cols(m)], bank[QO_BANK[c]][:, :], ACT.Copy).then_inc(a_qo, 1)

                sqrt_x(b * NB)
                x_high(b * NB, True)
                silu_u(b * NB, True)
                sqrt_x(b * NB + 1)

                def body(g, m, has_prev, ahead):
                    if has_prev:
                        values_out(g - 1, m - 1)
                    for t in range(TB):
                        act.wait_ge(p_v, g * TB + (t + 1))
                        nc.scalar.activation(vt[:, t, :], bank[t % 2][:, :], ACT.Silu).then_inc(a_v, 1)
                        act.wait_ge(a_v, g * TB + (t + 1))
                        nc.scalar.activation(vh[:, t, :], vt[:, t, :], ACT.Copy).then_inc(a_vh, 1)
                        if t == 1:
                            act.wait_ge(d_head, g + 1)
                            nc.scalar.activation(pbh[:, :, :], hr[:, :, 2:4, :].rearrange("p t h d -> p t (h d)"), ACT.Copy) \
                                .then_inc(a_pbh, 1)
                    act.wait_ge(p_ta, g + 1)
                    nc.scalar.activation(lqh[QK:2 * QK, cols(m)], bank[3][QK:2 * QK, :], ACT.Copy).then_inc(a_ta, 1)
                    if ahead >= 1:
                        x_high(g + 1, False)
                        silu_u(g + 1, False)
                    if ahead >= 2:
                        sqrt_x(g + 2)

                blocks_a(act, b, body)
                values_out(b * NB + (NB - 1), NB - 1)
                act.wait_ge(p_kv, (b + 1) * (NB * TB))
                nc.scalar.activation(kvh[QK:2 * QK, :], bank[7][QK:2 * QK, :], ACT.Copy, scale=1.0 / S).then_inc(a_kvh, 1)

            def pass_b(b):
                def gates(g, c, has_prev):
                    act.wait_ge(p_g, g * KH + (c + 1))
                    if c >= 2 or has_prev:
                        act.wait_ge(d_og, g * KH + (c - 1))
                    nc.scalar.activation(gsb[c % 2][:, :], bank[c % 2][:, :], ACT.Silu, bias=gb[:, c:c + 1]).then_inc(a_gs, 1)

                def norm(dst_, src, rs, nm, first, done):
                    for t in range(TB):
                        ins = nc.scalar.activation(dst_[:, t, :], src[:, t, :], ACT.Identity,
                                                   bias=nm[:, first + t:first + t + 1], scale=rs[:, first + t:first + t + 1])
                    ins.then_inc(done, 1)

                def roots(g, on):
                    if on[1]:
                        act.wait_ge(d_st1, g)
                    elif on[3]:
                        act.wait_ge(d_st3, g - 2)
                    nc.scalar.activation(sd_b[:, :], mv_b[:, :, 1], ACT.Sqrt, bias=eps[:, 0:1]).then_inc(a_root, 1)

                def turn(g, has_prev):
                    if has_prev:
                        act.wait_ge(p_lg, g)
                    for k in range(KD):
                        act.wait_ge(p_xt, g * KD + (k + 1))
                        nc.scalar.activation(xft[:, k, :], bank[6 + k][:, :], ACT.Copy).then_inc(a_xft, 1)

                def expo(g):
                    act.wait_ge(d_lg, g + 1)
                    nc.scalar.activation(pr[:, :, :], lg[:, :, :], ACT.Exp).then_inc(a_exp, 1)

                def body(g, m, on):
                    if on[0]:
                        for c in range(KH):
                            gates(g, c, on[1])
                    if on[4]:
                        expo(g - 4)
                    if on[1] or on[2] or on[3]:
                        roots(g, on)
                        act.wait_ge(d_inv, g + b * 2)
                    if on[3]:
                        if on[4]:
                            act.wait_ge(st_xf, (g - 3) * 16)
                            act.wait_ge(p_xt, (g - 3) * KD)
                        norm(xfb, x2b, rs_b, nm_b, 2 * TB, a_n3)
                    if on[2]:
                        if on[3]:
                            act.wait_ge(d_x2, g - 2)
                        norm(yn, yb, rs_b, nm_b, TB, a_n2)
                    if on[1]:
                        if on[2]:
                            act.wait_ge(a_n2, g - 1)
                        norm(yb, yo, rs_b, nm_b, 0, a_n1)
                    if on[3]:
                        turn(g - 3, on[4])
                    if on[0]:
                        if on[1]:
                            act.wait_ge(a_n1, g)
                        for h in range(2):
                            act.wait_ge(p_wo, g * 2 + (h + 1))
                            nc.scalar.activation(yo[:, 2 * h:2 * h + 2, :],
                                                 bank[4 + h][:, :].rearrange("p (t d) -> p t d", t=2), ACT.Copy) \
                                .then_inc(a_yo, 1)

                blocks_b(act, b, body)

            attention(act, "act", pass_a, pass_b)

            def split_w(e, q):
                act.wait_ge(ld_w, (e + 1) * 48)
                for j in range(3):
                    nc.scalar.activation(wh[q][:, j], wld[:, j], ACT.Copy).then_inc(a_wh, 1)

            def e_high(n, q):
                act.wait_ge(p_et, n + 1)
                nc.scalar.activation(eh[q][:, :, :], bank[q][:, :].rearrange("p (k n) -> p k n", k=KD), ACT.Copy) \
                    .then_inc(a_eh, 1)

            def silu(n, q):
                act.wait_ge(p_up, n + 1)
                nc.scalar.activation(sa[q][:, :, :], bank[2 + q][:, :].rearrange("p (k n) -> p k n", k=KD), ACT.Silu) \
                    .then_inc(a_sa, 1)

            def h_high(n, q):
                act.wait_ge(d_hf, n + 1)
                nc.scalar.activation(hh[q][:, :, :], hf[q][:, :, :], ACT.Copy).then_inc(a_hh, 1)

            def weighted(c, i, first):
                buf, n = c % NXB, i * (2 * NCH) + c
                act.wait_ge(p_dn, n + 1)
                act.wait_ge(d_sx, n + 1)
                if not (first and c < NXB):
                    act.wait_ge(st_eo[buf], (i * 2 + c // NXB) * (16 * CH))
                for t in range(CH):
                    ins = nc.scalar.activation(eo[buf][:, t, :], bank[6 + c % 2][:, t * D:(t + 1) * D], ACT.Copy,
                                               scale=sx[buf][:, t, 2:3].bitcast(F32))
                ins.then_inc(a_eo, 1)

            split_w(0, 0)
            meet(act, "act", 6)
            e_high(0, 0)

            def pair(i, first, last):
                for c in range(2 * NCH):
                    n = i * (2 * NCH) + c
                    if not (last and c == 2 * NCH - 1):
                        e_high(n + 1, (c + 1) % 2)
                    silu(n, c % 2)
                    h_high(n, c % 2)
                    if c > 0:
                        weighted(c - 1, i, first)
                    if c % NCH == 2:
                        split_w(i * 2 + (c // NCH + 1), (c // NCH + 1) % 2)
                weighted(2 * NCH - 1, i, first)

            pair(0, True, False)
            with act.Fori(1, E // 2 - 1) as i:
                pair(i, False, False)
            pair(E // 2 - 1, False, True)

            NC, N0 = NT // (CH * P), E * NCH

            def c_root(i):
                act.wait_ge(d_cst, i * GC)
                nc.scalar.activation(sd_c[:, :], mv_c[:, :, 1], ACT.Sqrt, bias=eps[:, 0:1]).then_inc(a_csd, 1)
                act.wait_ge(d_crs, i)

            def c_norm(i, q):
                act.wait_ge(st_out[q], i * 16)
                for t in range(CH):
                    c = q * CH + t
                    ins = nc.scalar.activation(yout[q][:, t, :], ytot[q][:, t, :], ACT.Identity, bias=nm_c[:, c:c + 1],
                                               scale=rs_c[:, c:c + 1])
                ins.then_inc(a_cn, 1)

            e_high(N0, 0)

            def group(i, first, last):
                for q in range(GC):
                    n = i * GC + q
                    if not (last and q == GC - 1):
                        e_high(n + (N0 + 1), 1 - q % 2)
                    silu(n + N0, q % 2)
                    h_high(n + N0, q % 2)
                    if not first:
                        if q == 1:
                            c_root(i)
                            c_norm(i, 0)
                        if q == 2:
                            c_norm(i, 1)
                            c_norm(i, 2)
                        if q == 3:
                            c_norm(i, 3)

            group(0, True, False)
            with act.Fori(1, NC // GC - 1) as i:
                group(i, False, False)
            group(NC // GC - 1, False, True)
            c_root(NC // GC)
            for q in range(GC):
                c_norm(NC // GC, q)

        @block.vector
        def _(dve):
            own = Own(dve, s_dve, 0)
            own.step(nc.vector.memset(eps[:, 0:1], EPS))
            own.step(nc.vector.memset(eps[:, 1:2], EPS * EPS))
            own.step(nc.vector.memset(hit_all[:, :], 0.0))
            own.step(nc.vector.memset(ones_b[:, :], 1.0))
            own.step(nc.vector.memset(ones_r[:, :].bitcast(F32), 1.0))
            own.step(nc.vector.memset(qb_f[:, :], 0.0))
            nc.vector.memset(rec[:, :, :], 0)
            nc.vector.memset(dsti[:, :], FAR)
            for z in (vb_r, ob_r, kvh, kvl, lqh, lql):
                nc.vector.memset(z[:, :].bitcast(F32), 0.0)
            dve.wait_ge(s_pos, 16)
            M, R = G64 - 1, MAXREL
            edge = pe_row[:, R:R + 1]
            nc.vector.tensor_copy(ext[:, 0:M - R], edge.to_broadcast([G64, M - R])).then_inc(s_ext, 1)
            nc.vector.tensor_copy(ext[:, M:M + R + 1], pe_row[:, 0:R + 1]).then_inc(s_ext, 1)
            nc.vector.tensor_copy(ext[:, M + R + 1:2 * G64], edge.to_broadcast([G64, 2 * G64 - M - R - 1])).then_inc(s_ext, 1)
            nc.vector.tensor_copy(ext[:, M - R:M], pe_row[:, R:0:-1]).then_inc(s_ext, 1)
            nc.vector.memset(toep[:, :], 0.0).then_inc(s_ext, 1)
            dve.wait_ge(s_load, 16 * 8)
            dve.wait_ge(s_loada, 16 * 9)
            for k in range(KD):
                own.step(nc.vector.tensor_copy(bmat[:, k, :], l1b[:, k:k + 1].to_broadcast([P, P])))
            for k in range(KD):
                ins = nc.vector.tensor_scalar(wq[:, k, :], qraw[:, k, :], l1w[:, k:k + 1], None, ALU.mult)
            own.step(ins)
            for j, (hi, lo) in enumerate(((wvh, wvl), (wgh, wgl))):
                own.wait()
                for k in range(KD):
                    ins = nc.vector.tensor_scalar(wscl[:, k, :], wraw[:, j, k, :], l1w[:, k:k + 1], None, ALU.mult)
                own.step(ins)
                dve.wait_ge(s_act, j + 1)
                own.wait()
                own.step(nc.vector.tensor_tensor(lo[:, :, :], wscl[:, :, :], hi[:, :, :].bitcast(F32), ALU.subtract))
            dve.wait_ge(s_pe, 1)
            own.step(nc.vector.tensor_tensor(gb[:, :], bank[1][:, 0:KH], gbi[:, :], ALU.add))
            own.step(nc.vector.tensor_tensor(vb[:, :], bank[2][:, :], vb[:, :], ALU.add))
            own.step(nc.vector.tensor_tensor(qb[:, :], bank[0][:, 0:QK], qb[:, :], ALU.add))
            own.step(nc.vector.tensor_copy(tri[:, :], cst[:, P:2 * P]))
            dve.wait_ge(s_act, 4)
            own.wait()
            own.step(nc.vector.tensor_tensor(vbl[:, :], vb[:, :], vbh[:, :].bitcast(F32), ALU.subtract))
            own.step(nc.vector.tensor_tensor(obl[:, :], ob[:, :], obh[:, :].bitcast(F32), ALU.subtract))
            own.wait()
            own.step(nc.vector.tensor_copy(qb_f[0:1, :], qb[0:1, :]))
            for dst_, hi, lo in ((vb_r, vbh, vbl), (ob_r, obh, obl)):
                own.step(nc.vector.tensor_copy(dst_[0:1, :], hi[0:1, :].bitcast(F32)))
                own.step(nc.vector.tensor_copy(dst_[32:33, :], lo[32:33, :].bitcast(F32)))
            own.step(nc.vector.memset(hit_was[:, :], 0.0))
            own.step(nc.vector.tensor_copy(base_f[:, :], tok_id[:, :]))
            dve.wait_ge(s_tl, 32)
            own.wait()
            own.step(nc.vector.tensor_tensor(bias_s[:, :], toep[:, :], off_block, ALU.add))
            dve.sem_inc(d_rec, 1)
            meet(dve, "dve", 1)

            def stats(own_, src, st, mv, tiles, done):
                for t in range(tiles):
                    ins = nc.vector.bn_stats(st[:, t, :], src(t))
                own_.step(ins)
                own_.wait()
                nc.vector.memset(gate_cell[:, :], 0.0)
                for t in range(tiles):
                    ins = nc.vector.bn_aggr(mv[:, t, :], st[:, t, :])
                ins.then_inc(done, 1)

            def inverse(own_, sd, rs, nm, mv, done):
                own_.step(nc.vector.reciprocal(rs[:, :], sd[:, :]))
                own_.wait()
                nc.vector.scalar_tensor_tensor(nm[:, :], mv[:, :, 0], -1.0, rs[:, :], ALU.mult, ALU.mult).then_inc(done, 1)

            def pass_a(b):
                def x_stats(g):
                    dve.wait_ge(ld_x, (g + 1) * 16)
                    stats(Own(dve, o_ln, g), lambda t: xa[:, t, :], st_a, mv_a, TB, d_stat)

                def x_scale(g, has_prev):
                    dve.wait_ge(a_sd, g + 1)
                    if has_prev:
                        dve.wait_ge(g_xn, g)
                    inverse(Own(dve, o_rs, g), sd_a, rs_a, nm_a, mv_a, d_rs)

                def x_low(g, first):
                    if not first:
                        dve.wait_ge(st_xl, g * 16)
                    for k in range(KD):
                        dve.wait_ge(a_xh, g * KD + (k + 1))
                        nc.vector.tensor_tensor(xl[:, k, :], bank[k][:, :], xh[:, k, :].bitcast(F32),
                                                ALU.subtract).then_inc(d_xl, 1)

                def rotate(g, m):
                    a1, a2 = hd[:, :, :, 0:HALF], hd[:, :, :, HALF:QK]
                    c_, s_ = (w[:, bass.ds(m * TB, TB), :].unsqueeze(2).to_broadcast([P, TB, 4, HALF]) for w in (cos, sin))
                    dve.wait_ge(g_hd, g + 1)
                    h1, h2 = hr[:, :, :, 0:HALF], hr[:, :, :, HALF:QK]
                    nc.vector.tensor_tensor(h1, a1, c_, ALU.mult)
                    nc.vector.tensor_tensor(prod[0][:, :, :, :], a2, s_, ALU.mult)
                    nc.vector.tensor_tensor(h2, a2, c_, ALU.mult)
                    nc.vector.tensor_tensor(prod[1][:, :, :, :], a1, s_, ALU.mult).then_inc(d_prod, 1)
                    dve.wait_ge(d_prod, g + 1)
                    nc.vector.tensor_tensor(h1, h1, prod[0][:, :, :, :], ALU.subtract)
                    nc.vector.tensor_tensor(h2, h2, prod[1][:, :, :, :], ALU.add) \
                        .then_inc(d_head, 1)

                def kb_low(g):
                    dve.wait_ge(a_pbh, g + 1)
                    nc.vector.tensor_tensor(pbl[:, :, :], hr[:, :, 2:4, :].rearrange("p t h d -> p t (h d)"),
                                            pbh[:, :, :].bitcast(F32), ALU.subtract).then_inc(d_pbl, 1)

                def v_low(g, t):
                    dve.wait_ge(a_vh, g * TB + (t + 1))
                    nc.vector.tensor_tensor(vl[:, t, :], vt[:, t, :], vh[:, t, :].bitcast(F32), ALU.subtract) \
                        .then_inc(d_vl, 1)

                def q_and_k(g):
                    dve.wait_ge(p_ta, g + 1)
                    nc.vector.tensor_copy(qqt[:, :], bank[3][0:QK, :])
                    dve.wait_ge(p_tb, g + 1)
                    nc.vector.tensor_copy(kkt[:, :], bank[4][0:QK, :]).then_inc(d_tab, 1)

                def q_low(g, m):
                    dve.wait_ge(a_ta, g + 1)
                    nc.vector.tensor_tensor(lql[QK:2 * QK, cols(m)], bank[3][QK:2 * QK, :],
                                            lqh[QK:2 * QK, cols(m)].bitcast(F32), ALU.subtract).then_inc(d_lql, 1)

                def scores(g):
                    dve.wait_ge(p_s, g + 1)
                    nc.vector.scalar_tensor_tensor(at[:, :].rearrange("p (t n) -> p t n", t=TB),
                                                   bank[5][:, :].rearrange("p (t n) -> p t n", t=TB), 1.0 / G64,
                                                   bias_s[:, :].unsqueeze(1).to_broadcast([P, TB, P]),
                                                   ALU.mult, ALU.add).then_inc(o_at, 1)
                    dve.wait_ge(o_at, g + 1)
                    nc.vector.scalar_tensor_tensor(at[:, :], at[:, :], 0.0, at[:, :], ALU.max, ALU.mult).then_inc(d_at, 1)

                g0 = b * NB
                x_stats(g0)
                x_scale(g0, False)
                x_low(g0, True)
                x_stats(g0 + 1)
                x_scale(g0 + 1, True)

                def body(g, m, has_prev, ahead):
                    rotate(g, m)
                    v_low(g, 0)
                    v_low(g, 1)
                    kb_low(g)
                    v_low(g, 2)
                    v_low(g, 3)
                    q_and_k(g)
                    if ahead >= 2:
                        x_stats(g + 2)
                    q_low(g, m)
                    scores(g)
                    if ahead >= 1:
                        x_low(g + 1, False)
                    if ahead >= 2:
                        x_scale(g + 2, True)

                blocks_a(dve, b, body)
                dve.wait_ge(a_kvh, b + 1)
                nc.vector.scalar_tensor_tensor(kvl[QK:2 * QK, :], bank[7][QK:2 * QK, :], 1.0 / S,
                                               kvh[QK:2 * QK, :].bitcast(F32), ALU.mult, ALU.subtract).then_inc(o_kv, 1)

            def pass_b(b):
                nc.vector.memset(mv_b[:, :, :], 0.0)

                def gated(g, c, m, has_prev):
                    dve.wait_ge(p_lo, g * KH + (c + 1))
                    both = bank[2 + c % 2][:, :]
                    if c not in PE_ADDS:
                        nc.vector.tensor_tensor(mixed[:, :], both, qo_all[:, c, cols(m)], ALU.add).then_inc(d_mix, 1)
                        dve.wait_ge(d_mix, g * (KH - len(PE_ADDS)) + (c + 1 - sum(k < c for k in PE_ADDS)))
                        both = mixed[:, :]
                    dve.wait_ge(a_gs, g * KH + (c + 1))
                    if c == 0 and has_prev:
                        dve.wait_ge(p_wo, g * 2)
                    nc.vector.tensor_tensor(og[:, c, :], both, gsb[c % 2][:, :], ALU.mult).then_inc(d_og, 1)

                def wide(ap, n):
                    return ap.unsqueeze(2).to_broadcast([P, TB, n])

                def less_max(g, own_):
                    dve.wait_ge(p_lg, g + 1)
                    z = bank[6][:, 0:TB * E].rearrange("p (t e) -> p t e", t=TB)
                    own_.step(nc.vector.tensor_reduce(mx[:, :], z, AX, ALU.max))
                    own_.wait()
                    nc.vector.tensor_tensor(lg[:, :, :], z, wide(mx[:, :], E), ALU.subtract).then_inc(d_lg, 1)

                def softmax(g, own_):
                    dve.wait_ge(a_exp, g + 1)
                    own_.step(nc.vector.tensor_reduce(sm[:, :], pr[:, :, :], AX, ALU.add))
                    own_.wait()
                    own_.step(nc.vector.reciprocal(rsm[:, :], sm[:, :]))
                    own_.wait()
                    own_.step(nc.vector.tensor_tensor(pr[:, :, :], pr[:, :, :], wide(rsm[:, :], E), ALU.mult))
                    own_.wait()
                    own_.step(nc.vector.tensor_reduce(gs[:, :, :], pr[:, :, :].rearrange("p t (a c) -> p t a c", a=GRP), AX, ALU.max))
                    own_.wait()
                    nc.vector.memset(gate_cell[:, :], 0.0)

                def groups(own_):
                    top4(own_, gs, top_g, ix_g, fx_g)

                def masked(own_):
                    own_.step(nc.vector.tensor_tensor(
                        eq_g[:, :, :, :], iota_e[:, 0:GRP].unsqueeze(1).unsqueeze(1).to_broadcast([P, TB, TOPK, GRP]),
                        fx_g[:, :, 0:TOPK].unsqueeze(3).to_broadcast([P, TB, TOPK, GRP]), ALU.is_equal))
                    own_.wait()
                    own_.step(nc.vector.tensor_reduce(keep[:, :, :], eq_g[:, :, :, :].rearrange("p t k a -> p t a k"), AX, ALU.add))
                    own_.wait()
                    nc.vector.tensor_scalar(kneg[:, :, :], keep[:, :, :], -1.0, None, ALU.add)
                    m4 = msk[:, :, :].rearrange("p t (a c) -> p t a c", a=GRP)
                    own_.step(nc.vector.tensor_tensor(m4, pr[:, :, :].rearrange("p t (a c) -> p t a c", a=GRP),
                                                      keep[:, :, :].unsqueeze(3).to_broadcast([P, TB, GRP, EG]), ALU.mult))
                    own_.wait()
                    own_.step(nc.vector.tensor_tensor(m4, m4, kneg[:, :, :].unsqueeze(3).to_broadcast([P, TB, GRP, EG]), ALU.add))
                    own_.wait()
                    nc.vector.memset(gate_cell[:, :], 0.0)

                def experts(own_):
                    top4(own_, msk, top_e, ix_e, fx_e)

                def hits(own_):
                    own_.step(nc.vector.tensor_tensor(
                        oh[:, :, :, :], iota_e.unsqueeze(1).unsqueeze(1).to_broadcast([P, TB, TOPK, E]),
                        fx_e[:, :, 0:TOPK].unsqueeze(3).to_broadcast([P, TB, TOPK, E]), ALU.is_equal))
                    own_.wait()
                    nc.vector.tensor_reduce(wsum[:, :], top_e[:, :, 0:TOPK], AX, ALU.add)
                    with nc.allow_low_precision("0 and 1 are exact"):
                        nc.vector.tensor_reduce(hit[:, :, :], oh[:, :, :, :].rearrange("p t k e -> p t e k"), AX, ALU.add) \
                            .then_inc(d_hit, 1)
                    assert own_.n == 16, own_.n

                def top4(own_, src, val, ix, fx):
                    for t in range(TB):
                        ins = nc.vector.max(val[:, t, :], src[:, t, :])
                    own_.step(ins)
                    own_.wait()
                    nc.vector.memset(gate_cell[:, :], 0.0)
                    for t in range(TB):
                        ins = nc.vector.max_index(ix[:, t, :], val[:, t, :], src[:, t, :])
                    own_.step(ins)
                    own_.wait()
                    own_.step(nc.vector.tensor_copy(fx[:, :, :], ix[:, :, :]))
                    own_.wait()

                def slots(g):
                    own_ = Own(dve, o_fin, g * 7)
                    dve.wait_ge(p_cs, g + 1)
                    n4 = bank[3][:, 0:TB * E].rearrange("p (t e) -> p t e", t=TB)
                    nc.vector.tensor_reduce(hsum[:, :], hit[:, :, :].rearrange("p t e -> p e t"), AX, ALU.add)
                    nc.vector.tensor_scalar(wrec[:, :], wsum[:, :], 1e-9, None, ALU.add)
                    own_.step(nc.vector.tensor_tensor(ohp[:, :, :, :], oh[:, :, :, :],
                                                      n4.unsqueeze(2).to_broadcast([P, TB, TOPK, E]), ALU.mult))
                    own_.wait()
                    own_.step(nc.vector.tensor_reduce(pos[:, :, :], ohp[:, :, :, :], AX, ALU.add))
                    nc.vector.tensor_tensor(hit_all[:, :], hit_all[:, :], hsum[:, :], ALU.add)
                    own_.step(nc.vector.reciprocal(wrec[:, :], wrec[:, :]))
                    own_.wait()
                    own_.step(nc.vector.tensor_copy(hit_was[:, :], hit_all[:, :]))
                    nc.vector.tensor_scalar(over[:, :, :], pos[:, :, :], float(CAP), float(FAR), ALU.is_ge, ALU.mult)
                    own_.step(nc.vector.scalar_tensor_tensor(dst[:, :, :], fx_e[:, :, 0:TOPK], float(CAP), pos[:, :, :],
                                                             ALU.mult, ALU.add))
                    dve.wait_ge(g_rec, g + 1)
                    own_.wait()
                    own_.step(nc.vector.tensor_tensor(dsti[:, :].rearrange("p (t k) -> p t k", t=TB), dst[:, :, :],
                                                      over[:, :, :], ALU.add))
                    nc.vector.tensor_copy(rec[:, :, 0:2], base_f[:, :].rearrange("p (n r) -> p n r", r=2))
                    own_.step(nc.vector.tensor_tensor(
                        rec[:, :, 2:3].bitcast(F32).rearrange("p (t k) r -> p t (k r)", t=TB), top_e[:, :, 0:TOPK],
                        wrec[:, :].unsqueeze(2).to_broadcast([P, TB, TOPK]), ALU.mult))
                    own_.wait()
                    step_ = base_f[:, :].rearrange("p (n r) -> p n r", r=2)
                    nc.vector.tensor_scalar(step_[:, :, 0:1], step_[:, :, 0:1], float(BLK), None, ALU.add)
                    nc.vector.tensor_scalar(step_[:, :, 1:2], step_[:, :, 1:2], float(BLK * TOPK), None, ALU.add) \
                        .then_inc(d_rec, 1)
                    assert own_.n == 7, own_.n

                def add_bias(g):
                    dve.wait_ge(g_w2, g + 1)
                    nc.vector.tensor_tensor(yb[:, :, :], yb[:, :, :], b2b[:, :].unsqueeze(1).to_broadcast([P, TB, D]),
                                            ALU.add).then_inc(o_wb, 1)

                def add_x(g, has_prev):
                    dve.wait_ge(a_n2, g + 1)
                    dve.wait_ge(ld_xb, g * 16 + 16)
                    if has_prev:
                        dve.wait_ge(st_x2, g * 16)
                        dve.wait_ge(a_n3, g)
                    nc.vector.tensor_tensor(x2b[:, :, :], yn[:, :, :], xb[:, :, :], ALU.add).then_inc(d_x2, 1)

                def body(g, m, on):
                    routing = Own(dve, o_rt, (g - 4) * 16)
                    if on[0]:
                        gated(g, 0, m, on[1])
                    if on[4]:
                        less_max(g - 4, routing)
                    if on[0]:
                        gated(g, 1, m, on[1])
                    if on[2]:
                        add_bias(g - 2)
                    if on[0]:
                        gated(g, 2, m, on[1])
                    if on[2]:
                        dve.wait_ge(o_wb, g - 1)
                        stats(Own(dve, o_s2, g - 2), lambda t: yb[:, t, :], st_2, mv_b[:, TB:2 * TB, :], TB, d_st2)
                    if on[0]:
                        gated(g, 3, m, on[1])
                    if on[3]:
                        dve.wait_ge(d_x2, g - 2)
                        stats(Own(dve, o_s3, g - 3), lambda t: x2b[:, t, :], st_3, mv_b[:, 2 * TB:3 * TB, :], TB, d_st3)
                    if on[1]:
                        dve.wait_ge(a_yo, g * 2)
                        stats(Own(dve, o_s1, g - 1), lambda t: yo[:, t, :], st_1, mv_b[:, 0:TB, :], TB, d_st1)
                    if on[4]:
                        softmax(g - 4, routing)
                    if on[1] or on[2] or on[3]:
                        dve.wait_ge(a_root, g + b * 2)
                        inverse(Own(dve, o_inv, g + (b * 2 - 1)), sd_b, rs_b, nm_b, mv_b, d_inv)
                    if on[4]:
                        groups(routing)
                        masked(routing)
                        experts(routing)
                        hits(routing)
                    if on[2]:
                        add_x(g - 2, on[3])
                    if on[4]:
                        slots(g - 4)

                blocks_b(dve, b, body)

            attention(dve, "dve", pass_a, pass_b)

            def split_w(e, q):
                for j in range(3):
                    dve.wait_ge(a_wh, e * 3 + (j + 1))
                    ins = nc.vector.tensor_tensor(wl[q][:, j], wld[:, j], wh[q][:, j].bitcast(F32), ALU.subtract)
                ins.then_inc(d_wl, 1)

            def e_low(n, q):
                dve.wait_ge(a_eh, n + 1)
                nc.vector.tensor_tensor(el[q][:, :, :], bank[q][:, :].rearrange("p (k n) -> p k n", k=KD),
                                        eh[q][:, :, :].bitcast(F32), ALU.subtract).then_inc(d_el, 1)

            def product(n, q):
                dve.wait_ge(a_sa, n + 1)
                nc.vector.tensor_tensor(hf[q][:, :, :], bank[4 + q][:, :].rearrange("p (k n) -> p k n", k=KD),
                                        sa[q][:, :, :], ALU.mult).then_inc(d_hf, 1)

            def h_low(n, q):
                dve.wait_ge(a_hh, n + 1)
                nc.vector.tensor_tensor(hl[q][:, :, :], hf[q][:, :, :], hh[q][:, :, :].bitcast(F32), ALU.subtract) \
                    .then_inc(d_hl, 1)

            split_w(0, 0)
            meet(dve, "dve", 6)
            e_low(0, 0)

            def records(c, i, first):
                q, buf, n = c // NCH, c % NXB, i * (2 * NCH) + c
                if c % NCH == 0:
                    dve.wait_ge(ld_six[q], (i + 1) * 16)
                if not (first and c < NXB):
                    dve.wait_ge(st_eo[buf], (i * 2 + c // NXB) * (16 * CH))
                s = (c % NCH) * CH
                nc.vector.tensor_copy(sx[buf][:, :, :], six[q][:, s:s + CH, :]).then_inc(d_sx, 1)

            def pair(i, first, last):
                for c in range(2 * NCH):
                    n = i * (2 * NCH) + c
                    if not (last and c == 2 * NCH - 1):
                        e_low(n + 1, (c + 1) % 2)
                    records(c, i, first)
                    product(n, c % 2)
                    h_low(n, c % 2)
                    if c % NCH == 2:
                        split_w(i * 2 + (c // NCH + 1), (c // NCH + 1) % 2)

            pair(0, True, False)
            with dve.Fori(1, E // 2 - 1) as i:
                pair(i, False, False)
            pair(E // 2 - 1, False, True)

            NC, N0 = NT // (CH * P), E * NCH

            def total(n, q, first):
                dve.wait_ge(g_ys, n + 1)
                dve.wait_ge(p_dn, n + (N0 + 1))
                if not first:
                    dve.wait_ge(a_cn, n - (GC - 1))
                nc.vector.tensor_tensor(ytot[q][:, :, :], ysum[q % 2][:, :, 0, :],
                                        bank[6 + q % 2][:, :].rearrange("p (t d) -> p t d", t=CH), ALU.add).then_inc(d_acc, 1)
                dve.wait_ge(d_acc, n + 1)
                stats(Own(dve, o_c, n), lambda t: ytot[q][:, t, :], st_c, mv_c[:, q * CH:(q + 1) * CH, :], CH, d_cst)

            def c_inverse(i):
                dve.wait_ge(a_csd, i)
                inverse(Own(dve, o_cr, i - 1), sd_c, rs_c, nm_c, mv_c, d_crs)

            def final(i, q):
                dve.wait_ge(a_cn, i * GC + (q + 1 - GC))
                dve.wait_ge(ld_r[q], i * 16)
                nc.vector.tensor_tensor(yout[q][:, :, :], yout[q][:, :, :], xr[q][:, :, :], ALU.add).then_inc(d_out, 1)

            e_low(N0, 0)

            def group(i, first, last):
                for q in range(GC):
                    n = i * GC + q
                    if not (last and q == GC - 1):
                        e_low(n + (N0 + 1), 1 - q % 2)
                    product(n + N0, q % 2)
                    h_low(n + N0, q % 2)
                    if not first:
                        if q == 1:
                            c_inverse(i)
                        if q == 2:
                            final(i, 0)
                        if q == 3:
                            final(i, 1)
                            final(i, 2)
                    if not (first and q == 0):
                        total(n - 1, (q - 1) % GC, first or q == 0)
                    if q == 3 and not first:
                        final(i, 3)

            group(0, True, False)
            with dve.Fori(1, NC // GC - 1) as i:
                group(i, False, False)
            group(NC // GC - 1, False, True)
            total(NC - 1, GC - 1, False)
            c_inverse(NC // GC)
            for q in range(GC):
                final(NC // GC, q)

        @block.tensor
        def _(pe):
            pe.wait_ge(s_dve, 8)
            pe.wait_ge(s_load, 16 * 8)
            pe.wait_ge(s_loada, 16 * 9)
            for c in range(KH):
                for k in range(KD):
                    nc.tensor.matmul(bank[1][:, c:c + 1], wraw[:, 1, k, c * P:(c + 1) * P], l1b[:, k:k + 1],
                                     start=(k == 0), stop=(k == KD - 1))
            for k in range(KD):
                nc.tensor.matmul(bank[0][:, 0:QK], bmat[:, k, :], qraw[:, k, :], start=(k == 0), stop=(k == KD - 1))
            for k in range(KD):
                ins = nc.tensor.matmul(bank[2][:, :], bmat[:, k, :], wraw[:, 0, k, :], start=(k == 0), stop=(k == KD - 1))
            ins.then_inc(s_pe, 1)
            meet(pe, "pe", 1)

            def three(dst_, ah, al, bh, bl, start, stop, check=False):
                kw = {"skip_group_check": True} if check else {}
                nc.tensor.matmul(dst_, ah, bh, start=start, stop=False, **kw)
                nc.tensor.matmul(dst_, ah, bl, start=False, stop=False, **kw)
                return nc.tensor.matmul(dst_, al, bh, start=False, stop=stop, **kw)

            def pass_a(b):
                def turn_x(g, first):
                    pe.wait_ge(g_xn, g + 1)
                    for k in range(KD):
                        if not first:
                            pe.wait_ge(a_v, (g - 1) * TB + (k + 3))
                        for t in range(TB):
                            ins = nc.tensor.transpose(bank[k][:, t * P:(t + 1) * P], xn[:, t, k * P:(k + 1) * P], ident)
                        ins.then_inc(p_x, 1)

                def project(dst_, t, bias, w_h, w_l):
                    nc.tensor.matmul(dst_, ones_r[:, :], bias[:, :], start=True, stop=False)
                    for k in range(KD):
                        ins = three(dst_, xh[:, k, t * P:(t + 1) * P], xl[:, k, t * P:(t + 1) * P], w_h[:, k, :], w_l[:, k, :],
                                    False, k == KD - 1)
                    return ins

                def queries(g):
                    pe.wait_ge(a_xt, g + 1)
                    for t in range(TB):
                        dst_ = bank[2][:, t * QK:(t + 1) * QK]
                        nc.tensor.matmul(dst_, ones_f, qb_f[:, :], start=True, stop=False)
                        for k in range(KD):
                            ins = nc.tensor.matmul(dst_, xta[:, k, t * P:(t + 1) * P], wq[:, k, :], start=False,
                                                   stop=(k == KD - 1))
                    ins.then_inc(p_u, 1)

                def weigh(g):
                    pe.wait_ge(d_at, g + 1)
                    for c in range(KH):
                        if c == 1:
                            pe.wait_ge(d_lql, g + 1)
                        for t in range(TB):
                            ins = nc.tensor.matmul(bank[QO_BANK[c]][:, t * P:(t + 1) * P], vt[:, t, c * P:(c + 1) * P],
                                                   at[:, t * P:(t + 1) * P], start=True, stop=True)
                        ins.then_inc(p_qo, 1)

                def add_kv(g, t):
                    pe.wait_ge(d_vl, g * TB + (t + 1))
                    three(bank[7][:, :], pbh[:, t, :], pbl[:, t, :], vh[:, t, :], vl[:, t, :], False, False, True) \
                        .then_inc(p_kv, 1)

                nc.tensor.matmul(bank[7][:, :], zero[:, 0:P], zero[:, 0:H], start=True, stop=True, skip_group_check=True)
                turn_x(b * NB, True)
                queries(b * NB)

                def body(g, m, has_prev, ahead):
                    if has_prev:
                        pe.wait_ge(a_u, g + 1)
                        weigh(g - 1)
                    pe.wait_ge(d_xl, g * KD + KD)
                    for t in range(TB):
                        if t >= 2:
                            pe.wait_ge(a_v, g * TB + (t - 1))
                        project(bank[t % 2][:, :], t, vb_r, wvh, wvl).then_inc(p_v, 1)
                    pe.wait_ge(d_head, g + 1)
                    for h, (bk, done) in enumerate(((3, p_ta), (4, p_tb))):
                        if has_prev:
                            pe.wait_ge(a_qo, (g - 1) * KH + (h + 2))
                        for t in range(TB):
                            ins = nc.tensor.transpose(bank[bk][:, t * P:(t + 1) * P],
                                                      hr[:, t, 2 * h:2 * h + 2, :].rearrange("p h d -> p (h d)"), ident)
                        ins.then_inc(done, 1)
                    pe.wait_ge(d_pbl, g + 1)
                    add_kv(g, 0)
                    add_kv(g, 1)
                    pe.wait_ge(d_tab, g + 1)
                    for t in range(TB):
                        ins = nc.tensor.matmul(bank[5][:, t * P:(t + 1) * P], kkt[:, t * P:(t + 1) * P],
                                               qqt[:, t * P:(t + 1) * P], start=True, stop=True)
                    ins.then_inc(p_s, 1)
                    if ahead >= 1:
                        turn_x(g + 1, False)
                    add_kv(g, 2)
                    add_kv(g, 3)
                    if ahead >= 1:
                        if has_prev:
                            pe.wait_ge(a_qo, g * KH)
                        else:
                            pe.wait_ge(a_u, g + 1)
                        queries(g + 1)

                blocks_a(pe, b, body)
                weigh(b * NB + (NB - 1))

            def pass_b(b):
                def mix(g, c, m, has_prev):
                    if c == 0:
                        pe.wait_ge(ld_xh, g * 32 + 32)
                    if has_prev or c >= 2:
                        pe.wait_ge(a_gs, g * KH + (c - 1))
                    for k in range(KD):
                        ins = three(bank[c % 2][:, :], wgh[:, k, c * P:(c + 1) * P], wgl[:, k, c * P:(c + 1) * P],
                                    xh[:, k, :], xl[:, k, :], k == 0, k == KD - 1)
                    ins.then_inc(p_g, 1)
                    if has_prev or c >= 2:
                        pe.wait_ge(d_og, g * KH + (c - 1))
                    adds = c in PE_ADDS
                    ins = three(bank[2 + c % 2][:, :], kvh[:, c * P:(c + 1) * P], kvl[:, c * P:(c + 1) * P],
                                lqh[:, cols(m)], lql[:, cols(m)], True, not adds)
                    if adds:
                        ins = nc.tensor.matmul(bank[2 + c % 2][:, :], ident, qo_all[:, c, cols(m)], start=False, stop=True)
                    ins.then_inc(p_lo, 1)

                def turn_xf(g, has_prev):
                    pe.wait_ge(a_n3, g + 1)
                    if has_prev:
                        pe.wait_ge(d_lg, g)
                    for k in range(KD):
                        for t in range(TB):
                            ins = nc.tensor.transpose(bank[6 + k][:, t * P:(t + 1) * P], xfb[:, t, k * P:(k + 1) * P], ident)
                        ins.then_inc(p_xt, 1)

                def logits(g):
                    pe.wait_ge(a_xft, g * KD + KD)
                    for t in range(TB):
                        for k in range(KD):
                            ins = nc.tensor.matmul(bank[6][:, t * E:(t + 1) * E], xft[:, k, t * P:(t + 1) * P], wr[:, k, :],
                                                   start=(k == 0), stop=(k == KD - 1))
                    ins.then_inc(p_lg, 1)

                def wo_(g, h, has_prev):
                    pe.wait_ge(d_og, g * KH + KH)
                    if has_prev:
                        pe.wait_ge(a_yo, g * 2)
                    for t in (2 * h, 2 * h + 1):
                        dst_ = bank[4 + h][:, (t % 2) * D:(t % 2 + 1) * D]
                        nc.tensor.matmul(dst_, ones_r[:, :], ob_r[:, :], start=True, stop=False)
                        for k in range(KH):
                            ins = nc.tensor.matmul(dst_, og[:, k, t * P:(t + 1) * P], wo[:, k, :], start=False,
                                                   stop=(k == KH - 1))
                    ins.then_inc(p_wo, 1)

                def count(g, mixed_):
                    pe.wait_ge(d_hit, g + 1)
                    if mixed_:
                        pe.wait_ge(d_og, (g + (LAG + 1)) * KH)
                    else:
                        pe.wait_ge(d_rec, g + 1)
                    for t in range(TB):
                        dst_ = bank[3][:, t * E:(t + 1) * E]
                        nc.tensor.matmul(dst_, ones_b[:, :], hit_was[:, :], start=True, stop=False)
                        for s in range(t):
                            nc.tensor.matmul(dst_, ones_b[:, :], hit[:, s, :], start=False, stop=False)
                        ins = nc.tensor.matmul(dst_, tri[:, :], hit[:, t, :], start=False, stop=True)
                    ins.then_inc(p_cs, 1)

                def body(g, m, on):
                    if on[0]:
                        mix(g, 0, m, on[1])
                    if on[4]:
                        logits(g - 4)
                    if on[0]:
                        for c in range(1, KH):
                            if c == 1 and on[4]:
                                pe.wait_ge(d_rec, g - 3)
                            mix(g, c, m, on[1])
                        wo_(g, 0, on[1])
                        wo_(g, 1, on[1])
                    if on[3]:
                        turn_xf(g - 3, on[4])
                    if on[4]:
                        count(g - 4, on[0])

                blocks_b(pe, b, body)

            attention(pe, "pe", pass_a, pass_b)
            meet(pe, "pe", 6)

            def turn_e(n, q, src, arrived):
                arrived()
                for k in range(KD):
                    for t in range(CH):
                        ins = nc.tensor.transpose(bank[q][:, (k * CH + t) * P:(k * CH + t + 1) * P],
                                                  src[:, t, k * P:(k + 1) * P], ident)
                ins.then_inc(p_et, 1)

            def up(n, q, wq, e, first):
                pe.wait_ge(d_el, n + 1)
                if not first:
                    pe.wait_ge(d_hf, n - 1)
                for j in range(2):
                    for c in range(KD):
                        for k in range(KD):
                            ins = three(bank[2 + 2 * j + q][:, c * CH * P:(c + 1) * CH * P],
                                        wh[wq][:, j, k, c * P:(c + 1) * P], wl[wq][:, j, k, c * P:(c + 1) * P],
                                        eh[q][:, k, :], el[q][:, k, :], k == 0, k == KD - 1)
                ins.then_inc(p_up, 1)

            def down(n, q, wq, free):
                pe.wait_ge(d_hl, n + 1)
                free()
                for t in range(CH):
                    for k in range(KD):
                        ins = three(bank[6 + q][:, t * D:(t + 1) * D], hh[q][:, k, t * P:(t + 1) * P],
                                    hl[q][:, k, t * P:(t + 1) * P], wh[wq][:, 2, k, :], wl[wq][:, 2, k, :],
                                    k == 0, k == KD - 1)
                ins.then_inc(p_dn, 1)

            def turn_g(c, i, first):
                i, c = (i + 1, c - 2 * NCH) if c >= 2 * NCH else (i, c)
                n = i * (2 * NCH) + c

                def arrived():
                    pe.wait_ge(ld_xg[c % NXB], (i * 2 + (c // NXB + 1)) * (16 * CH))
                    if not first:
                        pe.wait_ge(d_el, n - 1)

                turn_e(n, c % 2, xg[c % NXB], arrived)

            turn_g(0, 0, True)

            def pair(i, first, last):
                for c in range(2 * NCH):
                    n = i * (2 * NCH) + c
                    if not (last and c == 2 * NCH - 1):
                        turn_g(c + 1, i, first and c + 1 < 2)
                    if c % NCH == 0:
                        pe.wait_ge(d_wl, i * 2 + (c // NCH + 1))
                    up(n, c % 2, c // NCH, None, first and c < 2)
                    if c > 0:
                        m = c - 1
                        down(n - 1, m % 2, m // NCH, lambda: None if first and m < 2 else pe.wait_ge(a_eo, n - 2))
                m = 2 * NCH - 1
                n = i * (2 * NCH) + m
                down(n, m % 2, m // NCH, lambda: pe.wait_ge(a_eo, n - 1))

            pair(0, True, False)
            with pe.Fori(1, E // 2 - 1) as i:
                pair(i, False, False)
            pair(E // 2 - 1, False, True)

            NC, N0 = NT // (CH * P), E * NCH

            def turn_c(n, q, i):
                def arrived():
                    pe.wait_ge(ld_c[q], i * 16 + 16)
                    pe.wait_ge(d_el, n + (N0 - 1))

                turn_e(n + N0, q % 2, xg[q], arrived)

            turn_c(0, 0, 0)
            pe.wait_ge(d_wl, E + 1)

            def group(i, first, last):
                for q in range(GC):
                    n = i * GC + q
                    if not (last and q == GC - 1):
                        turn_c(n + 1, (q + 1) % GC, i + (q + 1) // GC)
                    up(n + N0, q % 2, 0, None, False)
                    if not (first and q == 0):
                        down(n + (N0 - 1), 1 - q % 2, 0, lambda: pe.wait_ge(a_eo, N0 + n - 2) if first and q < 3
                             else pe.wait_ge(d_acc, n - 2))

            group(0, True, False)
            with pe.Fori(1, NC // GC - 1) as i:
                group(i, False, False)
            group(NC // GC - 1, False, True)
            down(N0 + NC - 1, 1, 0, lambda: pe.wait_ge(d_acc, NC - 2))


_OUT = (2, 4096, 256)


def kernel(L0_attn_x, L0_attn_ln1_w, L0_attn_ln1_b, L0_attn_Wqk, L0_attn_bqk, L0_attn_Wv, L0_attn_bv, L0_attn_Wg,
           L0_attn_bg, L0_attn_Wo, L0_attn_bo, L0_attn_ln2_w, L0_attn_ln2_b, L0_attn_gamma, L0_attn_beta,
           L0_attn_pos_emb, L0_ffn_wg, L0_ffn_w1, L0_ffn_w2, L0_ffn_w3, L0_ffn_sw1, L0_ffn_sw2, L0_ffn_sw3):
    import numpy as np
    import concourse.bacc as bacc
    from concourse import mybir
    from concourse.bass_utils import run_bass_kernel_spmd

    def rows(a):
        return np.ascontiguousarray(a)

    def columns(a):
        return rows(np.asarray(a).reshape(-1, 128).T)

    n, half = 4096, 32
    inv_freq = np.power(np.float32(10000.0), -(np.arange(half, dtype=np.float32) / np.float32(half)))
    angle = np.arange(n, dtype=np.float32)[:, None] * inv_freq[None, :]
    rope = np.stack([np.cos(angle), np.sin(angle)]).reshape(2, n // 128, 128, half).transpose(0, 2, 1, 3)
    p = np.arange(128)
    ident = np.eye(128, dtype=np.float32)
    before = (p[:, None] < p[None, :]).astype(np.float32)
    off_block = np.where(p[:, None] // 64 == p[None, :] // 64, 0.0, -1e30).astype(np.float32)
    experts = np.broadcast_to(np.arange(32, dtype=np.float32), (128, 32))
    tok = np.arange(4)[None, :, None] * 128 + p[:, None, None] + np.zeros((1, 1, 4), np.int64)
    token_ids = np.stack([tok, tok * 4 + np.arange(4)], -1).reshape(128, 32).astype(np.int32)

    arrays = {
        "x": rows(np.asarray(L0_attn_x).reshape(8192, 256)),
        "wqk_t": rows(np.asarray(L0_attn_Wqk).T), "wv_t": rows(np.asarray(L0_attn_Wv).T),
        "wg_t": rows(np.asarray(L0_attn_Wg).T), "wo_t": rows(np.asarray(L0_attn_Wo).T),
        "ln1_w": columns(L0_attn_ln1_w), "ln1_b": columns(L0_attn_ln1_b),
        "bqk": rows(L0_attn_bqk), "bg": columns(L0_attn_bg),
        "bv": rows(L0_attn_bv), "bo": rows(L0_attn_bo),
        "ln2_w": rows(L0_attn_ln2_w), "ln2_b": rows(L0_attn_ln2_b),
        "gamma": rows(np.asarray(L0_attn_gamma).reshape(-1)), "beta": rows(np.asarray(L0_attn_beta).reshape(-1)), "pos_emb": rows(L0_attn_pos_emb),
        "rope": rows(rope), "consts": rows(np.concatenate([ident, before, off_block, experts], 1)),
        "token_ids": token_ids, "route_t": rows(np.asarray(L0_ffn_wg).T),
        "w1": rows(L0_ffn_w1), "w2": rows(L0_ffn_w2), "w3": rows(L0_ffn_w3),
        "sw1": rows(L0_ffn_sw1), "sw2": rows(L0_ffn_sw2), "sw3": rows(L0_ffn_sw3),
    }
    nc = bacc.Bacc("TRN2", target_bir_lowering=False, num_devices=1)
    args = {k: nc.dram_tensor("in_" + k, a.shape, mybir.dt.from_np(a.dtype), kind="ExternalInput").ap()
            for k, a in arrays.items()}
    args["out"] = nc.dram_tensor("out", (8192, 256), mybir.dt.float32, kind="ExternalOutput").ap()
    build_program(nc, **args)
    r = run_bass_kernel_spmd(nc, [{"in_" + k: a for k, a in arrays.items()}], core_ids=[0])
    return r.results[0]["out"].reshape(_OUT)
```
